# Optimizing a Trainium2 kernel written in Bass

```python
import numpy as np
import jax
import jax.numpy as jnp

def _softmax(x, axis=-1):
    return jax.nn.softmax(x, axis=axis)

def _gelu(x):
    return jax.nn.gelu(x, approximate=True)

def _silu(x):
    return jax.nn.silu(x)

def _sigmoid(x):
    return jax.nn.sigmoid(x)

def _layernorm(x, axis=-1, eps=1e-05):
    m = jnp.mean(x, axis=axis, keepdims=True)
    v = jnp.var(x, axis=axis, keepdims=True)
    return (x - m) / jnp.sqrt(v + eps)

def _scatter_add(tgt, idx, src, axis=0):
    return tgt.at[idx].add(src)

def _segment_sum(src, seg, n):
    return jax.ops.segment_sum(src, seg, n)
kernel_name = 'mk_gnn_preln_d4_gnn_r8_bce3ed'

def setup_inputs(seed: int=0):
    np.random.seed(seed)
    _w = jnp.asarray

    def _rec_inputs():
        import jax
        import jax.numpy as jnp
        _gk = jax.random.key(seed)
        x = -0.0003713 + 1 * jax.random.normal(jax.random.fold_in(_gk, 1), (12500, 128), jnp.float32)
        src = jax.random.randint(jax.random.fold_in(_gk, 2), (200000,), 0, 12500, jnp.int32)
        dst = jax.random.randint(jax.random.fold_in(_gk, 3), (200000,), 0, 12500, jnp.int32)
        _o = jnp.argsort(dst, stable=True)
        src = src[_o]
        dst = dst[_o]
        edge_attr_16 = 0.000268479 + 0.999861 * jax.random.normal(jax.random.fold_in(_gk, 12), (200000, 16), jnp.float32)
        edge_attr_64 = -5.16925e-05 + 1.00005 * jax.random.normal(jax.random.fold_in(_gk, 13), (200000, 64), jnp.float32)
        edge_weight = jax.random.uniform(jax.random.fold_in(_gk, 15), (200000,), jnp.float32, 0.0, 12)
        return (x, src, dst, edge_attr_16, edge_attr_64, edge_weight)
    x, src, dst, edge_attr_16, edge_attr_64, edge_weight = _rec_inputs()

    def _L0_gnn_setup():
        import jax, jax.numpy as jnp
        import numpy as np
        NEG_SLOPE = 0.2
        key = jax.random.key(seed)
        ks = jax.random.split(key, 8)
        N, E, F_IN, H, D = (12500, 200000, 128, 4, 32)
        x = jax.random.normal(ks[0], (N, F_IN), dtype=jnp.float32)
        src = jax.random.randint(ks[1], (E,), 0, N, dtype=jnp.int32)
        dst = jax.random.randint(ks[2], (E,), 0, N, dtype=jnp.int32)
        s = 1.0 / np.sqrt(F_IN)
        W_src = jax.random.normal(ks[3], (F_IN, H * D), dtype=jnp.float32) * s
        b_src = jax.random.normal(ks[4], (H * D,), dtype=jnp.float32) * 0.02
        W_dst = jax.random.normal(ks[5], (F_IN, H * D), dtype=jnp.float32) * s
        b_dst = jax.random.normal(ks[6], (H * D,), dtype=jnp.float32) * 0.02
        attn = jax.random.normal(ks[7], (H, D), dtype=jnp.float32) * s
        return {'x': x, 'src': src, 'dst': dst, 'W_src': W_src, 'b_src': b_src, 'W_dst': W_dst, 'b_dst': b_dst, 'attn': attn}
    _L0_gnn_all = _L0_gnn_setup()
    _L0_gnn_in = {k: v for k, v in _L0_gnn_all.items() if k in ('W_src', 'b_src', 'W_dst', 'b_dst', 'attn')}
    del _L0_gnn_all

    def _L1_gnn_setup():
        import jax, jax.numpy as jnp
        import numpy as np
        N_NODES = 12500
        N_EDGES = 200000
        IN_CH = 128
        OUT_CH = 128
        EDGE_DIM = 64
        key = jax.random.key(seed)
        ks = jax.random.split(key, 7)
        x = jax.random.normal(ks[0], (N_NODES, IN_CH), dtype=jnp.float32)
        edge_index = jax.random.randint(ks[1], (2, N_EDGES), 0, N_NODES, dtype=jnp.int64)
        edge_attr = jax.random.normal(ks[2], (N_EDGES, EDGE_DIM), dtype=jnp.float32)
        lim1 = 1.0 / np.sqrt(IN_CH)
        W_lin = jax.random.uniform(ks[3], (IN_CH, OUT_CH), minval=-lim1, maxval=lim1, dtype=jnp.float32)
        b_lin = jax.random.uniform(ks[4], (OUT_CH,), minval=-lim1, maxval=lim1, dtype=jnp.float32)
        lim2 = 1.0 / np.sqrt(EDGE_DIM)
        W_edge = jax.random.uniform(ks[5], (EDGE_DIM, OUT_CH), minval=-lim2, maxval=lim2, dtype=jnp.float32)
        b_edge = jax.random.uniform(ks[6], (OUT_CH,), minval=-lim2, maxval=lim2, dtype=jnp.float32)
        return {'x': x, 'edge_index': edge_index, 'edge_attr': edge_attr, 'W_lin': W_lin, 'b_lin': b_lin, 'W_edge': W_edge, 'b_edge': b_edge}
    _L1_gnn_all = _L1_gnn_setup()
    _L1_gnn_in = {k: v for k, v in _L1_gnn_all.items() if k in ('W_lin', 'b_lin', 'W_edge', 'b_edge')}
    del _L1_gnn_all

    def _L2_gnn_setup():
        import jax, jax.numpy as jnp
        import numpy as np
        import math
        N_ATOMS = 5000
        HIDDEN = 128
        NUM_RBF = 50
        CUTOFF = 10.0
        N_EDGES = 80000
        key = jax.random.key(seed)
        ks = jax.random.split(key, 12)
        s = lambda fan_in: 1.0 / np.sqrt(fan_in)
        inp = {'h': jax.random.normal(ks[0], (N_ATOMS, HIDDEN), dtype=jnp.float32), 'edge_index': jax.random.randint(ks[1], (2, N_EDGES), 0, N_ATOMS, dtype=jnp.int64), 'distances': jax.random.uniform(ks[2], (N_EDGES,), dtype=jnp.float32) * 12.0, 'fw1': jax.random.uniform(ks[3], (NUM_RBF, HIDDEN), jnp.float32, -s(NUM_RBF), s(NUM_RBF)), 'fb1': jnp.zeros((HIDDEN,), jnp.float32), 'fw2': jax.random.uniform(ks[4], (HIDDEN, HIDDEN), jnp.float32, -s(HIDDEN), s(HIDDEN)), 'fb2': jnp.zeros((HIDDEN,), jnp.float32), 'pw': jax.random.uniform(ks[5], (HIDDEN, HIDDEN), jnp.float32, -s(HIDDEN), s(HIDDEN)), 'pb': jnp.zeros((HIDDEN,), jnp.float32), 'mw1': jax.random.uniform(ks[6], (HIDDEN, HIDDEN), jnp.float32, -s(HIDDEN), s(HIDDEN)), 'mb1': jnp.zeros((HIDDEN,), jnp.float32), 'mw2': jax.random.uniform(ks[7], (HIDDEN, HIDDEN), jnp.float32, -s(HIDDEN), s(HIDDEN)), 'mb2': jnp.zeros((HIDDEN,), jnp.float32)}
        return inp
    _L2_gnn_all = _L2_gnn_setup()
    _L2_gnn_in = {k: v for k, v in _L2_gnn_all.items() if k in ('fw1', 'fb1', 'fw2', 'fb2', 'pw', 'pb', 'mw1', 'mb1', 'mw2', 'mb2')}
    del _L2_gnn_all

    def _L3_gnn_setup():
        import jax, jax.numpy as jnp
        import numpy as np
        N_NODES = 6250
        N_EDGES = 80000
        IN_DIM = 128
        OUT_DIM = 128
        EDGE_DIM = 16
        N_HEADS = 4
        HEAD_DIM = OUT_DIM // N_HEADS
        LN_EPS = 1e-05

        def _layer_norm(x, scale, bias):
            mu = jnp.mean(x, axis=-1, keepdims=True)
            var = jnp.mean(jnp.square(x - mu), axis=-1, keepdims=True)
            return (x - mu) * jax.lax.rsqrt(var + LN_EPS) * scale + bias
        key = jax.random.key(seed)
        ks = jax.random.split(key, 6)
        h = jax.random.normal(ks[0], (N_NODES, IN_DIM), dtype=jnp.float32)
        edge_index = jax.random.randint(ks[1], (2, N_EDGES), 0, N_NODES, dtype=jnp.int64)
        edge_feat = jax.random.normal(ks[2], (N_EDGES, EDGE_DIM), dtype=jnp.float32)
        W = jax.random.normal(ks[3], (OUT_DIM, IN_DIM), dtype=jnp.float32) * (1.0 / np.sqrt(IN_DIM))
        W_e = jax.random.normal(ks[4], (N_HEADS, EDGE_DIM), dtype=jnp.float32) * (1.0 / np.sqrt(EDGE_DIM))
        a = jax.random.normal(ks[5], (N_HEADS, 2 * HEAD_DIM), dtype=jnp.float32) * (1.0 / np.sqrt(2 * HEAD_DIM))
        ln_scale = jnp.ones((OUT_DIM,), dtype=jnp.float32)
        ln_bias = jnp.zeros((OUT_DIM,), dtype=jnp.float32)
        return {'h': h, 'edge_index': edge_index, 'edge_feat': edge_feat, 'W': W, 'W_e': W_e, 'a': a, 'ln_scale': ln_scale, 'ln_bias': ln_bias}
    _L3_gnn_all = _L3_gnn_setup()
    _L3_gnn_in = {k: v for k, v in _L3_gnn_all.items() if k in ('W', 'W_e', 'a', 'ln_scale', 'ln_bias')}
    del _L3_gnn_all
    return {'x': x, 'src': src, 'dst': dst, 'edge_attr_16': edge_attr_16, 'edge_attr_64': edge_attr_64, 'edge_weight': edge_weight, 'L0_gnn_W_src': _L0_gnn_in['W_src'], 'L0_gnn_b_src': _L0_gnn_in['b_src'], 'L0_gnn_W_dst': _L0_gnn_in['W_dst'], 'L0_gnn_b_dst': _L0_gnn_in['b_dst'], 'L0_gnn_attn': _L0_gnn_in['attn'], 'L1_gnn_W_lin': _L1_gnn_in['W_lin'], 'L1_gnn_b_lin': _L1_gnn_in['b_lin'], 'L1_gnn_W_edge': _L1_gnn_in['W_edge'], 'L1_gnn_b_edge': _L1_gnn_in['b_edge'], 'L2_gnn_fw1': _L2_gnn_in['fw1'], 'L2_gnn_fb1': _L2_gnn_in['fb1'], 'L2_gnn_fw2': _L2_gnn_in['fw2'], 'L2_gnn_fb2': _L2_gnn_in['fb2'], 'L2_gnn_pw': _L2_gnn_in['pw'], 'L2_gnn_pb': _L2_gnn_in['pb'], 'L2_gnn_mw1': _L2_gnn_in['mw1'], 'L2_gnn_mb1': _L2_gnn_in['mb1'], 'L2_gnn_mw2': _L2_gnn_in['mw2'], 'L2_gnn_mb2': _L2_gnn_in['mb2'], 'L3_gnn_W': _L3_gnn_in['W'], 'L3_gnn_W_e': _L3_gnn_in['W_e'], 'L3_gnn_a': _L3_gnn_in['a'], 'L3_gnn_ln_scale': _L3_gnn_in['ln_scale'], 'L3_gnn_ln_bias': _L3_gnn_in['ln_bias']}

def reference(x, src, dst, edge_attr_16, edge_attr_64, edge_weight, L0_gnn_W_src, L0_gnn_b_src, L0_gnn_W_dst, L0_gnn_b_dst, L0_gnn_attn, L1_gnn_W_lin, L1_gnn_b_lin, L1_gnn_W_edge, L1_gnn_b_edge, L2_gnn_fw1, L2_gnn_fb1, L2_gnn_fw2, L2_gnn_fb2, L2_gnn_pw, L2_gnn_pb, L2_gnn_mw1, L2_gnn_mb1, L2_gnn_mw2, L2_gnn_mb2, L3_gnn_W, L3_gnn_W_e, L3_gnn_a, L3_gnn_ln_scale, L3_gnn_ln_bias):
    import jax
    import jax.numpy as jnp

    def _L0_gnn_ref(x, src, dst, W_src, b_src, W_dst, b_dst, attn):
        import jax, jax.numpy as jnp
        import numpy as np
        NEG_SLOPE = 0.2
        N = x.shape[0]
        H, D = attn.shape
        loop = jnp.arange(N, dtype=src.dtype)
        s_idx = jnp.concatenate([src, loop])
        d_idx = jnp.concatenate([dst, loop])
        feat_src = (x @ W_src + b_src).reshape(N, H, D)
        feat_dst = (x @ W_dst + b_dst).reshape(N, H, D)
        e = feat_src[s_idx] + feat_dst[d_idx]
        e = jnp.where(e > 0, e, NEG_SLOPE * e)
        score = jnp.einsum('ehd,hd->eh', e, attn)
        smax = jax.ops.segment_max(score, d_idx, num_segments=N)
        es = jnp.exp(score - smax[d_idx])
        denom = jax.ops.segment_sum(es, d_idx, num_segments=N)
        alpha = es / denom[d_idx]
        msg = alpha[:, :, None] * feat_src[s_idx]
        out = jax.ops.segment_sum(msg, d_idx, num_segments=N)
        out = jax.nn.relu(out)
        return out.reshape(N, H * D)

    def _L1_gnn_ref(x, edge_index, edge_attr, W_lin, b_lin, W_edge, b_edge):
        import jax, jax.numpy as jnp
        import numpy as np
        N_NODES = 12500
        N_EDGES = 200000
        IN_CH = 128
        OUT_CH = 128
        EDGE_DIM = 64
        h = x @ W_lin + b_lin
        row, col = (edge_index[0], edge_index[1])
        x_j = h[col]
        msg = x_j + (edge_attr @ W_edge + b_edge)
        aggr = jax.ops.segment_sum(msg, row, num_segments=h.shape[0])
        return jax.nn.relu(aggr)

    def _L2_gnn_ref(h, edge_index, distances, fw1, fb1, fw2, fb2, pw, pb, mw1, mb1, mw2, mb2):
        import jax, jax.numpy as jnp
        import numpy as np
        import math
        N_ATOMS = 5000
        HIDDEN = 128
        NUM_RBF = 50
        CUTOFF = 10.0
        N_EDGES = 80000
        src, dst = (edge_index[0], edge_index[1])
        num_atoms = h.shape[0]
        width = CUTOFF / NUM_RBF * 0.5
        centers = jnp.linspace(0.0, CUTOFF, NUM_RBF)
        rbf = jnp.exp(-(distances[:, None] - centers) ** 2 / (2.0 * width * width))
        cut = 0.5 * (jnp.cos(jnp.pi * distances / CUTOFF) + 1.0) * (distances <= CUTOFF).astype(h.dtype)
        W = (jax.nn.silu(rbf @ fw1 + fb1) @ fw2 + fb2) * cut[:, None]
        messages = (h[src] @ pw + pb) * W
        agg = jax.ops.segment_sum(messages, dst, num_segments=num_atoms)
        return h + (jax.nn.silu(agg @ mw1 + mb1) @ mw2 + mb2)

    def _L3_gnn_ref(h, edge_index, edge_feat, W, W_e, a, ln_scale, ln_bias):
        import jax, jax.numpy as jnp
        import numpy as np
        N_NODES = 6250
        N_EDGES = 80000
        IN_DIM = 128
        OUT_DIM = 128
        EDGE_DIM = 16
        N_HEADS = 4
        HEAD_DIM = OUT_DIM // N_HEADS
        LN_EPS = 1e-05

        def _layer_norm(x, scale, bias):
            mu = jnp.mean(x, axis=-1, keepdims=True)
            var = jnp.mean(jnp.square(x - mu), axis=-1, keepdims=True)
            return (x - mu) * jax.lax.rsqrt(var + LN_EPS) * scale + bias
        N = h.shape[0]
        H, D = (N_HEADS, HEAD_DIM)
        src, dst = (edge_index[0], edge_index[1])
        Wh = (h @ W.T).reshape(N, H, D)
        Wh_src = Wh[src]
        Wh_dst = Wh[dst]
        attn = (jnp.concatenate([Wh_src, Wh_dst], axis=-1) * a[None]).sum(-1)
        attn = jax.nn.leaky_relu(attn, negative_slope=0.2)
        attn = attn + edge_feat @ W_e.T
        max_v = jax.ops.segment_max(attn, dst, num_segments=N)
        max_v = jnp.maximum(max_v, -1000000000.0)
        exp_v = jnp.exp(attn - max_v[dst])
        denom = jax.ops.segment_sum(exp_v, dst, num_segments=N)
        alpha = exp_v / (denom[dst] + 1e-09)
        agg = jax.ops.segment_sum(alpha[..., None] * Wh_src, dst, num_segments=N)
        out = agg.reshape(N, H * D)
        return _layer_norm(jax.nn.gelu(out, approximate=False), ln_scale, ln_bias)
    edge_index = jnp.stack([src, dst])
    h = jnp.maximum(_layernorm(x, axis=-1), 0.0)
    x = x + _L0_gnn_ref(h, src, dst, L0_gnn_W_src, L0_gnn_b_src, L0_gnn_W_dst, L0_gnn_b_dst, L0_gnn_attn)
    h = jnp.maximum(_layernorm(x, axis=-1), 0.0)
    x = x + _L1_gnn_ref(h, edge_index, edge_attr_64, L1_gnn_W_lin, L1_gnn_b_lin, L1_gnn_W_edge, L1_gnn_b_edge)
    h = jnp.maximum(_layernorm(x, axis=-1), 0.0)
    x = x + _L2_gnn_ref(h, edge_index, edge_weight, L2_gnn_fw1, L2_gnn_fb1, L2_gnn_fw2, L2_gnn_fb2, L2_gnn_pw, L2_gnn_pb, L2_gnn_mw1, L2_gnn_mb1, L2_gnn_mw2, L2_gnn_mb2)
    h = jnp.maximum(_layernorm(x, axis=-1), 0.0)
    x = x + _L3_gnn_ref(h, edge_index, edge_attr_16, L3_gnn_W, L3_gnn_W_e, L3_gnn_a, L3_gnn_ln_scale, L3_gnn_ln_bias)
    return x

_drawn_inputs = setup_inputs


def setup_inputs(seed=0):
    import zlib

    import numpy as np

    out = dict(_drawn_inputs(seed))
    spreads = {'L2_gnn_fb1': (0.0, 0.8),
     'L2_gnn_fb2': (0.0, 0.52),
     'L2_gnn_pb': (0.0, 0.8),
     'L2_gnn_mb1': (0.0, 0.8),
     'L2_gnn_mb2': (0.0, 1.608),
     'L3_gnn_ln_scale': (1.0, 0.6),
     'L3_gnn_ln_bias': (0.0, 1.403)}
    factors = {'edge_weight': 8.0,
     'L0_gnn_b_src': 4.683,
     'L0_gnn_W_dst': 8.0,
     'L0_gnn_b_dst': 64.0,
     'L0_gnn_attn': 3.816,
     'L2_gnn_fw1': 8.0,
     'L2_gnn_fw2': 8.0,
     'L2_gnn_pw': 3.49,
     'L2_gnn_mw1': 3.935,
     'L2_gnn_mw2': 3.291,
     'L3_gnn_a': 13.839,
     'edge_attr_16': 5.048,
     'L3_gnn_W_e': 4.955}
    for name, (base, spread) in spreads.items():
        noise = np.random.default_rng([zlib.crc32(name.encode()), seed]).standard_normal(out[name].shape)
        drawn = base * np.exp(spread * noise) if base else spread * noise
        out[name] = jnp.asarray(drawn.astype(out[name].dtype))
    for name, factor in factors.items():
        out[name] = (out[name] * factor).astype(out[name].dtype)
    return out
```

```python
import concourse.bass as bass
from concourse import mybir
from contextlib import ExitStack

P = 128
HEADS, HDIM = 4, 32
D = HEADS * HDIM
JC = 28
GT = 7
SUMS = 4
BIG = 1.0e38
EPS = 1e-5
PI = 3.141592653589793
FP = mybir.dt.float32
I32 = mybir.dt.int32
ALU = mybir.AluOpType
ACT = mybir.ActivationFunctionType
AX = mybir.AxisListType


class Chain:

    def __init__(self, eng, sem):
        self.eng, self.sem, self.base, self.n = eng, sem, 0, 0

    def loop(self, i, per_turn):
        self.start = self.base + self.n
        self.base = i * per_turn + self.start
        self.n = 0
        self.per_turn = per_turn

    def end(self, turns):
        assert self.n == self.per_turn, (self.n, self.per_turn)
        self.base, self.n = self.start + turns * self.per_turn, 0

    def step(self, ins):
        ins.then_inc(self.sem, 1)
        self.n += 1

    def link(self, ins):
        self.step(ins)
        self.eng.wait_ge(self.sem, self.base + self.n)


class Ctx:
    pass


def bc_mid(ap, n):
    return ap.unsqueeze(1).to_broadcast([ap.shape[0], n, ap.shape[1]])


def bc_last(ap, n):
    return ap.unsqueeze(len(ap.shape)).to_broadcast(list(ap.shape) + [n])


class Phase:

    def __init__(self, nc, name):
        self.nc, self.name, self.stack, self.sems, self.credits = nc, name, ExitStack(), [], []

    def __enter__(self):
        self.stack.__enter__()
        return self

    def __exit__(self, *a):
        self.stack.__exit__(*a)
        if a[0] is None:
            self.nc.clear_and_free_semaphores(self.sems)
            self.nc.all_engine_barrier()

    def sb(self, n, shape, dt=FP):
        return self.stack.enter_context(self.nc.sbuf_tensor(f"{self.name}_{n}", shape, dt))

    def ps(self, n, shape):
        return self.stack.enter_context(self.nc.psum_tensor(f"{self.name}_{n}", shape, FP))

    def sem(self, n, credit=0):
        self.sems.append(self.nc.alloc_semaphore(f"{self.name}_{n}"))
        if credit:
            self.credits.append((self.sems[-1], credit))
        return self.sems[-1]

    def give_credits(self, sp):
        for sem, credit in self.credits:
            sp.sem_inc(sem, credit)

    def block(self):
        return self.stack.enter_context(self.nc.Block())




def setup_phase(nc, k, a):
    S, NT = k.S, k.NT
    with Phase(nc, "setup") as ph:
        dst_i = ph.sb("dst_i", [P, S], I32)
        dst_f = ph.sb("dst_f", [P, S])
        lastd_i = ph.sb("lastd_i", [P, P], I32)
        lastd_f = ph.sb("lastd_f", [P, P])
        col = ph.sb("col", [P, P])
        part = ph.sb("part", [P, 1])
        eqf = ph.sb("eqf", [P, S])
        cnt = ph.sb("cnt", [P, 1])
        rowf = ph.sb("rowf", [P, 1])
        mlow = ph.sb("mlow", [P, P])
        seam_ps = ph.ps("seam_ps", [P, 512])
        w3_ps = ph.ps("w3_ps", [P, 512])
        zrow = ph.sb("zrow", [1, 192])
        fd_i = ph.sb("fd_i", [P, 1], I32)
        wfull = ph.sb("wfull", [P, D])
        acol = ph.sb("acol", [P, 8])
        dist = ph.sb("dist", [P, S])
        dgt = ph.sb("dgt", [P, S])

        dma_in = ph.sem("dma_in")
        acol_zero = ph.sem("acol_zero")
        acol_in = ph.sem("acol_in")
        pool_step = ph.sem("pool_step")
        dve_step = ph.sem("dve_step")
        pe_step = ph.sem("pe_step")
        seamT_ready = ph.sem("seamT_ready")
        cut_arg = ph.sem("cut_arg")
        cut_cos = ph.sem("cut_cos")
        zero_ready = ph.sem("zero_ready")
        zero_out = ph.sem("zero_out")
        waited = ph.sem("waited")
        block = ph.block()
        loads = [
            (dst_i[:, :], a["dst"]), (lastd_i[:, :], a["dst_last"].to_broadcast([P, P])),
            (k.X[:, :, :], a["x"].rearrange("(p t) c -> p t c", t=NT)),
            (k.w0[:, 0:D], a["L0_gnn_W_src"]), (k.w0[:, D:2 * D], a["L0_gnn_W_dst"]),
            (k.b0[:, 0:D], a["L0_gnn_b_src"].to_broadcast([P, D])),
            (k.b0[:, D:2 * D], a["L0_gnn_b_dst"].to_broadcast([P, D])),
            (k.attn[:, :], a["L0_gnn_attn"].rearrange("h d -> (h d)").unsqueeze(0).to_broadcast([P, D])),
            (k.w1[:, :], a["L1_gnn_W_lin"]), (k.b1[:, :], a["L1_gnn_b_lin"].to_broadcast([P, D])),
            (k.we[0:64, :], a["L1_gnn_W_edge"]), (k.we[64:65, :], a["L1_gnn_b_edge"]),
            (k.fw1[0:50, :], a["L2_gnn_fw1"]), (k.fw1[50:51, :], a["L2_gnn_fb1"]),
            (k.fw2[:, :], a["L2_gnn_fw2"]),
            (k.pw[:, :], a["L2_gnn_pw"]), (k.pb[:, :], a["L2_gnn_pb"].to_broadcast([P, D])),
            (k.mw1[:, :], a["L2_gnn_mw1"]), (k.mb1[:, :], a["L2_gnn_mb1"].rearrange("o c -> c o")),
            (k.mw2[:, :], a["L2_gnn_mw2"]), (k.mb2[:, :], a["L2_gnn_mb2"].to_broadcast([P, D])),
            (k.w3[:, 0:D], a["L3_gnn_W_T"]), (wfull[:, :], a["L3_gnn_W"]),
            (k.wet[:, :], a["L3_gnn_W_e_T"]),
            (k.lns[:, :], a["L3_gnn_ln_scale"].to_broadcast([P, D])),
            (k.lnb[:, :], a["L3_gnn_ln_bias"].to_broadcast([P, D])),
            (dist[:, :], a["edge_weight"]),
        ] + [(k.fb2[:, j * D:(j + 1) * D], a["L2_gnn_fb2"]) for j in range(4)]

        @block.sync
        def _(sp):
            ph.give_credits(sp)
            with nc.allow_non_contiguous_dma(reason="a bias column"):
                for out, in_ in loads:
                    sp.dma_start(out, in_).then_inc(dma_in, 16)
            sp.wait_ge(acol_zero, 1)
            with nc.allow_non_contiguous_dma(reason="the attention vectors as columns"):
                for h in range(HEADS):
                    for half in range(2):
                        sp.dma_start(acol[h * HDIM:(h + 1) * HDIM, half * 4 + h:half * 4 + h + 1],
                                     a["L3_gnn_a"][h:h + 1, half * HDIM:(half + 1) * HDIM]
                                     .rearrange("o c -> c o")).then_inc(acol_in, 16)
            sp.wait_ge(zero_ready, 1)
            sp.dma_start(k.rows0[k.EP:k.EP + 1, :], zrow[0:1, 0:136]).then_inc(zero_out, 16)
            sp.dma_start(k.rows2[k.EP:k.EP + 1, :], zrow[0:1, 0:128]).then_inc(zero_out, 16)
            sp.wait_ge(zero_out, 32)

        @block.gpsimd
        def _(pool):
            ch = Chain(pool, pool_step)
            ch.link(pool.memset(k.ident[:, :], 0.0))
            ch.step(pool.affine_select(out=k.ident[:, :], in_=k.ident[:, :], compare_op=ALU.not_equal, fill=1.0,
                                       base=0, pattern=[[-1, P]], channel_multiplier=1))
            ch.step(pool.iota(col[:, :], pattern=[[1, P]], base=0, channel_multiplier=0,
                              allow_small_or_imprecise_dtypes=True))
            ch.step(pool.iota(part[:, :], pattern=[[0, 1]], base=0, channel_multiplier=1,
                              allow_small_or_imprecise_dtypes=True))
            ch.step(pool.iota(rowf[:, :], pattern=[[0, 1]], base=0, channel_multiplier=S,
                              allow_small_or_imprecise_dtypes=True))
            ch.step(pool.iota(k.node[:, :], pattern=[[1, NT]], base=0, channel_multiplier=NT,
                              allow_small_or_imprecise_dtypes=True))

        @block.vector
        def _(v):
            ch = Chain(v, dve_step)
            v.memset(acol[:, :], 0.0).then_inc(acol_zero, 1)
            ch.step(v.memset(k.ones[:, :], 1.0))
            ch.link(v.memset(zrow[:, :], 0.0))
            v.memset(zrow[:, 132:136], -BIG).then_inc(zero_ready, 1)
            v.wait_ge(dma_in, 16 * len(loads))
            v.wait_ge(pool_step, 6)
            ch.link(v.scalar_tensor_tensor(out=dgt[:, :], in0=dist[:, :], scalar=-1.0, in1=dist[:, :], op0=ALU.mult, op1=ALU.max))
            ch.link(v.tensor_scalar(dgt[:, :], dgt[:, :], 10.0, -PI / 10.0, ALU.min, ALU.mult))
            ch.link(v.tensor_scalar(dgt[:, :], dgt[:, :], PI / 2, None, ALU.add))
            v.tensor_scalar(dist[:, :], dist[:, :], 10.0, 0.5, ALU.is_le, ALU.mult).then_inc(cut_arg, 1)
            ch.link(v.tensor_scalar(k.rbf_bias[0:51, :], part[0:51, :], -10.0 / 49.0, None, ALU.mult))
            ch.link(v.tensor_scalar(k.rbf_scale[0:51, :], part[0:51, :], 49.5, None, ALU.is_lt))
            ch.link(v.tensor_tensor(k.rbf_bias[0:51, :], k.rbf_bias[0:51, :], k.rbf_scale[0:51, :], ALU.mult))
            ch.link(v.tensor_copy(dst_f[:, :], dst_i[:, :]))
            ch.step(v.memset(k.keep[:, 0:1], 0.0))
            ch.step(v.memset(k.keep[:, S:S + 1], 0.0))
            ch.link(v.tensor_tensor(k.keep[:, 1:S], dst_f[:, 1:S], dst_f[:, 0:S - 1], ALU.is_equal))
            ch.link(v.tensor_tensor(eqf[:, :], dst_f[:, :], dst_f[:, 0:1].to_broadcast([P, S]), ALU.is_equal))
            ch.link(v.tensor_reduce(out=cnt[:, :], in_=eqf[:, :], op=ALU.add, axis=AX.X))
            ch.link(v.scalar_tensor_tensor(out=cnt[:, :], in0=cnt[:, :], scalar=-1.0, in1=rowf[:, :],
                                           op0=ALU.add, op1=ALU.add))
            ch.link(v.tensor_copy(k.seam_row[:, :], cnt[:, :]))
            ch.link(v.tensor_copy(k.first_dst[:, :], dst_i[:, 0:1]))
            ch.link(v.tensor_copy(lastd_f[:, :], lastd_i[:, :]))
            ch.link(v.tensor_scalar(mlow[:, :], col[:, :], part[:, 0:1], None, ALU.is_lt))
            v.scalar_tensor_tensor(out=k.seamT[:, :], in0=lastd_f[:, :], scalar=dst_f[:, 0:1],
                                   in1=mlow[:, :], op0=ALU.is_equal, op1=ALU.mult).then_inc(seamT_ready, 1)
            ch.step(v.tensor_copy(k.before[:, :], mlow[:, :]))
            ch.link(v.tensor_scalar(k.trash[:, :], part[:, :], float(P * NT), None, ALU.add))
            v.wait_ge(pe_step, 1)
            ch.link(v.tensor_copy(k.seam[:, :], seam_ps[:, 0:P]))
            v.wait_ge(pe_step, 2)
            ch.link(v.tensor_copy(k.w3[:, D:D + 8], w3_ps[:, 0:8]))
            v.wait_ge(cut_cos, 1)
            ch.link(v.scalar_tensor_tensor(out=k.cut[:, :], in0=dgt[:, :], scalar=1.0, in1=dist[:, :],
                                           op0=ALU.add, op1=ALU.mult))

        @block.scalar
        def _(act):
            act.wait_ge(cut_arg, 1)
            act.activation(dgt[:, :], dgt[:, :], ACT.Sin).then_inc(cut_cos, 1)

        @block.tensor
        def _(pe):
            pe.wait_ge(pool_step, 6)
            pe.wait_ge(seamT_ready, 1)
            pe.transpose(seam_ps[:, 0:P], k.seamT[:, :], k.ident[:, :]).then_inc(pe_step, 1)
            pe.wait_ge(dma_in, 16 * len(loads))
            pe.wait_ge(acol_in, 128)
            pe.matmul(w3_ps[:, 0:8], wfull[:, :], acol[:, :], start=True, stop=True).then_inc(pe_step, 1)


def ends_phase(nc, k, a):
    S, NT, NG = k.S, k.NT, k.NG
    with Phase(nc, "ends") as ph:
        coarse_i = ph.sb("coarse_i", [P, S], I32)
        coarse = ph.sb("coarse", [P, S])
        below = ph.sb("below", [P, S])
        blk = ph.sb("blk", [P, NT])
        blk_i = ph.sb("blk_i", [P, NT], I32)
        bidx = ph.sb("bidx", [P, GT], I32)
        fine_i = ph.sb("fine_i", [P, GT, P], I32)
        fine = ph.sb("fine", [P, GT, P])
        le = ph.sb("le", [P, GT, P])
        c2 = ph.sb("c2", [P, NT])
        cnt = ph.sb("cnt", [P, NT])
        prev = ph.sb("prev", [P, NT])
        has = ph.sb("has", [P, NT])
        tmp = ph.sb("tmp", [P, NT])
        zero1 = ph.sb("zero1", [1, 1])
        coarse_in = ph.sem("coarse_in")
        dve_step = ph.sem("dve_step")
        blocks_found = ph.sem("blocks_found")
        bidx_ready = ph.sem("bidx_ready")
        fine_in = ph.sem("fine_in")
        fine_used = ph.sem("fine_used", credit=1)
        cnt_ready = ph.sem("cnt_ready")
        cnt_out = ph.sem("cnt_out")
        prev_in = ph.sem("prev_in")
        waited = ph.sem("waited")
        block = ph.block()

        @block.sync
        def _(sp):
            ph.give_credits(sp)
            sp.dma_start(coarse_i[:, :], a["dst_coarse"].to_broadcast([P, S])).then_inc(coarse_in, 16)
            sp.wait_ge(cnt_ready, 1)
            sp.dma_start(k.counts[0:1, 0:1], zero1[:, :]).then_inc(cnt_out, 16)
            sp.dma_start(k.counts[0:1, 1:1 + P * NT].rearrange("o (p t) -> (o p) t", t=NT), cnt[:, :]).then_inc(cnt_out, 16)
            sp.wait_ge(cnt_out, 32)
            sp.dma_start(prev[:, :], k.counts[0:1, 0:P * NT].rearrange("o (p t) -> (o p) t", t=NT)).then_inc(prev_in, 16)
            sp.wait_ge(prev_in, 16)

        @block.gpsimd
        def _(pool):
            pool.wait_ge(blocks_found, 1)
            with pool.Fori(0, NG) as g:
                pool.wait_ge(fine_used, g + 1)
                pool.tensor_copy(bidx[:, :], blk_i[:, bass.ds(g * GT, GT)]).then_inc(bidx_ready, 1)
                pool.wait_ge(bidx_ready, g + 1)
                pool.sem_inc(waited, 1)
                for t in range(GT):
                    pool.indirect_dma_start(fine_i[:, t, :], None, a["dst_blocks"],
                                            bass.IndirectOffsetOnAxis(ap=bidx[:, t:t + 1], axis=0)).then_inc(fine_in, 16)

        @block.vector
        def _(v):
            ch = Chain(v, dve_step)
            ch.step(v.memset(zero1[:, :], 0.0))
            v.wait_ge(coarse_in, 16)
            ch.link(v.tensor_copy(coarse[:, :], coarse_i[:, :]))
            with v.Fori(0, NT) as t:
                ch.loop(t, 2)
                ch.link(v.tensor_scalar(below[:, :], coarse[:, :], k.node[:, bass.ds(t, 1)], None, ALU.is_le))
                v.sem_inc(waited, 1)
                ch.link(v.tensor_reduce(out=blk[:, bass.ds(t, 1)], in_=below[:, :], op=ALU.add, axis=AX.X))
            ch.end(NT)
            ch.link(v.tensor_scalar(blk[:, :], blk[:, :], -1.0, 0.0, ALU.add, ALU.max))
            v.tensor_copy(blk_i[:, :], blk[:, :]).then_inc(blocks_found, 1)
            with v.Fori(0, NG) as g:
                ch.loop(g, 2)
                v.wait_ge(fine_in, g * (16 * GT) + 16 * GT)
                ch.link(v.tensor_copy(fine[:, :, :], fine_i[:, :, :]))
                ch.link(v.tensor_tensor(le[:, :, :], fine[:, :, :], bc_last(k.node[:, bass.ds(g * GT, GT)], P), ALU.is_le))
                v.sem_inc(waited, 1)
                v.tensor_reduce(out=c2[:, bass.ds(g * GT, GT)], in_=le[:, :, :], op=ALU.add, axis=AX.X).then_inc(fine_used, 1)
                v.wait_ge(fine_used, g + 2)
            ch.end(NG)
            v.scalar_tensor_tensor(out=cnt[:, :], in0=blk[:, :], scalar=float(P), in1=c2[:, :],
                                   op0=ALU.mult, op1=ALU.add).then_inc(cnt_ready, 1)
            v.wait_ge(cnt_ready, 1)
            v.wait_ge(prev_in, 16)
            ch.link(v.tensor_tensor(k.deg[:, :], cnt[:, :], prev[:, :], ALU.subtract))
            ch.link(v.tensor_scalar(has[:, :], k.deg[:, :], 0.5, None, ALU.is_gt))
            ch.link(v.tensor_scalar(tmp[:, :], cnt[:, :], -1.0 - k.EP, None, ALU.add))
            ch.link(v.tensor_tensor(tmp[:, :], tmp[:, :], has[:, :], ALU.mult))
            ch.link(v.tensor_scalar(tmp[:, :], tmp[:, :], float(k.EP), None, ALU.add))
            ch.link(v.tensor_copy(k.end_row[:, :], tmp[:, :]))
            ch.link(v.tensor_tensor(tmp[:, :], prev[:, :], k.node[:, :], ALU.subtract))
            ch.link(v.tensor_scalar(tmp[:, :], tmp[:, :], -float(k.EP), None, ALU.add))
            ch.link(v.tensor_tensor(tmp[:, :], tmp[:, :], has[:, :], ALU.mult))
            ch.link(v.tensor_tensor(tmp[:, :], tmp[:, :], k.node[:, :], ALU.add))
            ch.link(v.tensor_scalar(tmp[:, :], tmp[:, :], float(k.EP), None, ALU.add))
            ch.link(v.tensor_copy(k.start_row[:, :], tmp[:, :]))




def node_phase(nc, k, a, post, pre):
    NT, NG = k.NT, k.NG
    W = {None: 0, 0: 136, 1: 0, 2: 128, 3: 136}[post]
    NC = {0: 256, 1: 128, 2: 128, 3: 136, None: 0}[pre]
    ST = {0: 256, 1: 128, 2: 128, 3: 256, None: 0}[pre]
    rows = {0: k.rows0, 1: None, 2: k.rows2, 3: k.rows0, None: None}[post]
    GW = {0: 136, 1: 0, 2: 128, 3: 136, None: 0}[post]
    n_out = {0: 32, 1: 16, 2: 16, 3: 32, None: 16}[pre]
    with Phase(nc, f"n{post}{pre}") as ph:
        N3 = [P, GT, D]
        s7, m7, v7, r7 = (ph.sb(x, [P, GT]) for x in ("s7", "m7", "v7", "r7"))
        cen, sq, h = ph.sb("cen", N3), ph.sb("sq", N3), ph.sb("h", N3)
        hT = ph.sb("hT", [P, GT * P])
        psA = ph.ps("psA", [P, 1024])
        psB = ph.ps("psB", [P, 1024])
        psC = ph.ps("psC", [P, 2048])
        if post is not None:
            y = ph.sb("y", N3)
        if post == 1:
            part = ph.sb("part", [P, SUMS, GT, D])
            y2 = ph.sb("y2", N3)
        elif post is not None:
            rg = ph.sb("rg", [P, GT, W])
            gidx = ph.sb("gidx", [P, GT], I32)
        if post == 0:
            fsn = ph.sb("fsn", N3)
            mx = ph.sb("mx", [P, GT, HEADS])
            ex = ph.sb("ex", [P, 2, GT * HEADS])
            den = ph.sb("den", [P, GT * HEADS])
        if post == 3:
            den = ph.sb("den", [P, GT, HEADS])
        if post == 2:
            aT = ph.sb("aT", [P, GT * P])
            uT = ph.sb("uT", [P, GT * P])
        if pre is not None:
            tab = ph.sb("tab", [P, GT, NC])
        if pre == 0:
            e = ph.sb("e", N3)

        dve_step = ph.sem("dve_step")
        gidx_ready, rows_in, rows_used = ph.sem("gidx_ready"), ph.sem("rows_in"), ph.sem("rows_used", credit=1)
        fsn_in, fsn_used = ph.sem("fsn_in"), ph.sem("fsn_used", credit=1)
        ex_arg, ex_done = ph.sem("ex_arg"), ph.sem("ex_done")
        aT_ps, aT_ready, post_mm = ph.sem("aT_ps"), ph.sem("aT_ready"), ph.sem("post_mm")
        z_ps, u_ready = ph.sem("z_ps"), ph.sem("u_ready")
        x_done = ph.sem("x_done")
        cen_ready, sq_ready, var_ready, std_ready = ph.sem("cen_ready"), ph.sem("sq_ready"), ph.sem("var_ready"), ph.sem("std_ready")
        h_ready, hT_ps, hT_ready = ph.sem("h_ready"), ph.sem("hT_ps"), ph.sem("hT_ready")
        tab_ps, tab_ready, tab_out = ph.sem("tab_ps"), ph.sem("tab_ready", credit=1), ph.sem("tab_out", credit=n_out)
        gelu_arg, gelu_done = ph.sem("gelu_arg"), ph.sem("gelu_done")
        waited = ph.sem("waited")
        block = ph.block()
        fs_v = k.tab0s.rearrange("(p t) c -> p t c", t=NT)
        fd_v = k.tab0d.rearrange("(p t) c -> p t c", t=NT)
        t1_v = k.tab1.rearrange("(p t) c -> p t c", t=NT)
        t3_v = k.tab3.rearrange("(p t) c -> p t c", t=NT)
        ar_v = k.ar_tab.rearrange("(p t) c -> p t c", t=NT)
        out_v = a["out"].rearrange("(p t) c -> p t c", t=NT)

        @block.sync
        def _(sp):
            ph.give_credits(sp)
            with sp.Fori(0, NG) as g:
                if post == 1:
                    sp.wait_ge(rows_used, g + 1)
                    for t in range(SUMS):
                        sp.dma_start(part[:, t, :, :], k.by_src[t][0:P * NT, :].rearrange("(p t) c -> p t c", t=NT)[:, bass.ds(g * GT, GT), :]).then_inc(rows_in, 16)
                if post == 0:
                    sp.wait_ge(fsn_used, g + 1)
                    sp.dma_start(fsn[:, :, :], fs_v[:, bass.ds(g * GT, GT), :]).then_inc(fsn_in, 16)
                if pre is not None:
                    sp.wait_ge(tab_ready, g + 2)
                if pre == 0:
                    sp.dma_start(fs_v[:, bass.ds(g * GT, GT), :], tab[:, :, 0:D]).then_inc(tab_out, 16)
                    sp.dma_start(fd_v[:, bass.ds(g * GT, GT), :], tab[:, :, D:2 * D]).then_inc(tab_out, 16)
                elif pre in (1, 2):
                    sp.dma_start(t1_v[:, bass.ds(g * GT, GT), :], tab[:, :, :]).then_inc(tab_out, 16)
                elif pre == 3:
                    sp.dma_start(t3_v[:, bass.ds(g * GT, GT), :], tab[:, :, 0:132]).then_inc(tab_out, 16)
                    sp.dma_start(ar_v[:, bass.ds(g * GT, GT), :], tab[:, :, 132:136]).then_inc(tab_out, 16)
                else:
                    sp.wait_ge(x_done, g + 1)
                    sp.sem_inc(waited, 1)
                    sp.dma_start(out_v[:, bass.ds(g * GT, GT), :], k.X[:, bass.ds(g * GT, GT), :]).then_inc(tab_out, 16)
                sp.wait_ge(tab_out, g * n_out + 2 * n_out)
                sp.sem_inc(waited, 1)

        @block.gpsimd
        def _(pool):
            if post in (None, 1):
                return
            with pool.Fori(0, NG) as g:
                pool.wait_ge(rows_used, g + 1)
                pool.tensor_copy(gidx[:, :], k.end_row[:, bass.ds(g * GT, GT)]).then_inc(gidx_ready, 1)
                pool.wait_ge(gidx_ready, g + 1)
                pool.sem_inc(waited, 1)
                for t in range(GT):
                    pool.indirect_dma_start(rg[:, t, 0:GW], None, rows,
                                            bass.IndirectOffsetOnAxis(ap=gidx[:, t:t + 1], axis=0)).then_inc(rows_in, 16)

        @block.vector
        def _(v):
            ch = Chain(v, dve_step)
            turn = {None: 0, 0: 6, 1: 2, 2: 1, 3: 9}[post] + {0: 8, 1: 4, 2: 5, 3: 4, None: 0}[pre]
            with v.Fori(0, NG) as g:
                ch.loop(g, turn)
                xg = k.X[:, bass.ds(g * GT, GT), :]
                if post == 1:
                    v.wait_ge(rows_in, g * (16 * SUMS) + 16 * SUMS)
                elif post is not None:
                    v.wait_ge(rows_in, g * (16 * GT) + 16 * GT)
                if post == 0:
                    ss = k.sself[:, bass.ds(g * GT, GT), :]
                    flat = "p t h -> p (t h)"
                    ch.link(v.tensor_tensor(mx[:, :, :], rg[:, :, 132:136], ss, ALU.max))
                    ch.step(v.tensor_tensor(ex[:, 0, :].rearrange("p (t h) -> p t h", h=HEADS), rg[:, :, 132:136], mx[:, :, :], ALU.subtract))
                    v.tensor_tensor(ex[:, 1, :].rearrange("p (t h) -> p t h", h=HEADS), ss, mx[:, :, :], ALU.subtract).then_inc(ex_arg, 1)
                    v.wait_ge(ex_done, g + 1)
                    d3 = den[:, :].rearrange("p (t h) -> p t h", h=HEADS)
                    ch.link(v.tensor_tensor(d3, rg[:, :, 128:132], ex[:, 0, :].rearrange("p (t h) -> p t h", h=HEADS), ALU.mult))
                    ch.link(v.tensor_tensor(den[:, :], den[:, :], ex[:, 1, :], ALU.add))
                    ch.link(v.reciprocal(den[:, :], den[:, :]))
                    ch.link(v.tensor_tensor(ex[:, :, :], ex[:, :, :], bc_mid(den[:, :], 2), ALU.mult))
                    q4 = "p t (h c) -> p (t h) c"
                    a4 = rg[:, :, 0:D].rearrange("p t (h c) -> p t h c", h=HEADS)
                    v.tensor_tensor(y[:, :, :].rearrange("p t (h c) -> p t h c", h=HEADS), a4,
                                    bc_last(ex[:, 0, :].rearrange("p (t h) -> p t h", h=HEADS), HDIM), ALU.mult).then_inc(rows_used, 1)
                    v.wait_ge(fsn_in, g * 16 + 16)
                    v.tensor_tensor(cen[:, :, :].rearrange(q4, h=HEADS), fsn[:, :, :].rearrange(q4, h=HEADS),
                                    bc_last(ex[:, 1, :], HDIM), ALU.mult).then_inc(fsn_used, 1)
                    v.wait_ge(rows_used, g + 2)
                    v.wait_ge(fsn_used, g + 2)
                    v.tensor_tensor(y[:, :, :], y[:, :, :], cen[:, :, :], ALU.add).then_inc(post_mm, 1)
                    v.wait_ge(post_mm, g + 1)
                    v.scalar_tensor_tensor(out=xg, in0=y[:, :, :], scalar=0.0, in1=xg, op0=ALU.max, op1=ALU.add).then_inc(x_done, 1)
                    v.wait_ge(x_done, g + 1)
                elif post == 1:
                    ch.step(v.tensor_tensor(y[:, :, :], part[:, 0, :, :], part[:, 1, :, :], ALU.add))
                    v.tensor_tensor(y2[:, :, :], part[:, 2, :, :], part[:, 3, :, :], ALU.add).then_inc(rows_used, 1)
                    v.wait_ge(rows_used, g + 2)
                    ch.link(v.tensor_tensor(y[:, :, :], y[:, :, :], y2[:, :, :], ALU.add))
                    v.scalar_tensor_tensor(out=xg, in0=y[:, :, :], scalar=0.0, in1=xg, op0=ALU.max, op1=ALU.add).then_inc(x_done, 1)
                    v.wait_ge(x_done, g + 1)
                elif post == 2:
                    v.wait_ge(post_mm, g + 1)
                    ch.link(v.tensor_tensor(y[:, :, :], psC[:, 0:GT * D].rearrange("p (t c) -> p t c", c=D), bc_mid(k.mb2[:, :], GT), ALU.add))
                    v.tensor_tensor(xg, y[:, :, :], xg, ALU.add).then_inc(x_done, 1)
                    v.wait_ge(x_done, g + 1)
                elif post == 3:
                    ch.link(v.tensor_scalar(den[:, :, :], rg[:, :, 128:132], 1e-9, None, ALU.add))
                    ch.link(v.reciprocal(den[:, :, :], den[:, :, :]))
                    v.tensor_tensor(y[:, :, :].rearrange("p t (h c) -> p t h c", h=HEADS),
                                    rg[:, :, 0:D].rearrange("p t (h c) -> p t h c", h=HEADS),
                                    bc_last(den[:, :, :], HDIM), ALU.mult).then_inc(rows_used, 1)
                    v.wait_ge(gelu_done, g + 1)
                    ch.link(v.tensor_reduce(out=s7[:, :], in_=y[:, :, :], op=ALU.add, axis=AX.X))
                    ch.link(v.tensor_scalar(m7[:, :], s7[:, :], 1.0 / D, None, ALU.mult))
                    v.tensor_tensor(cen[:, :, :], y[:, :, :], bc_last(m7[:, :], D), ALU.subtract).then_inc(cen_ready, 1)
                    v.wait_ge(sq_ready, g + 1)
                    ch.link(v.tensor_reduce(out=s7[:, :], in_=sq[:, :, :], op=ALU.add, axis=AX.X))
                    v.tensor_scalar(v7[:, :], s7[:, :], 1.0 / D, EPS, ALU.mult, ALU.add).then_inc(var_ready, 1)
                    v.wait_ge(std_ready, g + 1)
                    ch.link(v.reciprocal(r7[:, :], v7[:, :]))
                    ch.link(v.tensor_tensor(cen[:, :, :], cen[:, :, :], bc_last(r7[:, :], D), ALU.mult))
                    ch.link(v.tensor_tensor(cen[:, :, :], cen[:, :, :], bc_mid(k.lns[:, :], GT), ALU.mult))
                    ch.link(v.tensor_tensor(cen[:, :, :], cen[:, :, :], bc_mid(k.lnb[:, :], GT), ALU.add))
                    v.tensor_tensor(xg, cen[:, :, :], xg, ALU.add).then_inc(x_done, 1)
                    v.wait_ge(x_done, g + 1)
                if pre is not None:
                    v.sem_inc(waited, 1)
                    ch.link(v.tensor_reduce(out=s7[:, :], in_=xg, op=ALU.add, axis=AX.X))
                    ch.link(v.tensor_scalar(m7[:, :], s7[:, :], 1.0 / D, None, ALU.mult))
                    v.tensor_tensor(cen[:, :, :], xg, bc_last(m7[:, :], D), ALU.subtract).then_inc(cen_ready, 1)
                    v.wait_ge(sq_ready, g + 1)
                    ch.link(v.tensor_reduce(out=s7[:, :], in_=sq[:, :, :], op=ALU.add, axis=AX.X))
                    v.tensor_scalar(v7[:, :], s7[:, :], 1.0 / D, EPS, ALU.mult, ALU.add).then_inc(var_ready, 1)
                    v.wait_ge(std_ready, g + 1)
                    ch.link(v.reciprocal(r7[:, :], v7[:, :]))
                    v.scalar_tensor_tensor(out=h[:, :, :], in0=cen[:, :, :], scalar=0.0, in1=bc_last(r7[:, :], D),
                                           op0=ALU.max, op1=ALU.mult).then_inc(h_ready, 1)
                    if pre == 2:
                        v.wait_ge(h_ready, g + 1)
                        ch.link(v.tensor_tensor(xg, xg, h[:, :, :], ALU.add))
                    v.wait_ge(tab_ps, g + 1)
                    v.wait_ge(tab_out, g * n_out + n_out)
                    pc = psC[:, 0:GT * ST].rearrange("p (t c) -> p t c", c=ST)[:, :, 0:NC]
                    if pre == 3:
                        v.tensor_copy(tab[:, :, :], pc).then_inc(tab_ready, 1)
                    else:
                        bias = {0: k.b0, 1: k.b1, 2: k.pb}[pre]
                        v.tensor_tensor(tab[:, :, :], pc, bc_mid(bias[:, :], GT), ALU.add).then_inc(tab_ready, 1)
                    if pre == 3:
                        v.wait_ge(tab_ready, g + 2)
                    if pre == 0:
                        v.wait_ge(tab_ready, g + 2)
                        ch.link(v.tensor_tensor(e[:, :, :], tab[:, :, 0:D], tab[:, :, D:2 * D], ALU.add))
                        ch.link(v.scalar_tensor_tensor(out=e[:, :, :], in0=e[:, :, :], scalar=0.2, in1=e[:, :, :], op0=ALU.mult, op1=ALU.max))
                        ch.link(v.tensor_tensor(e[:, :, :], e[:, :, :], bc_mid(k.attn[:, :], GT), ALU.mult))
                        v.sem_inc(waited, 1)
                        ch.link(v.tensor_reduce(out=k.sself[:, bass.ds(g * GT, GT), :], in_=e[:, :, :].rearrange("p t (h c) -> p t h c", h=HEADS),
                                                op=ALU.add, axis=AX.X))
            ch.end(NG)

        @block.scalar
        def _(act):
            with act.Fori(0, NG) as g:
                if post == 0:
                    act.wait_ge(ex_arg, g + 1)
                    act.activation(ex[:, :, :], ex[:, :, :], ACT.Exp).then_inc(ex_done, 1)
                if post == 2:
                    act.wait_ge(aT_ps, g + 1)
                    act.activation(aT[:, :], psA[:, 0:GT * P], ACT.Copy).then_inc(aT_ready, 1)
                    act.wait_ge(z_ps, g + 1)
                    act.activation(uT[:, :], psB[:, 0:GT * P], ACT.Silu, bias=k.mb1[:, 0:1]).then_inc(u_ready, 1)
                if post == 3:
                    act.wait_ge(rows_used, g + 2)
                    act.activation(y[:, :, :], y[:, :, :], ACT.Gelu).then_inc(gelu_done, 1)
                if pre is not None or post == 3:
                    act.wait_ge(cen_ready, g + 1)
                    act.activation(sq[:, :, :], cen[:, :, :], ACT.Square).then_inc(sq_ready, 1)
                    act.wait_ge(var_ready, g + 1)
                    act.activation(v7[:, :], v7[:, :], ACT.Sqrt).then_inc(std_ready, 1)
                if pre is not None:
                    act.wait_ge(hT_ps, g + 1)
                    act.activation(hT[:, :], psA[:, 0:GT * P], ACT.Copy).then_inc(hT_ready, 1)

        @block.tensor
        def _(pe):
            if post is None and pre is None:
                return
            with pe.Fori(0, NG) as g:
                if post == 2:
                    pe.wait_ge(rows_in, g * (16 * GT) + 16 * GT)
                    for t in range(GT):
                        last = pe.transpose(psA[:, t * P:(t + 1) * P], rg[:, t, :], k.ident[:, :])
                    last.then_inc(aT_ps, 1)
                    pe.wait_ge(aT_ps, g + 1)
                    pe.sem_inc(rows_used, 1)
                    pe.wait_ge(aT_ready, g + 1)
                    pe.matmul(psB[:, 0:512], k.mw1[:, :], aT[:, 0:512], start=True, stop=True)
                    pe.matmul(psB[:, 512:GT * P], k.mw1[:, :], aT[:, 512:GT * P], start=True, stop=True).then_inc(z_ps, 1)
                    pe.wait_ge(u_ready, g + 1)
                    if pre is not None:
                        pe.wait_ge(tab_ready, g + 1)
                    for t in range(GT):
                        last = pe.matmul(psC[:, t * D:(t + 1) * D], uT[:, t * P:(t + 1) * P], k.mw2[:, :], start=True, stop=True)
                    last.then_inc(post_mm, 1)
                if pre is not None:
                    w = {0: k.w0, 1: k.w1, 2: k.pw, 3: k.w3}[pre]
                    pe.wait_ge(h_ready, g + 1)
                    for t in range(GT):
                        last = pe.transpose(psA[:, t * P:(t + 1) * P], h[:, t, :], k.ident[:, :])
                    last.then_inc(hT_ps, 1)
                    pe.wait_ge(hT_ready, g + 1)
                    pe.wait_ge(tab_ready, g + 1)
                    for t in range(GT):
                        last = pe.matmul(psC[:, t * ST:t * ST + NC], hT[:, t * P:(t + 1) * P], w[:, 0:NC], start=True, stop=True)
                    last.then_inc(tab_ps, 1)




def edge_phase(nc, k, a, layer):
    S, TURNS = k.S, k.TURNS
    SOFT = layer in (0, 3)
    W = {0: 136, 2: 128, 3: 136}[layer]
    SUM = {0: 132, 2: 128, 3: 132}[layer]
    GC = {0: 128, 2: 128, 3: 132}[layer]
    table = {0: k.tab0s, 2: k.tab1, 3: k.tab3}[layer]
    rows = {0: k.rows0, 2: k.rows2, 3: k.rows0}[layer]
    rows_v = rows[0:k.EP, :].rearrange("(p s) c -> p s c", s=S)
    with Phase(nc, f"e{layer}") as ph:
        R = [ph.sb(f"row{q}", [P, JC, W]) for q in range(2)]
        sidx = [ph.sb(f"sidx{q}", [P, JC], I32) for q in range(2)]
        kb = [ph.sb(f"kb{q}", [P, JC + 1]) for q in range(2)]
        last = k.last
        carry = ph.sb("carry", [P, 132])
        if layer == 0:
            didx = [ph.sb(f"didx{q}", [P, JC], I32) for q in range(2)]
            E = [ph.sb(f"e{q}", [P, JC, D]) for q in range(2)]
        if SOFT:
            ng = ph.sb("ng", [P, JC + 1])
            sc, run, M = (ph.sb(x, [P, HEADS, JC]) for x in ("sc", "run", "M"))
            df = [ph.sb(f"df{q}", [P, HEADS, JC + 1]) for q in range(2)]
            rc = ph.sb("rc", [P, HEADS])
        if layer == 3:
            floor = ph.sb("floor", [P, HEADS, JC])
            eft = [ph.sb(f"eft{q}", [16, JC * P]) for q in range(2)]
            efp = [ph.ps(f"efp{q}", [P, 512]) for q in range(2)]
        if layer == 2:
            cb = [ph.sb(f"cb{q}", [P, JC]) for q in range(2)]
            dist = ph.sb("dist", [51, JC * P])
            rbf = ph.sb("rbf", [51, JC * P])
            u = ph.sb("u", [P, JC * P])
            NB = JC // 4
            zps = ph.ps("zps", [P, 2048])
            wps = ph.ps("wps", [P, 2048])
            dist_in, dist_used = ph.sem("dist_in"), ph.sem("dist_used")
            rbf_ready = ph.sem("rbf_ready")
            z_ready, u_ready, w_ready, w_used = (ph.sem(x, credit=NB) for x in ("z_ready", "u_ready", "w_ready", "w_used"))

        dve_step = ph.sem("dve_step")
        idx_in = [ph.sem(f"idx_in{q}") for q in range(2)]
        rows_in = [ph.sem(f"rows_in{q}") for q in range(2)]
        attr_in = [ph.sem(f"attr_in{q}") for q in range(2)]
        dstrow_in = [ph.sem(f"dstrow_in{q}") for q in range(2)]
        e_used = [ph.sem(f"e_used{q}", credit=1) for q in range(2)]
        rows_out = [ph.sem(f"rows_out{q}", credit=16) for q in range(2)]
        summed = ph.sem("summed")
        exp_arg, exp_done = ph.sem("exp_arg"), ph.sem("exp_done")
        efp_ready, efp_used = ([ph.sem(f"{n}{q}", credit=1) for q in range(2)] for n in ("efp_ready", "efp_used"))
        waited = ph.sem("waited")
        block = ph.block()
        n_idx = 32 if layer == 0 else 16

        @block.sync
        def _(sp):
            ph.give_credits(sp)
            def load_idx(q, at):
                sp.dma_start(sidx[q][:, :], a["src"][:, at]).then_inc(idx_in[q], 16)
                if layer == 0:
                    sp.dma_start(didx[q][:, :], a["dst_pad"][:, at]).then_inc(idx_in[q], 16)

            for q in range(2):
                load_idx(q, bass.ds(q * JC, JC))
            if layer == 2:
                sp.dma_start(dist[:, :], a["dist_T"][0:1, 0:JC * P].to_broadcast([51, JC * P])).then_inc(dist_in, 16)
            with sp.Fori(0, TURNS) as i:
                for q in range(2):
                    if layer == 3:
                        sp.wait_ge(efp_ready[q], i + 1)
                        sp.dma_start(eft[q][:, :], a["edge_attr_16_T"][:, bass.ds((i * 2 + q) * (JC * P), JC * P)]).then_inc(attr_in[q], 16)
                for q in range(2):
                    sp.wait_ge(rows_in[q], (i + 1) * (16 * JC))
                    if layer == 0:
                        sp.wait_ge(dstrow_in[q], (i + 1) * (16 * JC))
                    load_idx(q, bass.ds((i + 1) * (2 * JC) + q * JC, JC))
                    if layer == 2:
                        sp.wait_ge(dist_used, i * 2 + q + 1)
                        sp.dma_start(dist[:, :], a["dist_T"][0:1, bass.ds((i * 2 + q + 1) * (JC * P), JC * P)].to_broadcast([51, JC * P])).then_inc(dist_in, 16)
                    sp.wait_ge(summed, i * 2 + q + 1)
                    sp.dma_start(rows_v[:, bass.ds(i * (2 * JC) + q * JC, JC), :], R[q][:, :, :]).then_inc(rows_out[q], 16)
            for q in range(2):
                sp.wait_ge(rows_out[q], TURNS * 16 + 16)
                sp.wait_ge(idx_in[q], (TURNS + 1) * n_idx)
            if layer == 2:
                sp.wait_ge(dist_in, (2 * TURNS + 1) * 16)

        @block.gpsimd
        def _(pool):
            with pool.Fori(0, TURNS) as i:
                for q in range(2):
                    pool.wait_ge(idx_in[q], (i + 1) * n_idx)
                    if layer == 0:
                        pool.wait_ge(e_used[q], i + 1)
                        pool.sem_inc(waited, 1)
                        for j in range(JC):
                            pool.indirect_dma_start(E[q][:, j, :], None, k.tab0d,
                                                    bass.IndirectOffsetOnAxis(ap=didx[q][:, j:j + 1], axis=0)).then_inc(dstrow_in[q], 16)
                    pool.wait_ge(rows_out[q], i * 16 + 16)
                    pool.sem_inc(waited, 1)
                    for j in range(JC):
                        pool.indirect_dma_start(R[q][:, j, 0:GC], None, table,
                                                bass.IndirectOffsetOnAxis(ap=sidx[q][:, j:j + 1], axis=0)).then_inc(rows_in[q], 16)

        @block.vector
        def _(v):
            ch = Chain(v, dve_step)
            ch.link(v.memset(last[:, 0:SUM], 0.0))
            if SOFT:
                ch.link(v.memset(last[:, 132:136], -BIG))
            turn = 2 * (JC + {0: 19, 2: 2 + 3 * JC // 4, 3: 19}[layer])
            with v.Fori(0, TURNS) as i:
                ch.loop(i, turn)
                for q in range(2):
                    at = i * (2 * JC) + q * JC
                    c1 = i * 2 + q + 1
                    rq = R[q]
                    ch.link(v.tensor_copy(kb[q][:, :], k.keep[:, bass.ds(at, JC + 1)]))
                    if SOFT:
                        ch.link(v.tensor_scalar(ng[:, :], kb[q][:, :], -1.0, BIG, ALU.add, ALU.mult))
                    v.wait_ge(rows_in[q], (i + 1) * (16 * JC))
                    if layer == 0:
                        v.wait_ge(dstrow_in[q], (i + 1) * (16 * JC))
                        ch.link(v.tensor_tensor(E[q][:, :, :], E[q][:, :, :], rq[:, :, 0:D], ALU.add))
                        ch.link(v.scalar_tensor_tensor(out=E[q][:, :, :], in0=E[q][:, :, :], scalar=0.2, in1=E[q][:, :, :], op0=ALU.mult, op1=ALU.max))
                        ch.link(v.tensor_tensor(E[q][:, :, :], E[q][:, :, :], bc_mid(k.attn[:, :], JC), ALU.mult))
                        v.tensor_reduce(out=sc[:, :, :].rearrange("p h j -> p j h"), in_=E[q][:, :, :].rearrange("p j (h c) -> p j h c", h=HEADS),
                                        op=ALU.add, axis=AX.X).then_inc(e_used[q], 1)
                        v.wait_ge(e_used[q], i + 2)
                        top = sc
                    if layer == 3:
                        ch.link(v.tensor_tensor(sc[:, :, :], rq[:, :, 128:132].rearrange("p j h -> p h j"), k.AR[:, :, bass.ds(at, JC)], ALU.add))
                        ch.link(v.scalar_tensor_tensor(out=sc[:, :, :], in0=sc[:, :, :], scalar=0.2, in1=sc[:, :, :], op0=ALU.mult, op1=ALU.max))
                        v.wait_ge(efp_ready[q], i + 2)
                        v.tensor_tensor(sc[:, :, :], sc[:, :, :], efp[q][:, 0:JC * HEADS].rearrange("p (j h) -> p h j", h=HEADS), ALU.add).then_inc(efp_used[q], 1)
                        v.wait_ge(efp_used[q], i + 2)
                        ch.link(v.tensor_scalar(floor[:, :, :], sc[:, :, :], -1e9, None, ALU.max))
                        top = floor
                    if SOFT:
                        for h in range(HEADS):
                            ch.step(v.tensor_tensor_scan(out=run[:, h, :], data0=ng[:, 0:JC], data1=top[:, h, :],
                                                         initial=last[:, 132 + h:133 + h], op0=ALU.add, op1=ALU.max))
                        v.wait_ge(dve_step, ch.base + ch.n)
                        for h in range(HEADS):
                            ch.step(v.tensor_tensor_scan(out=M[:, h, ::-1], data0=ng[:, JC:0:-1], data1=run[:, h, ::-1],
                                                         initial=-BIG, op0=ALU.add, op1=ALU.max))
                        v.wait_ge(dve_step, ch.base + ch.n)
                        ch.step(v.tensor_tensor(df[q][:, :, 0:JC], sc[:, :, :], M[:, :, :], ALU.subtract))
                        ch.link(v.tensor_tensor(df[q][:, :, JC:JC + 1], last[:, 132:136].unsqueeze(2), M[:, :, 0:1], ALU.subtract))
                        v.tensor_scalar(df[q][:, :, JC:JC + 1], df[q][:, :, JC:JC + 1], 0.0, None, ALU.min).then_inc(exp_arg, 1)
                        ch.step(v.tensor_copy(rq[:, :, 132:136].rearrange("p j h -> p h j"), M[:, :, :]))
                        v.wait_ge(exp_done, c1 * 2)
                        ch.step(v.tensor_tensor(rq[:, :, 0:D].rearrange("p j (h c) -> p j h c", h=HEADS), rq[:, :, 0:D].rearrange("p j (h c) -> p j h c", h=HEADS),
                                                bc_last(rq[:, :, 128:132], HDIM), ALU.mult))
                        ch.step(v.tensor_tensor(carry[:, 0:D].rearrange("p (h c) -> p h c", h=HEADS), last[:, 0:D].rearrange("p (h c) -> p h c", h=HEADS),
                                                bc_last(rc[:, :], HDIM), ALU.mult))
                        ch.link(v.tensor_tensor(carry[:, D:D + HEADS], last[:, D:D + HEADS], rc[:, :], ALU.mult))
                        before = carry[:, 0:SUM]
                    else:
                        before = last[:, 0:SUM]
                    if layer == 2:
                        ch.link(v.tensor_copy(cb[q][:, :], k.cut[:, bass.ds(at, JC)]))
                        for b in range(NB):
                            n0 = i * (2 * NB) + (q * NB + b + 1 + NB)
                            v.wait_ge(w_ready, n0)
                            for j in range(4):
                                s = 4 * b + j
                                ins = v.scalar_tensor_tensor(out=rq[:, s, :], in0=wps_at(wps, q * NB + b, j),
                                                             scalar=cb[q][:, s:s + 1], in1=rq[:, s, :], op0=ALU.mult, op1=ALU.mult)
                                if j < 3:
                                    ch.step(ins)
                                else:
                                    ins.then_inc(w_used, 1)
                        v.wait_ge(w_used, i * (2 * NB) + (q + 2) * NB)
                    for j in range(JC):
                        prev = before if j == 0 else rq[:, j - 1, 0:SUM]
                        ch.link(v.scalar_tensor_tensor(out=rq[:, j, 0:SUM], in0=prev, scalar=kb[q][:, j:j + 1], in1=rq[:, j, 0:SUM],
                                                       op0=ALU.mult, op1=ALU.add))
                    v.tensor_copy(last[:, 0:W], rq[:, JC - 1, 0:W]).then_inc(summed, 1)
                    v.wait_ge(summed, c1)
            ch.end(TURNS)

        @block.scalar
        def _(act):
            if SOFT:
                with act.Fori(0, TURNS) as i:
                    for q in range(2):
                        act.wait_ge(exp_arg, i * 2 + q + 1)
                        act.activation(R[q][:, :, 128:132].rearrange("p j h -> p h j"), df[q][:, :, 0:JC], ACT.Exp).then_inc(exp_done, 1)
                        act.activation(rc[:, :].unsqueeze(2), df[q][:, :, JC:JC + 1], ACT.Exp).then_inc(exp_done, 1)
            if layer == 2:
                with act.Fori(0, TURNS) as i:
                    for q in range(2):
                        n = i * 2 + q
                        act.wait_ge(dist_in, n * 16 + 16)
                        act.wait_ge(z_ready, n * NB + NB)
                        act.activation(rbf[:, :], dist[:, :], ACT.Square, bias=k.rbf_bias[0:51, 0:1], scale=k.rbf_scale[0:51, 0:1]).then_inc(dist_used, 1)
                        act.wait_ge(dist_used, n + 1)
                        act.activation(rbf[:, :], rbf[:, :], ACT.Exp, scale=-50.0).then_inc(rbf_ready, 1)
                        act.wait_ge(w_ready, n * NB + NB)
                        for b in range(NB):
                            act.wait_ge(z_ready, n * NB + b + 1 + NB)
                            act.activation(u[:, b * 512:(b + 1) * 512], wps_at(zps, q * NB + b, None), ACT.Silu).then_inc(u_ready, 1)

        @block.tensor
        def _(pe):
            if layer == 3:
                with pe.Fori(0, TURNS) as i:
                    for q in range(2):
                        pe.wait_ge(attr_in[q], i * 16 + 16)
                        pe.wait_ge(efp_used[q], i + 1)
                        for j in range(JC):
                            last_mm = pe.matmul(efp[q][:, j * HEADS:(j + 1) * HEADS], eft[q][:, j * P:(j + 1) * P], k.wet[:, :], start=True, stop=True)
                        last_mm.then_inc(efp_ready[q], 1)
            if layer == 2:
                def z_block(n, q, b):
                    pe.matmul(wps_at(zps, q * NB + b, None), k.fw1[:, :], rbf[:, b * 512:(b + 1) * 512], start=True, stop=True).then_inc(z_ready, 1)

                with pe.Fori(0, TURNS) as i:
                    for q in range(2):
                        n = i * 2 + q
                        pe.wait_ge(rbf_ready, n + 1)
                        pe.wait_ge(u_ready, n * NB + NB)
                        z_block(n, q, 0)
                        z_block(n, q, 1)
                        z_block(n, q, 2)
                        for b in range(NB):
                            if b + 3 < NB:
                                if b >= 1:
                                    pe.wait_ge(u_ready, n * NB + b + NB)
                                z_block(n, q, b + 3)
                            pe.wait_ge(u_ready, n * NB + b + 1 + NB)
                            if q * NB + b >= 4:
                                pe.wait_ge(w_used, n * NB + b - 3 + NB)
                            else:
                                pe.wait_ge(w_used, i * (2 * NB) + NB)
                            bank = wps_at(wps, q * NB + b, None)
                            pe.matmul(bank, k.ones[0:1, :], k.fb2[0:1, :], start=True, stop=False)
                            for j in range(4):
                                mm = pe.matmul(wps_at(wps, q * NB + b, j), u[:, (4 * b + j) * P:(4 * b + j + 1) * P], k.fw2[:, :], start=False, stop=(j == 3))
                            mm.then_inc(w_ready, 1)


def scatter_phase(nc, k, a):
    S, NT, TURNS, NP = k.S, k.NT, k.TURNS, P * k.NT
    NB = JC // 4
    with Phase(nc, "e1") as ph:
        didx, scol_i = ([ph.sb(f"{n}{q}", [P, JC], I32) for q in range(2)] for n in ("didx", "scol_i"))
        H = [ph.sb(f"h{q}", [P, JC, D]) for q in range(2)]
        attr = [ph.sb(f"attr{q}", [65, JC * P]) for q in range(2)]
        srow_i = ph.sb("srow_i", [1, JC * P], I32)
        srow = ph.sb("srow", [1, JC * P])
        scol = ph.sb("scol", [P, JC])
        same = [ph.sb(f"same{z}", [P, 4, P]) for z in range(2)]
        dup = ph.sb("dup", [P, 4, P])
        first = ph.sb("first", [P, JC])
        sums = [ph.sb(f"sums{q}", [P, JC, D]) for q in range(2)]
        to_f = ph.sb("to_f", [P, JC])
        to = [ph.sb(f"to{q}", [P, JC], I32) for q in range(2)]
        zn = max(z for z in range(1, JC + 1) if (NT + 1) % z == 0)
        zero = ph.sb("zero", [P, zn * D])
        bps = [ph.ps(f"bps{z}", [P, 512]) for z in range(2)]
        vps = [ph.ps(f"vps{z}", [P, 512]) for z in range(2)]
        sps = [ph.ps(f"sps{z}", [P, 512]) for z in range(2)]

        dve_step = ph.sem("dve_step")
        zero_ready = ph.sem("zero_ready")
        didx_in, rows_in = ([ph.sem(f"{n}{q}") for q in range(2)] for n in ("didx_in", "rows_in"))
        scol_in, attr_in = ([ph.sem(f"{n}{q}") for q in range(2)] for n in ("scol_in", "attr_in"))
        srow_in, srow_ready = ph.sem("srow_in"), ph.sem("srow_ready", credit=1)
        scol_ready = ph.sem("scol_ready", credit=1)
        to_ready = ph.sem("to_ready")
        scattered = [ph.sem(f"scattered{t}") for t in range(SUMS)]
        landed = ph.sem("landed", credit=2)
        b_ready, v_ready, same_ready, msg_ready, sum_ready, sum_out = (
            ph.sem(n, credit=NB) for n in ("b_ready", "v_ready", "same_ready", "msg_ready", "sum_ready", "sum_out"))
        waited = ph.sem("waited")
        block = ph.block()

        @block.sync
        def _(sp):
            ph.give_credits(sp)
            sp.dma_start(srow_i[:, :], a["src_T"][0:1, 0:JC * P]).then_inc(srow_in, 16)
            for q in range(2):
                sp.dma_start(didx[q][:, :], a["dst_pad"][:, q * JC:(q + 1) * JC]).then_inc(didx_in[q], 16)
            with sp.Fori(0, TURNS) as i:
                for q in range(2):
                    sp.wait_ge(msg_ready, i * (2 * NB) + (NB if q else 1))
                    sp.dma_start(attr[q][0:64, :], a["edge_attr_64_T"][:, bass.ds((i * 2 + q) * (JC * P), JC * P)]).then_inc(attr_in[q], 16)
                    sp.wait_ge(scol_ready, i * 2 + (q if q else 1))
                    sp.dma_start(scol_i[q][:, :], a["src"][:, bass.ds(i * (2 * JC) + q * JC, JC)]).then_inc(scol_in[q], 16)
                for q in range(2):
                    sp.wait_ge(srow_ready, i * 2 + q + 2)
                    sp.dma_start(srow_i[:, :], a["src_T"][0:1, bass.ds((i * 2 + q + 1) * (JC * P), JC * P)]).then_inc(srow_in, 16)
                    sp.wait_ge(rows_in[q], (i + 1) * (16 * JC))
                    sp.dma_start(didx[q][:, :], a["dst_pad"][:, bass.ds((i + 1) * (2 * JC) + q * JC, JC)]).then_inc(didx_in[q], 16)
            sp.wait_ge(srow_in, (2 * TURNS + 1) * 16)
            for q in range(2):
                sp.wait_ge(didx_in[q], (TURNS + 1) * 16)

        @block.gpsimd
        def _(pool):
            def gather(q):
                for j in range(JC):
                    pool.indirect_dma_start(H[q][:, j, :], None, k.tab1,
                                            bass.IndirectOffsetOnAxis(ap=didx[q][:, j:j + 1], axis=0)).then_inc(rows_in[q], 16)

            pool.wait_ge(didx_in[0], 16)
            gather(0)
            pool.wait_ge(zero_ready, 1)
            for t in range(SUMS):
                pool.dma_start(k.by_src[t].rearrange("(p r t) c -> p r (t c)", p=P, t=zn), bc_mid(zero[:, :], (NT + 1) // zn)).then_inc(scattered[t], 16)
            with pool.Fori(0, TURNS) as i:
                for q in range(2):
                    if q == 0:
                        pool.wait_ge(didx_in[1], (i + 1) * 16)
                        pool.wait_ge(sum_ready, i * (2 * NB) + NB)
                    else:
                        pool.wait_ge(didx_in[0], (i + 2) * 16)
                        pool.wait_ge(sum_ready, i * (2 * NB) + 2 * NB)
                    pool.sem_inc(waited, 1)
                    gather(1 - q)
                    pool.wait_ge(to_ready, i * 2 + q + 1)
                    for j in range(JC):
                        if j % 4 == 0:
                            pool.wait_ge(sum_out, i * (2 * NB) + (q * NB + j // 4 + 1 + NB))
                        pool.wait_ge(scattered[j % SUMS], i * (2 * JC // SUMS * 16) + ((q * JC + j) // SUMS + 1) * 16)
                        pool.sem_inc(landed if j == SUMS - 1 else waited, 1)
                        pool.indirect_dma_start(k.by_src[j % SUMS], bass.IndirectOffsetOnAxis(ap=to[q][:, j:j + 1], axis=0),
                                                sums[q][:, j, :], None, compute_op=ALU.add).then_inc(scattered[j % SUMS], 16)
            for t in range(SUMS):
                pool.wait_ge(scattered[t], TURNS * (2 * JC // SUMS * 16) + 16)
            pool.wait_ge(rows_in[0], (TURNS + 1) * (16 * JC))

        @block.vector
        def _(v):
            ch = Chain(v, dve_step)
            ch.step(v.memset(attr[0][64:65, :], 1.0))
            ch.link(v.memset(attr[1][64:65, :], 1.0))
            v.memset(zero[:, :], 0.0).then_inc(zero_ready, 1)
            with v.Fori(0, TURNS) as i:
                ch.loop(i, 2 * (2 * NB + 3))
                for q in range(2):
                    v.wait_ge(scol_in[q], i * 16 + 16)
                    v.tensor_copy(scol[:, :], scol_i[q][:, :]).then_inc(scol_ready, 1)
                    v.wait_ge(scol_ready, i * 2 + q + 2)
                    v.wait_ge(rows_in[q], (i + 1) * (16 * JC))
                    for b in range(NB):
                        n = i * (2 * NB) + (q * NB + b + 1 + NB)
                        z = (q * NB + b) % 2
                        hb = H[q][:, 4 * b:4 * b + 4, :]
                        v.wait_ge(v_ready, n)
                        v.tensor_tensor(hb, hb, vps[z][:, :].rearrange("p (j c) -> p j c", c=D), ALU.add).then_inc(msg_ready, 1)
                        if q * NB + b >= 2:
                            v.wait_ge(sum_ready, n - 2)
                        else:
                            v.wait_ge(sum_ready, i * (2 * NB) + NB)
                        v.wait_ge(b_ready, n)
                        v.tensor_tensor(same[z][:, :, :], bps[z][:, :].rearrange("p (j f) -> p j f", f=P),
                                        bc_last(scol[:, 4 * b:4 * b + 4], P), ALU.is_equal).then_inc(same_ready, 1)
                        v.wait_ge(same_ready, n)
                        ch.link(v.tensor_tensor(dup[:, :, :], same[z][:, :, :], bc_mid(k.before[:, :], 4), ALU.mult))
                        ch.link(v.tensor_reduce(out=first[:, 4 * b:4 * b + 4], in_=dup[:, :, :], op=ALU.add, axis=AX.X))
                    ch.link(v.tensor_scalar(first[:, :], first[:, :], 0.5, None, ALU.is_lt))
                    ch.link(v.scalar_tensor_tensor(out=to_f[:, :], in0=scol[:, :], scalar=k.trash[:, 0:1], in1=first[:, :],
                                                   op0=ALU.subtract, op1=ALU.mult))
                    ch.link(v.tensor_scalar(to_f[:, :], to_f[:, :], k.trash[:, 0:1], None, ALU.add))
                    v.wait_ge(landed, i * 2 + q + 2)
                    v.tensor_copy(to[q][:, :], to_f[:, :]).then_inc(to_ready, 1)
            ch.end(TURNS)

        @block.scalar
        def _(act):
            with act.Fori(0, TURNS) as i:
                for q in range(2):
                    act.wait_ge(srow_in, (i * 2 + q + 1) * 16)
                    act.wait_ge(b_ready, i * (2 * NB) + (q + 1) * NB)
                    act.activation(srow[:, :], srow_i[:, :], ACT.Copy).then_inc(srow_ready, 1)
                    act.wait_ge(landed, i * 2 + q + 2)
                    for b in range(NB):
                        n = i * (2 * NB) + (q * NB + b + 1 + NB)
                        act.wait_ge(sum_ready, n)
                        act.activation(sums[q][:, 4 * b:4 * b + 4, :], sps[(q * NB + b) % 2][:, :].rearrange("p (j c) -> p j c", c=D), ACT.Copy).then_inc(sum_out, 1)

        @block.tensor
        def _(pe):
            pe.wait_ge(dve_step, 2)
            with pe.Fori(0, TURNS) as i:
                for q in range(2):
                    pe.wait_ge(srow_ready, i * 2 + q + 2)
                    pe.wait_ge(attr_in[q], i * 16 + 16)

                    def fill(b):
                        z = (q * NB + b) % 2
                        c = slice(b * 512, (b + 1) * 512)
                        lo = (q * NB + b - 1 + NB) if q * NB + b >= 2 else NB
                        pe.wait_ge(same_ready, i * (2 * NB) + lo)
                        pe.matmul(bps[z][:, :], k.ones[0:1, :], srow[:, c], start=True, stop=True).then_inc(b_ready, 1)
                        pe.wait_ge(msg_ready, i * (2 * NB) + lo)
                        for j in range(4):
                            mm = pe.matmul(vps[z][:, j * P:(j + 1) * P], attr[q][0:65, (4 * b + j) * P:(4 * b + j + 1) * P], k.we[0:65, :], start=True, stop=True)
                        mm.then_inc(v_ready, 1)

                    fill(0)
                    for b in range(NB):
                        if b + 1 < NB:
                            fill(b + 1)
                        n = i * (2 * NB) + (q * NB + b + 1 + NB)
                        z = (q * NB + b) % 2
                        pe.wait_ge(msg_ready, n)
                        pe.wait_ge(same_ready, n)
                        lo = (q * NB + b - 1 + NB) if q * NB + b >= 2 else NB
                        pe.wait_ge(sum_out, i * (2 * NB) + lo)
                        for j in range(4):
                            mm = pe.matmul(sps[z][:, j * D:(j + 1) * D], same[z][:, j, :], H[q][:, 4 * b + j, :], start=True, stop=True)
                        mm.then_inc(sum_ready, 1)


def wps_at(ps, n, j):
    lo = n % 4 * 512
    return ps[:, lo:lo + 512] if j is None else ps[:, lo + j * D:lo + (j + 1) * D]


def seam_phase(nc, k, a, layer):
    SOFT = layer in (0, 3)
    W = {0: 136, 2: 128, 3: 136}[layer]
    rows = {0: k.rows0, 2: k.rows2, 3: k.rows0}[layer]
    with Phase(nc, f"s{layer}") as ph:
        row = ph.sb("row", [P, W])
        ps = ph.ps("ps", [P, 512])
        last = k.last
        row_in, row_out, fixed = ph.sem("row_in"), ph.sem("row_out"), ph.sem("fixed")
        dve_step, pe_step, act_step = ph.sem("dve_step"), ph.sem("pe_step"), ph.sem("act_step")
        if SOFT:
            dg = ph.sb("dg", [P, HEADS, P])
            am = ph.sb("am", [P, HEADS, P])
            ngm = ph.sb("ngm", [P, P])
            cm = ph.sb("cm", [P, HEADS])
            wt = ph.sb("wt", [P, HEADS, P])
            ex = ph.sb("ex", [P, 2, HEADS])
            mm = ph.sb("mm", [P, HEADS])
            ps2 = ph.ps("ps2", [P, 512])
        waited = ph.sem("waited")
        block = ph.block()

        @block.gpsimd
        def _(pool):
            pool.indirect_dma_start(row[:, :], None, rows, bass.IndirectOffsetOnAxis(ap=k.seam_row[:, 0:1], axis=0)).then_inc(row_in, 16)
            pool.wait_ge(fixed, 1)
            pool.indirect_dma_start(rows, bass.IndirectOffsetOnAxis(ap=k.seam_row[:, 0:1], axis=0), row[:, :], None).then_inc(row_out, 16)
            pool.wait_ge(row_out, 16)

        if not SOFT:
            @block.tensor
            def _(pe):
                pe.matmul(ps[:, 0:W], k.seam[:, :], last[:, 0:W], start=True, stop=True).then_inc(pe_step, 1)

            @block.vector
            def _(v):
                v.wait_ge(pe_step, 1)
                v.wait_ge(row_in, 16)
                v.tensor_tensor(row[:, :], row[:, :], ps[:, 0:W], ALU.add).then_inc(fixed, 1)
            return

        @block.tensor
        def _(pe):
            pe.wait_ge(dve_step, 4)
            pe.matmul(ps[:, :], k.ones[:, :], dg[:, :, :].rearrange("p h q -> p (h q)"), start=True, stop=True).then_inc(pe_step, 1)
            pe.wait_ge(dve_step, 10)
            for h in range(HEADS):
                t = pe.transpose(ps2[:, h * P:(h + 1) * P], am[:, h, :], k.ident[:, :])
            t.then_inc(pe_step, 1)
            pe.wait_ge(dve_step, 11)
            for h in range(HEADS):
                pe.matmul(ps[:, h * HDIM:(h + 1) * HDIM], wt[:, h, :], last[:, h * HDIM:(h + 1) * HDIM], start=True, stop=True)
                t = pe.matmul(ps[:, D + h:D + h + 1], wt[:, h, :], last[:, D + h:D + h + 1], start=True, stop=True)
            t.then_inc(pe_step, 1)

        @block.scalar
        def _(act):
            act.wait_ge(dve_step, 9)
            act.activation(am[:, :, :], am[:, :, :], ACT.Exp).then_inc(act_step, 1)
            act.wait_ge(dve_step, 14)
            act.activation(ex[:, :, :], ex[:, :, :], ACT.Exp).then_inc(act_step, 1)

        @block.vector
        def _(v):
            ch = Chain(v, dve_step)
            for h in range(HEADS):
                ch.step(v.tensor_scalar(dg[:, h, :], k.ident[:, :], last[:, 132 + h:133 + h], None, ALU.mult))
            ch.link(v.tensor_scalar(ngm[:, :], k.seamT[:, :], -1.0, BIG, ALU.add, ALU.mult))
            v.wait_ge(pe_step, 1)
            ch.link(v.tensor_tensor(am[:, :, :], ps[:, :].rearrange("p (h q) -> p h q", h=HEADS), bc_mid(ngm[:, :], HEADS), ALU.add))
            ch.link(v.tensor_reduce(out=cm[:, :], in_=am[:, :, :], op=ALU.max, axis=AX.X))
            ch.link(v.tensor_tensor(am[:, :, :], am[:, :, :], bc_last(cm[:, :], P), ALU.subtract))
            ch.link(v.tensor_scalar(am[:, :, :], am[:, :, :], 0.0, None, ALU.min))
            v.wait_ge(act_step, 1)
            ch.link(v.tensor_tensor(am[:, :, :], am[:, :, :], bc_mid(k.seamT[:, :], HEADS), ALU.mult))
            v.wait_ge(pe_step, 2)
            ch.link(v.tensor_copy(wt[:, :, :], ps2[:, :].rearrange("p (h q) -> p h q", h=HEADS)))
            v.wait_ge(row_in, 16)
            ch.link(v.tensor_tensor(mm[:, :], row[:, 132:136], cm[:, :], ALU.max))
            ch.step(v.tensor_tensor(ex[:, 0, :], row[:, 132:136], mm[:, :], ALU.subtract))
            ch.link(v.tensor_tensor(ex[:, 1, :], cm[:, :], mm[:, :], ALU.subtract))
            v.wait_ge(act_step, 2)
            v.wait_ge(pe_step, 3)
            ch.step(v.tensor_copy(row[:, 132:136], mm[:, :]))
            ch.step(v.tensor_tensor(row[:, 0:D].rearrange("p (h c) -> p h c", h=HEADS), row[:, 0:D].rearrange("p (h c) -> p h c", h=HEADS),
                                    bc_last(ex[:, 0, :], HDIM), ALU.mult))
            ch.step(v.tensor_tensor(row[:, D:132], row[:, D:132], ex[:, 0, :], ALU.mult))
            ch.step(v.tensor_tensor(dg[:, 0, :].rearrange("p (h c) -> p h c", h=HEADS), ps[:, 0:D].rearrange("p (h c) -> p h c", h=HEADS),
                                    bc_last(ex[:, 1, :], HDIM), ALU.mult))
            ch.link(v.tensor_tensor(dg[:, 1, 0:HEADS], ps[:, D:132], ex[:, 1, :], ALU.mult))
            ch.link(v.tensor_tensor(row[:, 0:D], row[:, 0:D], dg[:, 0, :], ALU.add))
            v.tensor_tensor(row[:, D:132], row[:, D:132], dg[:, 1, 0:HEADS], ALU.add).then_inc(fixed, 1)


def spread_phase(nc, k, a):
    S, NT, NG = k.S, k.NT, k.NG
    with Phase(nc, "spread") as ph:
        zero = ph.sb("zero", [P, S * HEADS])
        z = ph.sb("z", [P, S, HEADS])
        arn = ph.sb("arn", [P, NT, HEADS])
        arg = ph.sb("arg", [P, GT, HEADS])
        sidx = ph.sb("sidx", [P, GT], I32)
        z_cleared, zero_ready, arn_in, sidx_ready = ph.sem("z_cleared"), ph.sem("zero_ready"), ph.sem("arn_in"), ph.sem("sidx_ready")
        scattered, z_in, first_in, dve_step = ph.sem("scattered"), ph.sem("z_in"), ph.sem("first_in"), ph.sem("dve_step")
        waited = ph.sem("waited")
        block = ph.block()

        @block.sync
        def _(sp):
            ph.give_credits(sp)
            sp.dma_start(arn[:, :, :], k.ar_tab.rearrange("(p t) c -> p t c", t=NT)).then_inc(arn_in, 16)
            sp.wait_ge(zero_ready, 1)
            sp.dma_start(k.starts[0:k.EP, :].rearrange("(p s) c -> p (s c)", s=S), zero[:, :]).then_inc(z_cleared, 16)
            sp.wait_ge(scattered, NG * GT * 16)
            sp.dma_start(z[:, :, :], k.starts[0:k.EP, :].rearrange("(p s) c -> p s c", s=S)).then_inc(z_in, 16)

        @block.gpsimd
        def _(pool):
            pool.wait_ge(arn_in, 16)
            pool.wait_ge(z_cleared, 16)
            with pool.Fori(0, NG) as g:
                pool.tensor_copy(arg[:, :, :], arn[:, bass.ds(g * GT, GT), :]).then_inc(sidx_ready, 1)
                pool.tensor_copy(sidx[:, :], k.start_row[:, bass.ds(g * GT, GT)]).then_inc(sidx_ready, 1)
                pool.wait_ge(sidx_ready, g * 2 + 2)
                pool.sem_inc(waited, 1)
                for t in range(GT):
                    pool.indirect_dma_start(k.starts, bass.IndirectOffsetOnAxis(ap=sidx[:, t:t + 1], axis=0), arg[:, t, :], None).then_inc(scattered, 16)
                pool.wait_ge(scattered, (g + 1) * (16 * GT))
                pool.sem_inc(waited, 1)
            pool.wait_ge(z_in, 16)
            pool.indirect_dma_start(z[:, 0, :], None, k.ar_tab, bass.IndirectOffsetOnAxis(ap=k.first_dst[:, 0:1], axis=0)).then_inc(first_in, 16)

        @block.vector
        def _(v):
            v.memset(zero[:, :], 0.0).then_inc(zero_ready, 1)
            v.wait_ge(z_in, 16)
            v.wait_ge(first_in, 16)
            for h in range(HEADS):
                v.tensor_tensor_scan(out=k.AR[:, h, :], data0=k.keep[:, 0:S], data1=z[:, :, h], initial=0.0,
                                     op0=ALU.mult, op1=ALU.add).then_inc(dve_step, 1)


def gnn_program(nc, a):
    k = Ctx()
    k.EP = a["dst"].shape[0] * a["dst"].shape[1]
    k.S = a["dst"].shape[1]
    k.NT = a["x"].shape[0] // P
    k.NG = k.NT // GT
    k.TURNS = k.S // (2 * JC)
    NP = P * k.NT

    def dram(name, shape, dt=FP):
        return nc.dram_tensor(name, shape, dt, kind="Internal").ap()

    k.tab0s, k.tab0d, k.tab1 = (dram(n, (NP, D)) for n in ("tab0s", "tab0d", "tab1"))
    k.tab3, k.ar_tab = dram("tab3", (NP, 132)), dram("ar_tab", (NP, HEADS))
    k.rows0, k.rows2 = dram("rows0", (k.EP + 1, 136)), dram("rows2", (k.EP + 1, D))
    k.by_src = [dram(f"by_src{t}", (NP + P, D)) for t in range(SUMS)]
    k.starts = dram("starts", (k.EP + NP, HEADS))
    k.counts = dram("counts", (1, NP + 1))
    with ExitStack() as st:
        def sb(n, shape, dt=FP):
            return st.enter_context(nc.sbuf_tensor(n, shape, dt))

        k.X = sb("X", [P, k.NT, D])
        k.keep, k.cut = sb("keep", [P, k.S + 1]), sb("cut", [P, k.S])
        k.ident, k.ones, k.seam, k.seamT = (sb(n, [P, P]) for n in ("ident", "ones", "seam", "seamT"))
        k.node, k.deg = sb("node", [P, k.NT]), sb("deg", [P, k.NT])
        k.end_row, k.start_row = sb("end_row", [P, k.NT], I32), sb("start_row", [P, k.NT], I32)
        k.seam_row, k.first_dst = sb("seam_row", [P, 1], I32), sb("first_dst", [P, 1], I32)
        k.sself = sb("sself", [P, k.NT, HEADS])
        k.last = sb("last", [P, 136])
        k.trash, k.before = sb("trash", [P, 1]), sb("before", [P, P])
        k.w0, k.b0, k.attn = sb("w0", [P, 2 * D]), sb("b0", [P, 2 * D]), sb("attn", [P, D])
        k.w1, k.b1, k.we = sb("w1", [P, D]), sb("b1", [P, D]), sb("we", [65, D])
        k.fw1, k.fw2, k.fb2 = sb("fw1", [51, D]), sb("fw2", [P, D]), sb("fb2", [1, 4 * D])
        k.pw, k.pb, k.mw1, k.mw2, k.mb2 = (sb(n, [P, D]) for n in ("pw", "pb", "mw1", "mw2", "mb2"))
        k.mb1, k.rbf_bias, k.rbf_scale = sb("mb1", [P, 1]), sb("rbf_bias", [51, 1]), sb("rbf_scale", [51, 1])
        k.w3, k.wet, k.lns, k.lnb = sb("w3", [P, 136]), sb("wet", [16, HEADS]), sb("lns", [P, D]), sb("lnb", [P, D])

        setup_phase(nc, k, a)
        ends_phase(nc, k, a)
        node_phase(nc, k, a, None, 0)
        for layer in range(3):
            if layer == 1:
                scatter_phase(nc, k, a)
            else:
                edge_phase(nc, k, a, layer)
                seam_phase(nc, k, a, layer)
            node_phase(nc, k, a, layer, layer + 1)
        k.AR = sb("AR", [P, HEADS, k.S])
        spread_phase(nc, k, a)
        edge_phase(nc, k, a, 3)
        seam_phase(nc, k, a, 3)
        node_phase(nc, k, a, 3, None)




def kernel(**inputs):
    import numpy as np
    import concourse.bacc as _bacc
    from concourse import mybir as _mybir
    from concourse.bass_utils import run_bass_kernel_spmd as _run

    x, src, dst = (np.asarray(inputs[n]) for n in ("x", "src", "dst"))
    N, E = x.shape[0], src.shape[0]
    per = P * 2 * JC
    EP = -(-E // per) * per
    S = EP // P
    NP = -(-N // (P * GT)) * P * GT
    pad_e = EP - E

    def padded(v, n, fill=0):
        v = np.asarray(v)
        return np.concatenate([v, np.full((n,) + v.shape[1:], fill, v.dtype)])

    arrays = {"x": padded(x, NP - N)}
    src_p = padded(src, pad_e, NP - 1).reshape(P, S)
    dst_p = padded(dst, pad_e, NP - 1)
    arrays["dst"] = dst_p.reshape(P, S)
    more = np.zeros((P, 2 * JC), src.dtype)
    arrays["src"] = np.concatenate([src_p, more], axis=1)
    arrays["dst_pad"] = np.concatenate([dst_p.reshape(P, S), more], axis=1)
    arrays["dst_last"] = dst_p.reshape(P, S)[:, -1].reshape(1, P)
    arrays["dst_blocks"] = dst_p.reshape(S, P)
    arrays["dst_coarse"] = dst_p[::P].reshape(1, S)
    ew = padded(inputs["edge_weight"], pad_e).reshape(P, S)
    arrays["edge_weight"] = ew
    arrays["dist_T"] = np.concatenate([ew.T.reshape(1, EP), np.zeros((1, P * JC), ew.dtype)], axis=1)
    arrays["src_T"] = np.concatenate([src_p.T.reshape(1, EP), np.zeros((1, P * JC), src.dtype)], axis=1)
    e64 = padded(inputs["edge_attr_64"], pad_e).reshape(P, S, 64)
    arrays["edge_attr_64_T"] = e64.transpose(2, 1, 0).reshape(64, EP)
    ea = padded(inputs["edge_attr_16"], pad_e).reshape(P, S, 16)
    arrays["edge_attr_16_T"] = ea.transpose(2, 1, 0).reshape(16, EP)
    for n in sorted(inputs):
        if n.startswith("L"):
            v = np.asarray(inputs[n])
            arrays[n] = v.reshape(1, -1) if v.ndim == 1 else v
    arrays["L3_gnn_W_T"] = np.asarray(inputs["L3_gnn_W"]).T
    arrays["L3_gnn_W_e_T"] = np.asarray(inputs["L3_gnn_W_e"]).T

    nc = _bacc.Bacc("TRN2", target_bir_lowering=False, num_devices=1)
    feed, a = {}, {}
    for n, v in arrays.items():
        v = np.ascontiguousarray(v)
        feed[f"in_{n}"] = v
        a[n] = nc.dram_tensor(f"in_{n}", v.shape, _mybir.dt.from_np(v.dtype), kind="ExternalInput").ap()
    a["out"] = nc.dram_tensor("out_0", (NP, D), _mybir.dt.float32, kind="ExternalOutput").ap()
    gnn_program(nc, a)
    r = _run(nc, [feed], core_ids=[0])
    return r.results[0]["out_0"][:N]
```

```python
import concourse.bass as bass
from concourse import mybir
from contextlib import ExitStack

P = 128
HEADS, HDIM = 4, 32
D = HEADS * HDIM
JC = 28
BUFS = 4
GT = 7
SUMS = 4
BIG = 1.0e38
EPS = 1e-5
PI = 3.141592653589793
FP = mybir.dt.float32
BF = mybir.dt.bfloat16
I32 = mybir.dt.int32
ALU = mybir.AluOpType
ACT = mybir.ActivationFunctionType
AX = mybir.AxisListType


class Chain:

    def __init__(self, eng, sem):
        self.eng, self.sem, self.base, self.n = eng, sem, 0, 0

    def loop(self, i, per_turn):
        self.start = self.base + self.n
        self.base = i * per_turn + self.start
        self.n = 0
        self.per_turn = per_turn

    def end(self, turns):
        assert self.n == self.per_turn, (self.n, self.per_turn)
        self.base, self.n = self.start + turns * self.per_turn, 0

    def step(self, ins):
        ins.then_inc(self.sem, 1)
        self.n += 1

    def link(self, ins):
        self.step(ins)
        self.eng.wait_ge(self.sem, self.base + self.n)


class Ctx:
    pass


def bc_mid(ap, n):
    return ap.unsqueeze(1).to_broadcast([ap.shape[0], n, ap.shape[1]])


def bc_last(ap, n):
    return ap.unsqueeze(len(ap.shape)).to_broadcast(list(ap.shape) + [n])


class Phase:

    def __init__(self, nc, name):
        self.nc, self.name, self.stack, self.sems, self.credits = nc, name, ExitStack(), [], []

    def __enter__(self):
        self.stack.__enter__()
        return self

    def __exit__(self, *a):
        self.stack.__exit__(*a)
        if a[0] is None:
            self.nc.clear_and_free_semaphores(self.sems)
            self.nc.all_engine_barrier()

    def sb(self, n, shape, dt=FP):
        return self.stack.enter_context(self.nc.sbuf_tensor(f"{self.name}_{n}", shape, dt))

    def ps(self, n, shape):
        return self.stack.enter_context(self.nc.psum_tensor(f"{self.name}_{n}", shape, FP))

    def sem(self, n, credit=0):
        self.sems.append(self.nc.alloc_semaphore(f"{self.name}_{n}"))
        if credit:
            self.credits.append((self.sems[-1], credit))
        return self.sems[-1]

    def give_credits(self, sp):
        for sem, credit in self.credits:
            sp.sem_inc(sem, credit)

    def block(self):
        return self.stack.enter_context(self.nc.Block())




def setup_phase(nc, k, a):
    S, NT = k.S, k.NT
    with Phase(nc, "setup") as ph:
        dst_i = ph.sb("dst_i", [P, S], I32)
        dst_f = ph.sb("dst_f", [P, S])
        lastd_i = ph.sb("lastd_i", [P, P], I32)
        lastd_f = ph.sb("lastd_f", [P, P])
        col = ph.sb("col", [P, P])
        part = ph.sb("part", [P, 1])
        eqf = ph.sb("eqf", [P, S])
        cnt = ph.sb("cnt", [P, 1])
        rowf = ph.sb("rowf", [P, 1])
        mlow = ph.sb("mlow", [P, P])
        seam_ps = ph.ps("seam_ps", [P, 512])
        w3_ps = ph.ps("w3_ps", [P, 512])
        zrow = ph.sb("zrow", [1, 192])
        fd_i = ph.sb("fd_i", [P, 1], I32)
        wfull = ph.sb("wfull", [P, D])
        acol = ph.sb("acol", [P, 8])
        dist = ph.sb("dist", [P, S])
        dgt = ph.sb("dgt", [P, S])
        srcT_i = ph.sb("srcT_i", [P, S], I32)
        srcT = ph.sb("srcT", [P, S])
        src_hi, src_lo = ph.sb("src_hi", [P, S], BF), ph.sb("src_lo", [P, S], BF)
        fb, fb_sum = ph.sb("fb", [3, 4 * D]), ph.sb("fb_sum", [3, 4 * D])
        fb_part = ph.sb("fb_part", [3, 4 * D], BF)
        pick = ph.sb("pick", [P, 3])

        dma_in = ph.sem("dma_in")
        acol_zero = ph.sem("acol_zero")
        acol_in = ph.sem("acol_in")
        pool_step = ph.sem("pool_step")
        dve_step = ph.sem("dve_step")
        pe_step = ph.sem("pe_step")
        seamT_ready = ph.sem("seamT_ready")
        cut_arg = ph.sem("cut_arg")
        cut_cos = ph.sem("cut_cos")
        attn_in = ph.sem("attn_in")
        src_split = ph.sem("src_split")
        src_out = ph.sem("src_out")
        rows_zero = ph.sem("rows_zero")
        zero_ready = ph.sem("zero_ready")
        zero_out = ph.sem("zero_out")
        waited = ph.sem("waited")
        block = ph.block()
        loads = [
            (dst_i[:, :], a["dst"]), (lastd_i[:, :], a["dst_last"].to_broadcast([P, P])),
            (k.X[:, :, :], a["x"].rearrange("(p t) c -> p t c", t=NT)),
            (k.w0[:, 0:D], a["L0_gnn_W_src"]), (k.w0[:, D:2 * D], a["L0_gnn_W_dst"]),
            (k.b0[:, 0:D], a["L0_gnn_b_src"].to_broadcast([P, D])),
            (k.b0[:, D:2 * D], a["L0_gnn_b_dst"].to_broadcast([P, D])),
            (k.attn[:, :], a["L0_gnn_attn"].rearrange("h d -> (h d)").unsqueeze(0).to_broadcast([P, D])),
            (k.w1[:, :], a["L1_gnn_W_lin"]), (k.b1[:, :], a["L1_gnn_b_lin"].to_broadcast([P, D])),
            (k.we[0:64, :], a["L1_gnn_W_edge"]), (k.we[64:65, :], a["L1_gnn_b_edge"]),
            (k.fw1[0:50, :], a["L2_gnn_fw1"]), (k.fw1[50:51, :], a["L2_gnn_fb1"]),
            (k.fw2[:, :], a["L2_gnn_fw2"]),
            (k.pw[:, :], a["L2_gnn_pw"]), (k.pb[:, :], a["L2_gnn_pb"].to_broadcast([P, D])),
            (k.mw1[:, :], a["L2_gnn_mw1"]), (k.mb1[:, :], a["L2_gnn_mb1"].rearrange("o c -> c o")),
            (k.mw2[:, :], a["L2_gnn_mw2"]), (k.mb2[:, :], a["L2_gnn_mb2"].to_broadcast([P, D])),
            (k.w3[:, 0:D], a["L3_gnn_W_T"]), (wfull[:, :], a["L3_gnn_W"]),
            (k.wet[:, :], a["L3_gnn_W_e_T"]),
            (k.lns[:, :], a["L3_gnn_ln_scale"].to_broadcast([P, D])),
            (k.lnb[:, :], a["L3_gnn_ln_bias"].to_broadcast([P, D])),
            (dist[:, :], a["edge_weight"]), (srcT_i[:, :], a["src_T"].rearrange("o (p s) -> (o p) s", s=S)),
            (k.coarse_i[:, :], a["dst_coarse"].to_broadcast([P, a["dst_coarse"].shape[1]])),
        ] + [(fb[:, j * D:(j + 1) * D], a["L2_gnn_fb2"].to_broadcast([3, D])) for j in range(4)]

        @block.sync
        def _(sp):
            ph.give_credits(sp)
            with nc.allow_non_contiguous_dma(reason="a bias column"):
                for out, in_ in loads:
                    sp.dma_start(out, in_).then_inc(dma_in, 16)
            sp.wait_ge(acol_zero, 1)
            with nc.allow_non_contiguous_dma(reason="the attention vectors as columns"):
                for h in range(HEADS):
                    sp.dma_start(k.attn_cols[h * HDIM:(h + 1) * HDIM, h:h + 1], a["L0_gnn_attn"][h:h + 1, :].rearrange("o c -> c o")).then_inc(attn_in, 16)
                    for half in range(2):
                        sp.dma_start(acol[h * HDIM:(h + 1) * HDIM, half * 4 + h:half * 4 + h + 1],
                                     a["L3_gnn_a"][h:h + 1, half * HDIM:(half + 1) * HDIM]
                                     .rearrange("o c -> c o")).then_inc(acol_in, 16)
            sp.wait_ge(zero_ready, 1)
            sp.dma_start(k.rows0[k.EP:k.EP + 1, :], zrow[0:1, 0:136]).then_inc(zero_out, 16)
            sp.dma_start(k.rows2[k.EP:k.EP + 1, :], zrow[0:1, 0:128]).then_inc(zero_out, 16)
            sp.wait_ge(zero_out, 32)
            sp.wait_ge(attn_in, 16 * HEADS)
            sp.wait_ge(src_split, 2)
            for n, t in enumerate((src_hi, src_lo)):
                sp.dma_start(k.src_parts[n:n + 1, :].rearrange("o (p s) -> (o p) s", s=S), t[:, :]).then_inc(src_out, 16)
            sp.wait_ge(src_out, 32)

        @block.gpsimd
        def _(pool):
            ch = Chain(pool, pool_step)
            ch.link(pool.memset(k.ident[:, :], 0.0))
            ch.step(pool.affine_select(out=k.ident[:, :], in_=k.ident[:, :], compare_op=ALU.not_equal, fill=1.0,
                                       base=0, pattern=[[-1, P]], channel_multiplier=1))
            ch.step(pool.iota(col[:, :], pattern=[[1, P]], base=0, channel_multiplier=0,
                              allow_small_or_imprecise_dtypes=True))
            ch.step(pool.iota(part[:, :], pattern=[[0, 1]], base=0, channel_multiplier=1,
                              allow_small_or_imprecise_dtypes=True))
            ch.step(pool.iota(rowf[:, :], pattern=[[0, 1]], base=0, channel_multiplier=S,
                              allow_small_or_imprecise_dtypes=True))
            ch.step(pool.iota(k.node[:, :], pattern=[[1, NT]], base=0, channel_multiplier=NT,
                              allow_small_or_imprecise_dtypes=True))

        @block.vector
        def _(v):
            ch = Chain(v, dve_step)
            v.memset(k.zero_rows[:, :], 0.0).then_inc(rows_zero, 1)
            ch.link(v.memset(k.attn_cols[:, :], 0.0))
            v.memset(acol[:, :], 0.0).then_inc(acol_zero, 1)
            ch.step(v.memset(k.ones[:, :], 1.0))
            ch.link(v.memset(zrow[:, :], 0.0))
            v.memset(zrow[:, 132:136], -BIG).then_inc(zero_ready, 1)
            v.wait_ge(dma_in, 16 * len(loads))
            v.wait_ge(pool_step, 6)
            ch.step(v.tensor_scalar(k.attn02[:, :], k.attn[:, :], 0.2, None, ALU.mult))
            ch.link(v.scalar_tensor_tensor(out=dgt[:, :], in0=dist[:, :], scalar=-1.0, in1=dist[:, :], op0=ALU.mult, op1=ALU.max))
            ch.link(v.tensor_scalar(dgt[:, :], dgt[:, :], 10.0, -PI / 10.0, ALU.min, ALU.mult))
            ch.link(v.tensor_scalar(dgt[:, :], dgt[:, :], PI / 2, None, ALU.add))
            v.tensor_scalar(dist[:, :], dist[:, :], 10.0, 0.5, ALU.is_le, ALU.mult).then_inc(cut_arg, 1)
            ch.link(v.tensor_scalar(k.rbf_bias[0:51, :], part[0:51, :], -10.0 / 49.0, None, ALU.mult))
            ch.link(v.tensor_scalar(k.rbf_scale[0:51, :], part[0:51, :], 49.5, None, ALU.is_lt))
            ch.link(v.tensor_tensor(k.rbf_bias[0:51, :], k.rbf_bias[0:51, :], k.rbf_scale[0:51, :], ALU.mult))
            ch.link(v.tensor_copy(dst_f[:, :], dst_i[:, :]))
            ch.step(v.memset(k.keep[:, 0:1], 1.0))
            ch.step(v.memset(k.keep[:, S:S + 1], 0.0))
            ch.link(v.tensor_tensor(k.keep[:, 1:S], dst_f[:, 1:S], dst_f[:, 0:S - 1], ALU.is_equal))
            ch.link(v.tensor_tensor(eqf[:, :], dst_f[:, :], dst_f[:, 0:1].to_broadcast([P, S]), ALU.is_equal))
            ch.link(v.tensor_reduce(out=cnt[:, :], in_=eqf[:, :], op=ALU.add, axis=AX.X))
            ch.link(v.scalar_tensor_tensor(out=cnt[:, :], in0=cnt[:, :], scalar=-1.0, in1=rowf[:, :],
                                           op0=ALU.add, op1=ALU.add))
            ch.link(v.tensor_copy(k.seam_row[:, :], cnt[:, :]))
            ch.link(v.tensor_copy(k.first_dst[:, :], dst_i[:, 0:1]))
            ch.link(v.tensor_copy(lastd_f[:, :], lastd_i[:, :]))
            ch.link(v.tensor_scalar(mlow[:, :], col[:, :], part[:, 0:1], None, ALU.is_lt))
            v.scalar_tensor_tensor(out=k.seamT[:, :], in0=lastd_f[:, :], scalar=dst_f[:, 0:1],
                                   in1=mlow[:, :], op0=ALU.is_equal, op1=ALU.mult).then_inc(seamT_ready, 1)
            v.wait_ge(seamT_ready, 1)
            ch.step(v.tensor_reduce(out=k.cont[:, :], in_=k.seamT[:, :], op=ALU.max, axis=AX.X))
            ch.step(v.tensor_copy(k.before[:, :], mlow[:, :]))
            ch.link(v.tensor_scalar(k.trash[:, :], part[:, :], float(P * NT), None, ALU.add))
            ch.link(v.tensor_copy(srcT[:, :], srcT_i[:, :]))
            v.tensor_copy(src_hi[:, :], srcT[:, :]).then_inc(src_split, 1)
            v.wait_ge(src_split, 1)
            v.tensor_tensor(src_lo[:, :], srcT[:, :], src_hi[:, :], ALU.subtract).then_inc(src_split, 1)
            for i in range(3):
                ch.step(v.tensor_scalar(pick[:, i:i + 1], part[:, :], float(i), None, ALU.is_equal))
            ch.step(v.memset(k.ones_bf[:, :], 1.0))
            ch.link(v.memset(fb_sum[:, :], 0.0))
            for i in range(3):
                ch.link(v.tensor_copy(fb_part[:, :], fb[:, :]))
                ch.link(v.scalar_tensor_tensor(out=fb_sum[:, :], in0=fb_part[:, :], scalar=pick[0:3, i:i + 1], in1=fb_sum[:, :], op0=ALU.mult, op1=ALU.add))
                ch.link(v.tensor_tensor(fb[:, :], fb[:, :], fb_part[:, :], ALU.subtract))
            ch.step(v.tensor_copy(k.fb2[:, :], fb_sum[:, :]))
            v.wait_ge(pe_step, 1)
            ch.link(v.tensor_copy(k.seam[:, :], seam_ps[:, 0:P]))
            v.wait_ge(pe_step, 2)
            ch.link(v.tensor_copy(k.w3[:, D:D + 8], w3_ps[:, 0:8]))
            v.wait_ge(cut_cos, 1)
            ch.link(v.scalar_tensor_tensor(out=k.cut[:, :], in0=dgt[:, :], scalar=1.0, in1=dist[:, :],
                                           op0=ALU.add, op1=ALU.mult))

        @block.scalar
        def _(act):
            act.wait_ge(cut_arg, 1)
            act.activation(dgt[:, :], dgt[:, :], ACT.Sin).then_inc(cut_cos, 1)

        @block.tensor
        def _(pe):
            pe.wait_ge(pool_step, 6)
            pe.wait_ge(seamT_ready, 1)
            pe.transpose(seam_ps[:, 0:P], k.seamT[:, :], k.ident[:, :]).then_inc(pe_step, 1)
            pe.wait_ge(dma_in, 16 * len(loads))
            pe.wait_ge(acol_in, 128)
            pe.matmul(w3_ps[:, 0:8], wfull[:, :], acol[:, :], start=True, stop=True).then_inc(pe_step, 1)


def clear_spread(eng, k, lo, n):
    v = k.spread[0:k.EP, :].rearrange("(p r s) c -> p r (s c)", p=P, s=JC)
    eng.dma_start(v[:, bass.ds(lo * 2, 2 * n), :], bc_mid(k.zero_rows[:, :], 2 * n)).then_inc(k.spread_cleared, 16)


def ends_phase(nc, k, a):
    NT, NG = k.NT, k.NG
    BN, BW = a["dst_blocks"].shape
    with Phase(nc, "ends") as ph:
        coarse = ph.sb("coarse", [P, BN])
        below = ph.sb("below", [P, GT, BN])
        bg, cg = ph.sb("bg", [P, GT]), ph.sb("cg", [P, GT])
        blk = ph.sb("blk", [P, NT])
        blk_i = ph.sb("blk_i", [P, NT], I32)
        bidx = ph.sb("bidx", [P, GT], I32)
        fine_i = ph.sb("fine_i", [P, GT, BW], I32)
        le = ph.sb("le", [P, GT, BW])
        c2 = ph.sb("c2", [P, NT])
        cnt = ph.sb("cnt", [P, NT])
        prev = ph.sb("prev", [P, NT])
        has = ph.sb("has", [P, NT])
        tmp = ph.sb("tmp", [P, NT])
        zero1 = ph.sb("zero1", [1, 1])
        dve_step = ph.sem("dve_step")
        blocks_found = ph.sem("blocks_found")
        bidx_ready = ph.sem("bidx_ready")
        fine_in = ph.sem("fine_in")
        fine_used = ph.sem("fine_used", credit=1)
        cnt_ready = ph.sem("cnt_ready")
        cnt_out = ph.sem("cnt_out")
        prev_in = ph.sem("prev_in")
        waited, waited_act = ph.sem("waited"), ph.sem("waited_act")
        block = ph.block()

        @block.sync
        def _(sp):
            ph.give_credits(sp)
            sp.wait_ge(cnt_ready, 1)
            sp.dma_start(k.counts[0:1, 0:1], zero1[:, :]).then_inc(cnt_out, 16)
            sp.dma_start(k.counts[0:1, 1:1 + P * NT].rearrange("o (p t) -> (o p) t", t=NT), cnt[:, :]).then_inc(cnt_out, 16)
            sp.wait_ge(cnt_out, 32)
            sp.dma_start(prev[:, :], k.counts[0:1, 0:P * NT].rearrange("o (p t) -> (o p) t", t=NT)).then_inc(prev_in, 16)
            sp.wait_ge(prev_in, 16)

        @block.gpsimd
        def _(pool):
            with pool.Fori(0, NG) as g:
                pool.wait_ge(blocks_found, g + 1)
                pool.wait_ge(fine_used, g + 1)
                pool.tensor_copy(bidx[:, :], blk_i[:, bass.ds(g * GT, GT)]).then_inc(bidx_ready, 1)
                pool.wait_ge(bidx_ready, g + 1)
                pool.sem_inc(waited, 1)
                for t in range(GT):
                    pool.indirect_dma_start(fine_i[:, t, :], None, a["dst_blocks"],
                                            bass.IndirectOffsetOnAxis(ap=bidx[:, t:t + 1], axis=0)).then_inc(fine_in, 16)

        @block.scalar
        def _(act):
            act.dma_start(k.starts[0:k.EP, :].rearrange("(p r s) c -> p r (s c)", p=P, s=JC),
                          bc_mid(k.zero_rows[:, 0:JC * HEADS], k.S // JC)).then_inc(k.spread_cleared, 16)
            with act.Fori(0, k.PIECES // 2) as c:
                act.wait_ge(k.spread_cleared, c * 16 + 16)
                act.sem_inc(waited_act, 1)
                clear_spread(act, k, c, 1)
            act.wait_ge(k.spread_cleared, (k.PIECES // 2 + 1) * 16)

        @block.vector
        def _(v):
            ch = Chain(v, dve_step)
            ch.step(v.memset(zero1[:, :], 0.0))
            ch.link(v.tensor_copy(coarse[:, :], k.coarse_i[:, :]))

            def find(g):
                at = bass.ds(g * GT, GT)
                ch.link(v.tensor_tensor(below[:, :, :], bc_mid(coarse[:, :], GT), bc_last(k.node[:, at], BN), ALU.is_le))
                ch.link(v.tensor_reduce(out=bg[:, :], in_=below[:, :, :], op=ALU.add, axis=AX.X))
                ch.link(v.tensor_scalar(bg[:, :], bg[:, :], -1.0, 0.0, ALU.add, ALU.max))
                ch.step(v.tensor_copy(blk[:, at], bg[:, :]))
                v.tensor_copy(blk_i[:, at], bg[:, :]).then_inc(blocks_found, 1)
                v.wait_ge(blocks_found, g + 1)

            def count(g):
                at = bass.ds(g * GT, GT)
                v.wait_ge(fine_in, g * (16 * GT) + 16 * GT)
                ch.link(v.tensor_tensor(le[:, :, :], fine_i[:, :, :], bc_last(k.node[:, at], BW), ALU.is_le))
                v.tensor_reduce(out=cg[:, :], in_=le[:, :, :], op=ALU.add, axis=AX.X).then_inc(fine_used, 1)
                v.wait_ge(fine_used, g + 2)
                ch.link(v.tensor_copy(c2[:, at], cg[:, :]))

            find(0)
            with v.Fori(1, NG) as g:
                ch.loop(g - 1, 6)
                find(g)
                count(g - 1)
            ch.end(NG - 1)
            count(NG - 1)
            v.scalar_tensor_tensor(out=cnt[:, :], in0=blk[:, :], scalar=float(BW), in1=c2[:, :],
                                   op0=ALU.mult, op1=ALU.add).then_inc(cnt_ready, 1)
            v.wait_ge(cnt_ready, 1)
            v.wait_ge(prev_in, 16)
            ch.link(v.tensor_tensor(k.deg[:, :], cnt[:, :], prev[:, :], ALU.subtract))
            ch.link(v.tensor_scalar(has[:, :], k.deg[:, :], 0.5, None, ALU.is_gt))
            ch.link(v.tensor_scalar(tmp[:, :], cnt[:, :], -1.0 - k.EP, None, ALU.add))
            ch.link(v.tensor_tensor(tmp[:, :], tmp[:, :], has[:, :], ALU.mult))
            ch.link(v.tensor_scalar(tmp[:, :], tmp[:, :], float(k.EP), None, ALU.add))
            ch.link(v.tensor_copy(k.end_row[:, :], tmp[:, :]))
            ch.link(v.tensor_tensor(tmp[:, :], prev[:, :], k.node[:, :], ALU.subtract))
            ch.link(v.tensor_scalar(tmp[:, :], tmp[:, :], -float(k.EP), None, ALU.add))
            ch.link(v.tensor_tensor(tmp[:, :], tmp[:, :], has[:, :], ALU.mult))
            ch.link(v.tensor_tensor(tmp[:, :], tmp[:, :], k.node[:, :], ALU.add))
            ch.link(v.tensor_scalar(tmp[:, :], tmp[:, :], float(k.EP), None, ALU.add))
            ch.link(v.tensor_copy(k.start_row[:, :], tmp[:, :]))




def two_ahead(eng, n, ahead, behind):
    ahead(0)
    ahead(1)
    if n > 2:
        ahead(2)
    behind(0)
    if n > 3:
        with eng.Fori(1, n - 2) as g:
            ahead(g + 2)
            behind(g)
    for g in range(max(1, n - 2), n):
        behind(g)


def node_phase(nc, k, a, post, pre):
    NT, NG = k.NT, k.NG
    W = {None: 0, 0: 136, 1: 0, 2: 128, 3: 136}[post]
    NC = {0: 256, 1: 128, 2: 128, 3: 136, None: 0}[pre]
    ST = {0: 256, 1: 128, 2: 128, 3: 256, None: 0}[pre]
    rows = {0: k.rows0, 1: None, 2: k.rows2, 3: k.rows0, None: None}[post]
    GW = {0: 136, 1: 0, 2: 128, 3: 136, None: 0}[post]
    TW = {0: 264, 1: 132, 2: 128, 3: 136, None: 0}[pre]
    SPREAD = pre in (0, 1, 3)
    n_out = {0: 32, 1: 16, 2: 16, 3: 32, None: 16}[pre]
    with Phase(nc, f"n{post}{pre}") as ph:
        N3 = [P, GT, D]
        s7, m7, v7, r7 = (ph.sb(x, [P, GT]) for x in ("s7", "m7", "v7", "r7"))
        cen, sq, h = ph.sb("cen", N3), ph.sb("sq", N3), ph.sb("h", N3)
        hT = ph.sb("hT", [P, GT * P])
        psA = ph.ps("psA", [P, 1024])
        psB = ph.ps("psB", [P, 1024])
        psC = ph.ps("psC", [P, 2048])
        if post is not None:
            y = ph.sb("y", N3)
        if post == 1:
            part = ph.sb("part", [P, SUMS, GT, D])
            y2 = ph.sb("y2", N3)
        elif post is not None:
            rg = ph.sb("rg", [P, GT, W])
            gidx = ph.sb("gidx", [P, GT], I32)
        if post == 0:
            fsn = ph.sb("fsn", N3)
            mx = ph.sb("mx", [P, GT, HEADS])
            ex = ph.sb("ex", [P, 2, GT * HEADS])
            den = ph.sb("den", [P, GT * HEADS])
        if post == 3:
            den = ph.sb("den", [P, GT, HEADS])
        if post == 2:
            aT = ph.sb("aT", [P, GT * P])
            uT = ph.sb("uT", [P, GT * P])
        if pre is not None:
            tab = ph.sb("tab", [P, GT, TW])
        if SPREAD:
            sidx = ph.sb("sidx", [P, GT], I32)
            sidx_ready, sent, tab_sent = ph.sem("sidx_ready"), ph.sem("sent"), ph.sem("tab_sent", credit=1)
        if pre == 0:
            e = ph.sb("e", N3)

        dve_step = ph.sem("dve_step")
        gidx_ready, rows_in, rows_used = ph.sem("gidx_ready"), ph.sem("rows_in"), ph.sem("rows_used", credit=1)
        fsn_in, fsn_used = ph.sem("fsn_in"), ph.sem("fsn_used", credit=1)
        ex_arg, ex_done = ph.sem("ex_arg"), ph.sem("ex_done")
        aT_ps, aT_ready, post_mm = ph.sem("aT_ps"), ph.sem("aT_ready"), ph.sem("post_mm")
        z_ps, u_ready, post_used = ph.sem("z_ps"), ph.sem("u_ready"), ph.sem("post_used", credit=1)
        x_done = ph.sem("x_done")
        cen_ready, sq_ready, var_ready, std_ready = ph.sem("cen_ready"), ph.sem("sq_ready"), ph.sem("var_ready"), ph.sem("std_ready")
        h_ready, hT_ps, hT_ready = ph.sem("h_ready"), ph.sem("hT_ps"), ph.sem("hT_ready")
        tab_ps, tab_ready, tab_out = ph.sem("tab_ps"), ph.sem("tab_ready", credit=1), ph.sem("tab_out", credit=n_out)
        gelu_arg, gelu_done = ph.sem("gelu_arg"), ph.sem("gelu_done")
        waited = ph.sem("waited")
        block = ph.block()
        fs_v = k.tab0s.rearrange("(p t) c -> p t c", t=NT)
        fd_v = k.tab0d.rearrange("(p t) c -> p t c", t=NT)
        t1_v = k.tab1.rearrange("(p t) c -> p t c", t=NT)
        t2_v = k.tab2.rearrange("(p t) c -> p t c", t=NT)
        t3_v = k.tab3.rearrange("(p t) c -> p t c", t=NT)
        ar_v = k.ar_tab.rearrange("(p t) c -> p t c", t=NT)
        out_v = a["out"].rearrange("(p t) c -> p t c", t=NT)

        @block.sync
        def _(sp):
            ph.give_credits(sp)

            def load(g):
                if post == 1:
                    sp.wait_ge(rows_used, g + 1)
                    for t in range(SUMS):
                        sp.dma_start(part[:, t, :, :], k.by_src[t][0:P * NT, :].rearrange("(p t) c -> p t c", t=NT)[:, bass.ds(g * GT, GT), :]).then_inc(rows_in, 16)
                if post == 0:
                    sp.wait_ge(fsn_used, g + 1)
                    sp.dma_start(fsn[:, :, :], fs_v[:, bass.ds(g * GT, GT), 0:D]).then_inc(fsn_in, 16)

            def store(g):
                at = bass.ds(g * GT, GT)
                if pre is not None:
                    sp.wait_ge(tab_ready, g + 2)
                if pre == 0:
                    sp.dma_start(fs_v[:, at, :], tab[:, :, 0:132]).then_inc(tab_out, 16)
                    sp.dma_start(fd_v[:, at, :], tab[:, :, 132:264]).then_inc(tab_out, 16)
                elif pre in (1, 2):
                    sp.dma_start((t1_v if pre == 1 else t2_v)[:, at, :], tab[:, :, :]).then_inc(tab_out, 16)
                elif pre == 3:
                    sp.dma_start(t3_v[:, at, :], tab[:, :, 0:132]).then_inc(tab_out, 16)
                    sp.dma_start(ar_v[:, at, :], tab[:, :, 132:136]).then_inc(tab_out, 16)
                else:
                    sp.wait_ge(x_done, g + 1)
                    sp.sem_inc(waited, 1)
                    sp.dma_start(out_v[:, at, :], k.X[:, at, :]).then_inc(tab_out, 16)

            two_ahead(sp, NG, load, store)
            sp.wait_ge(tab_out, (NG + 1) * n_out)

        @block.gpsimd
        def _(pool):
            def gather(g):
                if post in (None, 1):
                    return
                pool.wait_ge(rows_used, g + 1)
                pool.tensor_copy(gidx[:, :], k.end_row[:, bass.ds(g * GT, GT)]).then_inc(gidx_ready, 1)
                pool.wait_ge(gidx_ready, g + 1)
                pool.sem_inc(waited, 1)
                for t in range(GT):
                    pool.indirect_dma_start(rg[:, t, 0:GW], None, rows,
                                            bass.IndirectOffsetOnAxis(ap=gidx[:, t:t + 1], axis=0)).then_inc(rows_in, 16)

            def scatter(g):
                if not SPREAD:
                    return
                to, at = (k.starts, 132) if pre == 3 else (k.spread, TW - 132)
                if not (isinstance(g, int) and g == 0):
                    pool.wait_ge(sent, g * (16 * GT))
                    pool.sem_inc(tab_sent, 1)
                pool.tensor_copy(sidx[:, :], k.start_row[:, bass.ds(g * GT, GT)]).then_inc(sidx_ready, 1)
                pool.wait_ge(sidx_ready, g + 1)
                pool.wait_ge(tab_ready, g + 2)
                pool.sem_inc(waited, 1)
                for t in range(GT):
                    pool.indirect_dma_start(to, bass.IndirectOffsetOnAxis(ap=sidx[:, t:t + 1], axis=0), tab[:, t, at:TW], None).then_inc(sent, 16)

            if pre == 0:
                pool.wait_ge(k.spread_cleared, (k.PIECES // 2 + 2) * 16)
            two_ahead(pool, NG, gather, scatter)
            if SPREAD:
                pool.wait_ge(sent, NG * (16 * GT))

        @block.vector
        def _(v):
            ch = Chain(v, dve_step)
            if pre == 1:
                ch.link(v.memset(tab[:, :, 128:132], 0.0))

            def finish(g):
                xg = k.X[:, bass.ds(g * GT, GT), :]
                if post == 1:
                    v.wait_ge(rows_in, g * (16 * SUMS) + 16 * SUMS)
                elif post is not None:
                    v.wait_ge(rows_in, g * (16 * GT) + 16 * GT)
                if post == 0:
                    ss = k.sself[:, bass.ds(g * GT, GT), :]
                    flat = "p t h -> p (t h)"
                    ch.link(v.tensor_tensor(mx[:, :, :], rg[:, :, 132:136], ss, ALU.max))
                    ch.step(v.tensor_tensor(ex[:, 0, :].rearrange("p (t h) -> p t h", h=HEADS), rg[:, :, 132:136], mx[:, :, :], ALU.subtract))
                    v.tensor_tensor(ex[:, 1, :].rearrange("p (t h) -> p t h", h=HEADS), ss, mx[:, :, :], ALU.subtract).then_inc(ex_arg, 1)
                    v.wait_ge(ex_done, g + 1)
                    d3 = den[:, :].rearrange("p (t h) -> p t h", h=HEADS)
                    ch.link(v.tensor_tensor(d3, rg[:, :, 128:132], ex[:, 0, :].rearrange("p (t h) -> p t h", h=HEADS), ALU.mult))
                    ch.link(v.tensor_tensor(den[:, :], den[:, :], ex[:, 1, :], ALU.add))
                    ch.link(v.reciprocal(den[:, :], den[:, :]))
                    ch.link(v.tensor_tensor(ex[:, :, :], ex[:, :, :], bc_mid(den[:, :], 2), ALU.mult))
                    q4 = "p t (h c) -> p (t h) c"
                    a4 = rg[:, :, 0:D].rearrange("p t (h c) -> p t h c", h=HEADS)
                    v.tensor_tensor(y[:, :, :].rearrange("p t (h c) -> p t h c", h=HEADS), a4,
                                    bc_last(ex[:, 0, :].rearrange("p (t h) -> p t h", h=HEADS), HDIM), ALU.mult).then_inc(rows_used, 1)
                    v.wait_ge(fsn_in, g * 16 + 16)
                    v.tensor_tensor(cen[:, :, :].rearrange(q4, h=HEADS), fsn[:, :, :].rearrange(q4, h=HEADS),
                                    bc_last(ex[:, 1, :], HDIM), ALU.mult).then_inc(fsn_used, 1)
                    v.wait_ge(rows_used, g + 2)
                    v.wait_ge(fsn_used, g + 2)
                    v.tensor_tensor(y[:, :, :], y[:, :, :], cen[:, :, :], ALU.add).then_inc(post_mm, 1)
                    v.wait_ge(post_mm, g + 1)
                    v.scalar_tensor_tensor(out=xg, in0=y[:, :, :], scalar=0.0, in1=xg, op0=ALU.max, op1=ALU.add).then_inc(x_done, 1)
                    v.wait_ge(x_done, g + 1)
                elif post == 1:
                    ch.step(v.tensor_tensor(y[:, :, :], part[:, 0, :, :], part[:, 1, :, :], ALU.add))
                    v.tensor_tensor(y2[:, :, :], part[:, 2, :, :], part[:, 3, :, :], ALU.add).then_inc(rows_used, 1)
                    v.wait_ge(rows_used, g + 2)
                    ch.link(v.tensor_tensor(y[:, :, :], y[:, :, :], y2[:, :, :], ALU.add))
                    v.scalar_tensor_tensor(out=xg, in0=y[:, :, :], scalar=0.0, in1=xg, op0=ALU.max, op1=ALU.add).then_inc(x_done, 1)
                    v.wait_ge(x_done, g + 1)
                elif post == 2:
                    v.wait_ge(post_mm, g + 1)
                    v.tensor_tensor(y[:, :, :], psB[:, 0:GT * D].rearrange("p (t c) -> p t c", c=D), bc_mid(k.mb2[:, :], GT), ALU.add).then_inc(post_used, 1)
                    v.wait_ge(post_used, g + 2)
                    v.tensor_tensor(xg, y[:, :, :], xg, ALU.add).then_inc(x_done, 1)
                    v.wait_ge(x_done, g + 1)
                elif post == 3:
                    ch.link(v.tensor_scalar(den[:, :, :], rg[:, :, 128:132], 1e-9, None, ALU.add))
                    ch.link(v.reciprocal(den[:, :, :], den[:, :, :]))
                    v.tensor_tensor(y[:, :, :].rearrange("p t (h c) -> p t h c", h=HEADS),
                                    rg[:, :, 0:D].rearrange("p t (h c) -> p t h c", h=HEADS),
                                    bc_last(den[:, :, :], HDIM), ALU.mult).then_inc(rows_used, 1)
                    v.wait_ge(gelu_done, g + 1)
                    ch.link(v.tensor_reduce(out=s7[:, :], in_=y[:, :, :], op=ALU.add, axis=AX.X))
                    ch.link(v.tensor_scalar(m7[:, :], s7[:, :], 1.0 / D, None, ALU.mult))
                    v.tensor_tensor(cen[:, :, :], y[:, :, :], bc_last(m7[:, :], D), ALU.subtract).then_inc(cen_ready, 1)
                    v.wait_ge(sq_ready, g + 1)
                    ch.link(v.tensor_reduce(out=s7[:, :], in_=sq[:, :, :], op=ALU.add, axis=AX.X))
                    v.tensor_scalar(v7[:, :], s7[:, :], 1.0 / D, EPS, ALU.mult, ALU.add).then_inc(var_ready, 1)
                    v.wait_ge(std_ready, g + 1)
                    ch.link(v.reciprocal(r7[:, :], v7[:, :]))
                    ch.link(v.tensor_tensor(cen[:, :, :], cen[:, :, :], bc_last(r7[:, :], D), ALU.mult))
                    ch.link(v.tensor_tensor(cen[:, :, :], cen[:, :, :], bc_mid(k.lns[:, :], GT), ALU.mult))
                    ch.link(v.tensor_tensor(cen[:, :, :], cen[:, :, :], bc_mid(k.lnb[:, :], GT), ALU.add))
                    v.tensor_tensor(xg, cen[:, :, :], xg, ALU.add).then_inc(x_done, 1)
                    v.wait_ge(x_done, g + 1)

            def norm(g):
                xg = k.X[:, bass.ds(g * GT, GT), :]
                if pre is not None:
                    v.sem_inc(waited, 1)
                    ch.link(v.tensor_reduce(out=s7[:, :], in_=xg, op=ALU.add, axis=AX.X))
                    ch.link(v.tensor_scalar(m7[:, :], s7[:, :], 1.0 / D, None, ALU.mult))
                    v.tensor_tensor(cen[:, :, :], xg, bc_last(m7[:, :], D), ALU.subtract).then_inc(cen_ready, 1)
                    v.wait_ge(sq_ready, g + 1)
                    ch.link(v.tensor_reduce(out=s7[:, :], in_=sq[:, :, :], op=ALU.add, axis=AX.X))
                    v.tensor_scalar(v7[:, :], s7[:, :], 1.0 / D, EPS, ALU.mult, ALU.add).then_inc(var_ready, 1)
                    v.wait_ge(std_ready, g + 1)
                    ch.link(v.reciprocal(r7[:, :], v7[:, :]))
                    v.scalar_tensor_tensor(out=h[:, :, :], in0=cen[:, :, :], scalar=0.0, in1=bc_last(r7[:, :], D),
                                           op0=ALU.max, op1=ALU.mult).then_inc(h_ready, 1)
                    if pre == 2:
                        v.wait_ge(h_ready, g + 1)
                        ch.link(v.tensor_tensor(xg, xg, h[:, :, :], ALU.add))

            def table(g):
                if pre is not None:
                    v.wait_ge(tab_ps, g + 1)
                    v.wait_ge(tab_out, g * n_out + n_out)
                    v.sem_inc(waited, 1)
                    pc = psC[:, 0:GT * ST].rearrange("p (t c) -> p t c", c=ST)[:, :, 0:NC]
                    if SPREAD:
                        v.wait_ge(tab_sent, g + 1)
                        v.sem_inc(waited, 1)
                    if pre == 3:
                        v.tensor_copy(tab[:, :, :], pc).then_inc(tab_ready, 1)
                    elif pre == 0:
                        for half in range(2):
                            lo = half * 132
                            ch.step(v.tensor_tensor(tab[:, :, lo:lo + D], pc[:, :, half * D:half * D + D], bc_mid(k.b0[:, half * D:half * D + D], GT), ALU.add))
                        v.wait_ge(dve_step, ch.base + ch.n)
                        for half in range(2):
                            lo = half * 132
                            ch.link(v.tensor_tensor(e[:, :, :], tab[:, :, lo:lo + D], bc_mid(k.attn02[:, :], GT), ALU.mult))
                            r = v.tensor_reduce(out=tab[:, :, lo + D:lo + 132], in_=e[:, :, :].rearrange("p t (h c) -> p t h c", h=HEADS), op=ALU.add, axis=AX.X)
                            if half == 0:
                                ch.link(r)
                            else:
                                r.then_inc(tab_ready, 1)
                    else:
                        bias = {1: k.b1, 2: k.pb}[pre]
                        v.tensor_tensor(tab[:, :, 0:D], pc, bc_mid(bias[:, :], GT), ALU.add).then_inc(tab_ready, 1)
                    if pre == 3:
                        v.wait_ge(tab_ready, g + 2)
                    if pre == 0:
                        v.wait_ge(tab_ready, g + 2)
                        ch.link(v.tensor_tensor(e[:, :, :], tab[:, :, 0:D], tab[:, :, 132:132 + D], ALU.add))
                        ch.link(v.scalar_tensor_tensor(out=e[:, :, :], in0=e[:, :, :], scalar=0.2, in1=e[:, :, :], op0=ALU.mult, op1=ALU.max))
                        ch.link(v.tensor_tensor(e[:, :, :], e[:, :, :], bc_mid(k.attn[:, :], GT), ALU.mult))
                        v.sem_inc(waited, 1)
                        ch.link(v.tensor_reduce(out=k.sself[:, bass.ds(g * GT, GT), :], in_=e[:, :, :].rearrange("p t (h c) -> p t h c", h=HEADS),
                                                op=ALU.add, axis=AX.X))

            turn = {None: 0, 0: 6, 1: 2, 2: 0, 3: 9}[post] + {0: 13, 1: 4, 2: 5, 3: 4, None: 0}[pre]
            finish(0)
            norm(0)
            with v.Fori(1, NG) as g:
                ch.loop(g - 1, turn)
                finish(g)
                norm(g)
                table(g - 1)
            ch.end(NG - 1)
            table(NG - 1)

        @block.scalar
        def _(act):
            if pre == 0:
                clear_spread(act, k, k.PIECES // 2, k.PIECES - k.PIECES // 2)

            def mlp(g):
                act.wait_ge(aT_ps, g + 1)
                act.activation(aT[:, :], psA[:, 0:GT * P], ACT.Copy).then_inc(aT_ready, 1)
                act.wait_ge(z_ps, g + 1)
                act.activation(uT[:, :], psB[:, 0:GT * P], ACT.Silu, bias=k.mb1[:, 0:1]).then_inc(u_ready, 1)

            def group(g, final):
                if post == 0:
                    act.wait_ge(ex_arg, g + 1)
                    act.activation(ex[:, :, :], ex[:, :, :], ACT.Exp).then_inc(ex_done, 1)
                if post == 3:
                    act.wait_ge(rows_used, g + 2)
                    act.activation(y[:, :, :], y[:, :, :], ACT.Gelu).then_inc(gelu_done, 1)
                if pre is not None or post == 3:
                    act.wait_ge(cen_ready, g + 1)
                    act.activation(sq[:, :, :], cen[:, :, :], ACT.Square).then_inc(sq_ready, 1)
                    act.wait_ge(var_ready, g + 1)
                    act.activation(v7[:, :], v7[:, :], ACT.Sqrt).then_inc(std_ready, 1)
                if post == 2 and not final:
                    mlp(g + 1)
                if pre is not None:
                    act.wait_ge(hT_ps, g + 1)
                    act.activation(hT[:, :], psA[:, 0:GT * P], ACT.Copy).then_inc(hT_ready, 1)

            if post == 2:
                mlp(0)
            with act.Fori(0, NG - 1) as g:
                group(g, False)
            group(NG - 1, True)

        @block.tensor
        def _(pe):
            def mlp(g):
                pe.wait_ge(rows_in, g * (16 * GT) + 16 * GT)
                for t in range(GT):
                    last = pe.transpose(psA[:, t * P:(t + 1) * P], rg[:, t, :], k.ident[:, :])
                last.then_inc(aT_ps, 1)
                pe.wait_ge(aT_ps, g + 1)
                pe.sem_inc(rows_used, 1)
                pe.wait_ge(aT_ready, g + 1)
                pe.wait_ge(post_used, g + 1)
                pe.matmul(psB[:, 0:512], k.mw1[:, :], aT[:, 0:512], start=True, stop=True)
                pe.matmul(psB[:, 512:GT * P], k.mw1[:, :], aT[:, 512:GT * P], start=True, stop=True).then_inc(z_ps, 1)
                pe.wait_ge(u_ready, g + 1)
                for t in range(GT):
                    last = pe.matmul(psB[:, t * D:(t + 1) * D], uT[:, t * P:(t + 1) * P], k.mw2[:, :], start=True, stop=True)
                last.then_inc(post_mm, 1)

            def group(g, final):
                if post == 2 and not final:
                    mlp(g + 1)
                if pre is not None:
                    w = {0: k.w0, 1: k.w1, 2: k.pw, 3: k.w3}[pre]
                    pe.wait_ge(h_ready, g + 1)
                    for t in range(GT):
                        last = pe.transpose(psA[:, t * P:(t + 1) * P], h[:, t, :], k.ident[:, :])
                    last.then_inc(hT_ps, 1)
                    pe.wait_ge(hT_ready, g + 1)
                    pe.wait_ge(tab_ready, g + 1)
                    for t in range(GT):
                        last = pe.matmul(psC[:, t * ST:t * ST + NC], hT[:, t * P:(t + 1) * P], w[:, 0:NC], start=True, stop=True)
                    last.then_inc(tab_ps, 1)

            if post == 2:
                mlp(0)
            if pre is not None:
                with pe.Fori(0, NG - 1) as g:
                    group(g, False)
                group(NG - 1, True)




def fill_step(v, ch, k, ph, z_in, n, F, kb, at, carry, filled, filled_at):
    ch.link(v.tensor_copy(kb[:, :], k.keep[:, at]))
    v.wait_ge(z_in, n)
    for j in range(JC):
        prev = carry[:, :] if j == 0 else F[:, j - 1, :]
        ch.link(v.scalar_tensor_tensor(out=F[:, j, :], in0=prev, scalar=kb[:, j:j + 1], in1=F[:, j, :], op0=ALU.mult, op1=ALU.add))
    v.tensor_copy(carry[:, :], F[:, JC - 1, :]).then_inc(filled, 1)
    v.wait_ge(filled, filled_at)


FILL_STEPS = 1 + JC


def edge_phase(nc, k, a, layer):
    S, TURNS = k.S, k.TURNS
    SOFT = layer in (0, 3)
    W = {0: 136, 2: 128, 3: 136}[layer]
    SUM = {0: 132, 2: 128, 3: 132}[layer]
    GC = {0: 132, 2: 128, 3: 132}[layer]
    table = {0: k.tab0s, 2: k.tab2, 3: k.tab3}[layer]
    rows = {0: k.rows0, 2: k.rows2, 3: k.rows0}[layer]
    rows_v = rows[0:k.EP, :].rearrange("(p s) c -> p s c", s=S)
    z_v = k.spread[0:k.EP, :].rearrange("(p s) c -> p s c", s=S)
    NB = JC // 4
    TB = BUFS * NB
    with Phase(nc, f"e{layer}") as ph:
        R = [ph.sb(f"row{q}", [P, JC, W]) for q in range(BUFS)]
        sidx = [ph.sb(f"sidx{q}", [P, JC], I32) for q in range(BUFS)]
        kb = [ph.sb(f"kb{q}", [P, JC + 1]) for q in range(BUFS)]
        last = k.last
        carry = ph.sb("carry", [P, 132])
        if SOFT:
            ng = ph.sb("ng", [P, JC + 1])
            sc, run, M = (ph.sb(x, [P, HEADS, JC]) for x in ("sc", "run", "M"))
            df = ph.sb("df", [P, HEADS, JC + 1])
            rc = ph.sb("rc", [P, HEADS])
            scp = [ph.ps(f"scp{z}", [P, 512]) for z in range(2)]
            scp_ready = ph.sem("scp_ready")
            scp_used = [ph.sem(f"scp_used{z}", credit=1) for z in range(2)]
        if layer == 0:
            F = [ph.sb(f"f{z}", [P, JC, 132]) for z in range(2)]
            fcarry = ph.sb("fcarry", [P, 132])
            rT = ph.sb("rT", [P, 2048])
            eT = ph.ps("eT", [P, 2048])
            z_in = [ph.sem(f"z_in{z}") for z in range(2)]
            filled, first_in = ph.sem("filled"), ph.sem("first_in")
            eT_ready, r_ready, r_used = ph.sem("eT_ready"), ph.sem("r_ready", credit=4), ph.sem("r_used", credit=4)
        if layer == 3:
            floor = ph.sb("floor", [P, HEADS, JC])
            eft = [ph.sb(f"eft{z}", [16, JC * P]) for z in range(2)]
            attr_in = [ph.sem(f"attr_in{z}") for z in range(2)]
        if layer == 2:
            cb = ph.sb("cb", [P, JC])
            dist = ph.sb("dist", [51, JC * P])
            rbf = ph.sb("rbf", [51, JC * P])
            u = ph.sb("u", [P, JC * P])
            zps = ph.ps("zps", [P, 2048])
            wps = ph.ps("wps", [P, 2048])
            dist_in, dist_used = ph.sem("dist_in"), ph.sem("dist_used")
            rbf_ready = ph.sem("rbf_ready")
            z_ready, u_ready, w_ready, w_used = (ph.sem(x, credit=NB) for x in ("z_ready", "u_ready", "w_ready", "w_used"))

        dve_step = ph.sem("dve_step")
        idx_in = [ph.sem(f"idx_in{q}") for q in range(BUFS)]
        rows_in = [ph.sem(f"rows_in{q}") for q in range(BUFS)]
        rows_out = [ph.sem(f"rows_out{q}", credit=16) for q in range(BUFS)]
        summed = ph.sem("summed")
        exp_arg, exp_done = ph.sem("exp_arg"), ph.sem("exp_done")
        waited = ph.sem("waited")
        block = ph.block()

        @block.sync
        def _(sp):
            ph.give_credits(sp)

            def load_idx(q, at):
                sp.dma_start(sidx[q][:, :], a["src"][:, at]).then_inc(idx_in[q], 16)

            def load_chunk(q, c):
                z = q % 2
                if layer == 0:
                    sp.dma_start(F[z][:, :, :], z_v[:, bass.ds(c * JC, JC), :]).then_inc(z_in[z], 16)
                if layer == 3:
                    sp.dma_start(eft[z][:, :], a["edge_attr_16_T"][:, bass.ds(c * (JC * P), JC * P)]).then_inc(attr_in[z], 16)

            def load_dist(c):
                sp.dma_start(dist[:, :], a["dist_T"][0:1, bass.ds(c * (JC * P), JC * P)].to_broadcast([51, JC * P])).then_inc(dist_in, 16)

            for q in range(BUFS):
                load_idx(q, bass.ds(q * JC, JC))
            for q in range(2):
                load_chunk(q, q)
            if layer == 2:
                load_dist(0)

            def turn(i, final):
                for q in range(BUFS):
                    if layer == 2 and not (final and q == BUFS - 1):
                        sp.wait_ge(dist_used, i * BUFS + q + 1)
                        sp.sem_inc(waited, 1)
                        load_dist(i * BUFS + (q + 1))
                    if not final:
                        sp.wait_ge(rows_in[q], (i + 1) * (16 * JC))
                        sp.sem_inc(waited, 1)
                        load_idx(q, bass.ds((i + 1) * (BUFS * JC) + q * JC, JC))
                    if SOFT and not (final and q >= BUFS - 2):
                        sp.wait_ge(scp_used[q % 2], i * (BUFS // 2) + (q // 2 + 2))
                        sp.sem_inc(waited, 1)
                        load_chunk(q, i * BUFS + (q + 2))
                    sp.wait_ge(summed, i * BUFS + (q + 1))
                    sp.dma_start(rows_v[:, bass.ds(i * (BUFS * JC) + q * JC, JC), :], R[q][:, :, :]).then_inc(rows_out[q], 16)

            with sp.Fori(0, TURNS - 1) as i:
                turn(i, False)
            turn(TURNS - 1, True)
            for q in range(BUFS):
                sp.wait_ge(rows_out[q], TURNS * 16 + 16)

        @block.gpsimd
        def _(pool):
            if layer == 0:
                pool.indirect_dma_start(fcarry[:, :], None, k.tab0d, bass.IndirectOffsetOnAxis(ap=k.first_dst[:, 0:1], axis=0)).then_inc(first_in, 16)
            with pool.Fori(0, TURNS) as i:
                for q in range(BUFS):
                    pool.wait_ge(idx_in[q], (i + 1) * 16)
                    pool.wait_ge(rows_out[q], i * 16 + 16)
                    pool.sem_inc(waited, 1)
                    for j in range(JC):
                        pool.indirect_dma_start(R[q][:, j, 0:GC], None, table,
                                                bass.IndirectOffsetOnAxis(ap=sidx[q][:, j:j + 1], axis=0)).then_inc(rows_in[q], 16)

        @block.vector
        def _(v):
            ch = Chain(v, dve_step)
            ch.link(v.memset(last[:, 0:SUM], 0.0))
            if SOFT:
                ch.link(v.memset(last[:, 132:136], -BIG))

            def fill(i, q, c):
                fill_step(v, ch, k, ph, z_in[q % 2], i * (BUFS // 2 * 16) + (q // 2 + 1) * 16, F[q % 2], kb[q % BUFS],
                          bass.ds(c * JC, JC + 1), fcarry, filled, c + 1)

            if layer == 0:
                v.wait_ge(first_in, 16)
                ch.link(v.tensor_scalar(fcarry[:, :], fcarry[:, :], k.cont[:, 0:1], None, ALU.mult))
                fill(0, 0, 0)

            def chunk(i, q, final):
                at = i * (BUFS * JC) + q * JC
                c1 = i * BUFS + (q + 1)
                z = q % 2
                rq = R[q]
                if layer == 0:
                    if not (final and q == BUFS - 1):
                        fill(i, q + 1, i * BUFS + (q + 1))
                else:
                    ch.link(v.tensor_copy(kb[q][:, :], k.keep[:, bass.ds(at, JC + 1)]))
                if SOFT:
                    ch.link(v.tensor_scalar(ng[:, :], kb[q][:, :], -1.0, BIG, ALU.add, ALU.mult))
                v.wait_ge(rows_in[q], (i + 1) * (16 * JC))
                if SOFT:
                    v.wait_ge(scp_ready, c1)
                    scv = scp[z][:, 0:JC * HEADS].rearrange("p (j h) -> p h j", h=HEADS)
                if layer == 0:
                    ch.link(v.tensor_tensor(sc[:, :, :], rq[:, :, 128:132].rearrange("p j h -> p h j"), F[z][:, :, 128:132].rearrange("p j h -> p h j"), ALU.add))
                    v.tensor_tensor(sc[:, :, :], sc[:, :, :], scv, ALU.add).then_inc(scp_used[z], 1)
                    v.wait_ge(scp_used[z], i * (BUFS // 2) + (q // 2 + 2))
                    top = sc
                if layer == 3:
                    ch.link(v.tensor_tensor(sc[:, :, :], rq[:, :, 128:132].rearrange("p j h -> p h j"), k.AR[:, :, bass.ds(at, JC)], ALU.add))
                    ch.link(v.scalar_tensor_tensor(out=sc[:, :, :], in0=sc[:, :, :], scalar=0.2, in1=sc[:, :, :], op0=ALU.mult, op1=ALU.max))
                    v.tensor_tensor(sc[:, :, :], sc[:, :, :], scv, ALU.add).then_inc(scp_used[z], 1)
                    v.wait_ge(scp_used[z], i * (BUFS // 2) + (q // 2 + 2))
                    ch.link(v.tensor_scalar(floor[:, :, :], sc[:, :, :], -1e9, None, ALU.max))
                    top = floor
                if SOFT:
                    for h in range(HEADS):
                        ch.step(v.tensor_tensor_scan(out=run[:, h, :], data0=ng[:, 0:JC], data1=top[:, h, :],
                                                     initial=last[:, 132 + h:133 + h], op0=ALU.add, op1=ALU.max))
                    v.wait_ge(dve_step, ch.base + ch.n)
                    for h in range(HEADS):
                        ch.step(v.tensor_tensor_scan(out=M[:, h, ::-1], data0=ng[:, JC:0:-1], data1=run[:, h, ::-1],
                                                     initial=-BIG, op0=ALU.add, op1=ALU.max))
                    v.wait_ge(dve_step, ch.base + ch.n)
                    ch.step(v.tensor_tensor(df[:, :, 0:JC], sc[:, :, :], M[:, :, :], ALU.subtract))
                    ch.link(v.tensor_tensor(df[:, :, JC:JC + 1], last[:, 132:136].unsqueeze(2), M[:, :, 0:1], ALU.subtract))
                    v.tensor_scalar(df[:, :, JC:JC + 1], df[:, :, JC:JC + 1], 0.0, None, ALU.min).then_inc(exp_arg, 1)
                    ch.step(v.tensor_copy(rq[:, :, 132:136].rearrange("p j h -> p h j"), M[:, :, :]))
                    v.wait_ge(exp_done, c1 * 2)
                    ch.step(v.tensor_tensor(rq[:, :, 0:D].rearrange("p j (h c) -> p j h c", h=HEADS), rq[:, :, 0:D].rearrange("p j (h c) -> p j h c", h=HEADS),
                                            bc_last(rq[:, :, 128:132], HDIM), ALU.mult))
                    ch.step(v.tensor_tensor(carry[:, 0:D].rearrange("p (h c) -> p h c", h=HEADS), last[:, 0:D].rearrange("p (h c) -> p h c", h=HEADS),
                                            bc_last(rc[:, :], HDIM), ALU.mult))
                    ch.link(v.tensor_tensor(carry[:, D:D + HEADS], last[:, D:D + HEADS], rc[:, :], ALU.mult))
                    before = carry[:, 0:SUM]
                else:
                    before = last[:, 0:SUM]
                if layer == 2:
                    ch.link(v.tensor_copy(cb[:, :], k.cut[:, bass.ds(at, JC)]))
                    for b in range(NB):
                        v.wait_ge(w_ready, i * TB + (q * NB + b + 1 + NB))
                        for j in range(4):
                            s = 4 * b + j
                            ins = v.scalar_tensor_tensor(out=rq[:, s, :], in0=ring(wps, q * NB + b, j), scalar=cb[:, s:s + 1], in1=rq[:, s, :],
                                                         op0=ALU.mult, op1=ALU.mult)
                            if j < 3:
                                ch.step(ins)
                            else:
                                ins.then_inc(w_used, 1)
                    v.wait_ge(w_used, i * TB + (q + 2) * NB)
                for j in range(JC):
                    prev = before if j == 0 else rq[:, j - 1, 0:SUM]
                    ch.link(v.scalar_tensor_tensor(out=rq[:, j, 0:SUM], in0=prev, scalar=kb[q][:, j:j + 1], in1=rq[:, j, 0:SUM],
                                                   op0=ALU.mult, op1=ALU.add))
                v.tensor_copy(last[:, 0:W], rq[:, JC - 1, 0:W]).then_inc(summed, 1)
                v.wait_ge(summed, c1)

            per_turn = BUFS * (JC + {0: 16 + FILL_STEPS, 2: 2 + 3 * NB, 3: 19}[layer])
            with v.Fori(0, TURNS - 1) as i:
                ch.loop(i, per_turn)
                for q in range(BUFS):
                    chunk(i, q, False)
            ch.end(TURNS - 1)
            for q in range(BUFS):
                chunk(TURNS - 1, q, True)

        @block.scalar
        def _(act):
            with act.Fori(0, TURNS) as i:
                for q in range(BUFS):
                    n = i * BUFS + q
                    if layer == 0:
                        for b in range(NB):
                            m = i * TB + (q * NB + b)
                            act.wait_ge(eT_ready, m + 1)
                            act.wait_ge(r_used, m + 1)
                            act.activation(ring(rT, q * NB + b), ring(eT, q * NB + b), ACT.Relu, scale=0.8).then_inc(r_ready, 1)
                    if SOFT:
                        act.wait_ge(exp_arg, n + 1)
                        act.activation(R[q][:, :, 128:132].rearrange("p j h -> p h j"), df[:, :, 0:JC], ACT.Exp).then_inc(exp_done, 1)
                        act.activation(rc[:, :].unsqueeze(2), df[:, :, JC:JC + 1], ACT.Exp).then_inc(exp_done, 1)
                    if layer == 2:
                        act.wait_ge(dist_in, n * 16 + 16)
                        act.wait_ge(z_ready, n * NB + NB)
                        act.activation(rbf[:, :], dist[:, :], ACT.Square, bias=k.rbf_bias[0:51, 0:1], scale=k.rbf_scale[0:51, 0:1]).then_inc(dist_used, 1)
                        act.wait_ge(dist_used, n + 1)
                        act.activation(rbf[:, :], rbf[:, :], ACT.Exp, scale=-50.0).then_inc(rbf_ready, 1)
                        act.wait_ge(w_ready, n * NB + NB)
                        for b in range(NB):
                            act.wait_ge(z_ready, n * NB + b + 1 + NB)
                            act.activation(u[:, b * 512:(b + 1) * 512], ring(zps, q * NB + b), ACT.Silu).then_inc(u_ready, 1)

        @block.tensor
        def _(pe):
            if layer == 0:
                with pe.Fori(0, TURNS) as i:
                    for q in range(BUFS):
                        z = q % 2
                        pe.wait_ge(rows_in[q], (i + 1) * (16 * JC))
                        pe.wait_ge(filled, i * BUFS + (q + 1))
                        pe.wait_ge(scp_used[z], i * (BUFS // 2) + (q // 2 + 1))

                        def sums(b):
                            pe.wait_ge(r_ready, i * TB + (q * NB + b + 1))
                            for j in range(4):
                                o = ring(eT, q * NB + b, j)
                                pe.matmul(o, R[q][:, 4 * b + j, 0:D], k.ident[:, :], start=True, stop=False)
                                mm = pe.matmul(o, F[z][:, 4 * b + j, 0:D], k.ident[:, :], start=False, stop=True)
                            mm.then_inc(eT_ready, 1)

                        def scores(b):
                            pe.wait_ge(r_ready, i * TB + (q * NB + b + 5))
                            for j in range(4):
                                mm = pe.matmul(scp[z][:, (4 * b + j) * HEADS:(4 * b + j + 1) * HEADS], ring(rT, q * NB + b, j), k.attn_cols[:, :], start=True, stop=True)
                            mm.then_inc(r_used, 1)

                        sums(0)
                        for b in range(NB):
                            if b + 1 < NB:
                                sums(b + 1)
                            scores(b)
                        pe.wait_ge(r_used, i * TB + (q * NB + NB + 4))
                        pe.sem_inc(scp_ready, 1)
            if layer == 3:
                with pe.Fori(0, TURNS) as i:
                    for q in range(BUFS):
                        z = q % 2
                        pe.wait_ge(attr_in[z], i * (BUFS // 2 * 16) + (q // 2 + 1) * 16)
                        pe.wait_ge(scp_used[z], i * (BUFS // 2) + (q // 2 + 1))
                        for j in range(JC):
                            mm = pe.matmul(scp[z][:, j * HEADS:(j + 1) * HEADS], eft[z][:, j * P:(j + 1) * P], k.wet[:, :], start=True, stop=True)
                        mm.then_inc(scp_ready, 1)
            if layer == 2:
                with pe.Fori(0, TURNS) as i:
                    for q in range(BUFS):
                        n = i * BUFS + q

                        def z_block(b):
                            pe.matmul(ring(zps, q * NB + b), k.fw1[:, :], rbf[:, b * 512:(b + 1) * 512], start=True, stop=True).then_inc(z_ready, 1)

                        pe.wait_ge(rbf_ready, n + 1)
                        pe.wait_ge(u_ready, n * NB + NB)
                        for b in range(3):
                            z_block(b)
                        for b in range(NB):
                            if b + 3 < NB:
                                if b >= 1:
                                    pe.wait_ge(u_ready, n * NB + b + NB)
                                z_block(b + 3)
                            pe.wait_ge(u_ready, n * NB + b + 1 + NB)
                            pe.wait_ge(w_used, n * NB + b - 3 + NB)
                            pe.matmul(ring(wps, q * NB + b), k.ones_bf[:, :], k.fb2[:, :], start=True, stop=False)
                            for j in range(4):
                                mm = pe.matmul(ring(wps, q * NB + b, j), u[:, (4 * b + j) * P:(4 * b + j + 1) * P], k.fw2[:, :], start=False, stop=(j == 3))
                            mm.then_inc(w_ready, 1)


def scatter_phase(nc, k, a):
    S, NT, NP = k.S, k.NT, P * k.NT
    TURNS = S // (2 * JC)
    NB = JC // 4
    z_v = k.spread[0:k.EP, :].rearrange("(p s) c -> p s c", s=S)
    with Phase(nc, "e1") as ph:
        scol_i = [ph.sb(f"scol_i{q}", [P, JC], I32) for q in range(2)]
        F = [ph.sb(f"f{q}", [P, JC, 132]) for q in range(2)]
        kb = [ph.sb(f"kb{q}", [P, JC + 1]) for q in range(2)]
        fcarry = ph.sb("fcarry", [P, 132])
        attr = [ph.sb(f"attr{q}", [65, JC * P]) for q in range(2)]
        srow = [ph.sb(f"srow{q}", [2, JC * P], BF) for q in range(2)]
        scol = ph.sb("scol", [P, JC])
        same = [ph.sb(f"same{z}", [P, 4, P]) for z in range(2)]
        dup = ph.sb("dup", [P, 4, P])
        first = ph.sb("first", [P, JC])
        sums = [ph.sb(f"sums{q}", [P, JC, D]) for q in range(2)]
        to_f = ph.sb("to_f", [P, JC])
        to = [ph.sb(f"to{q}", [P, JC], I32) for q in range(2)]
        zn = max(z for z in range(1, JC + 1) if (NT + 1) % z == 0)
        zero = ph.sb("zero", [P, zn * D])
        bps = [ph.ps(f"bps{z}", [P, 512]) for z in range(2)]
        vps = [ph.ps(f"vps{z}", [P, 512]) for z in range(2)]
        sps = [ph.ps(f"sps{z}", [P, 512]) for z in range(2)]

        dve_step = ph.sem("dve_step")
        zero_ready = ph.sem("zero_ready")
        z_in = [ph.sem(f"z_in{q}") for q in range(2)]
        filled, first_in = ph.sem("filled"), ph.sem("first_in")
        scol_in, attr_in = ([ph.sem(f"{n}{q}") for q in range(2)] for n in ("scol_in", "attr_in"))
        srow_in = [ph.sem(f"srow_in{q}") for q in range(2)]
        scol_ready = ph.sem("scol_ready", credit=1)
        to_ready = ph.sem("to_ready")
        scattered = [ph.sem(f"scattered{t}") for t in range(SUMS)]
        landed = ph.sem("landed", credit=2)
        b_ready, v_ready, same_ready, msg_ready, sum_ready, sum_out = (
            ph.sem(n, credit=NB) for n in ("b_ready", "v_ready", "same_ready", "msg_ready", "sum_ready", "sum_out"))
        waited = ph.sem("waited")
        block = ph.block()

        @block.sync
        def _(sp):
            ph.give_credits(sp)

            def load(q, c):
                sp.dma_start(F[q][:, :, :], z_v[:, bass.ds(c * JC, JC), :]).then_inc(z_in[q], 16)
                sp.dma_start(attr[q][0:64, :], a["edge_attr_64_T"][:, bass.ds(c * (JC * P), JC * P)]).then_inc(attr_in[q], 16)
                sp.dma_start(srow[q][:, :], k.src_parts[:, bass.ds(c * (JC * P), JC * P)]).then_inc(srow_in[q], 16)
                sp.dma_start(scol_i[q][:, :], a["src"][:, bass.ds(c * JC, JC)]).then_inc(scol_in[q], 16)

            load(0, 0)
            load(1, 1)
            with sp.Fori(0, TURNS - 1) as i:
                for q in range(2):
                    sp.wait_ge(sum_ready, i * (2 * NB) + (q + 2) * NB)
                    sp.sem_inc(waited, 1)
                    load(q, i * 2 + (q + 2))

        @block.gpsimd
        def _(pool):
            pool.indirect_dma_start(fcarry[:, :], None, k.tab1, bass.IndirectOffsetOnAxis(ap=k.first_dst[:, 0:1], axis=0)).then_inc(first_in, 16)
            pool.wait_ge(zero_ready, 1)
            for t in range(SUMS):
                pool.dma_start(k.by_src[t].rearrange("(p r t) c -> p r (t c)", p=P, t=zn), bc_mid(zero[:, :], (NT + 1) // zn)).then_inc(scattered[t], 16)
            with pool.Fori(0, TURNS) as i:
                for q in range(2):
                    pool.wait_ge(to_ready, i * 2 + q + 1)
                    for j in range(JC):
                        if j % 4 == 0:
                            pool.wait_ge(sum_out, i * (2 * NB) + (q * NB + j // 4 + 1 + NB))
                        pool.wait_ge(scattered[j % SUMS], i * (2 * JC // SUMS * 16) + ((q * JC + j) // SUMS + 1) * 16)
                        pool.sem_inc(landed if j == SUMS - 1 else waited, 1)
                        pool.indirect_dma_start(k.by_src[j % SUMS], bass.IndirectOffsetOnAxis(ap=to[q][:, j:j + 1], axis=0),
                                                sums[q][:, j, :], None, compute_op=ALU.add).then_inc(scattered[j % SUMS], 16)
            for t in range(SUMS):
                pool.wait_ge(scattered[t], TURNS * (2 * JC // SUMS * 16) + 16)

        @block.vector
        def _(v):
            ch = Chain(v, dve_step)
            ch.step(v.memset(attr[0][64:65, :], 1.0))
            ch.link(v.memset(attr[1][64:65, :], 1.0))
            v.memset(zero[:, :], 0.0).then_inc(zero_ready, 1)

            def fill(i, q, c):
                fill_step(v, ch, k, ph, z_in[q % 2], i * 16 + (q // 2 + 1) * 16, F[q % 2], kb[q % 2], bass.ds(c * JC, JC + 1), fcarry, filled, c + 1)

            v.wait_ge(first_in, 16)
            ch.link(v.tensor_scalar(fcarry[:, :], fcarry[:, :], k.cont[:, 0:1], None, ALU.mult))
            fill(0, 0, 0)

            def chunk(i, q, final):
                v.wait_ge(scol_in[q], i * 16 + 16)
                v.tensor_copy(scol[:, :], scol_i[q][:, :]).then_inc(scol_ready, 1)
                v.wait_ge(scol_ready, i * 2 + (q + 2))
                for b in range(NB):
                    n = i * (2 * NB) + (q * NB + b + 1 + NB)
                    z = (q * NB + b) % 2
                    hb = F[q][:, 4 * b:4 * b + 4, 0:D]
                    v.wait_ge(v_ready, n)
                    v.tensor_tensor(hb, hb, vps[z][:, :].rearrange("p (j c) -> p j c", c=D), ALU.add).then_inc(msg_ready, 1)
                    if q * NB + b >= 2:
                        v.wait_ge(sum_ready, n - 2)
                    else:
                        v.wait_ge(sum_ready, i * (2 * NB) + NB)
                    v.wait_ge(b_ready, n)
                    v.tensor_tensor(same[z][:, :, :], bps[z][:, :].rearrange("p (j f) -> p j f", f=P),
                                    bc_last(scol[:, 4 * b:4 * b + 4], P), ALU.is_equal).then_inc(same_ready, 1)
                    v.wait_ge(same_ready, n)
                    ch.link(v.tensor_tensor(dup[:, :, :], same[z][:, :, :], bc_mid(k.before[:, :], 4), ALU.mult))
                    ch.link(v.tensor_reduce(out=first[:, 4 * b:4 * b + 4], in_=dup[:, :, :], op=ALU.add, axis=AX.X))
                ch.link(v.tensor_scalar(first[:, :], first[:, :], 0.5, None, ALU.is_lt))
                ch.link(v.scalar_tensor_tensor(out=to_f[:, :], in0=scol[:, :], scalar=k.trash[:, 0:1], in1=first[:, :],
                                               op0=ALU.subtract, op1=ALU.mult))
                ch.link(v.tensor_scalar(to_f[:, :], to_f[:, :], k.trash[:, 0:1], None, ALU.add))
                v.wait_ge(landed, i * 2 + (q + 2))
                v.tensor_copy(to[q][:, :], to_f[:, :]).then_inc(to_ready, 1)
                if not (final and q == 1):
                    fill(i, q + 1, i * 2 + (q + 1))

            with v.Fori(0, TURNS - 1) as i:
                ch.loop(i, 2 * (2 * NB + 3 + FILL_STEPS))
                for q in range(2):
                    chunk(i, q, False)
            ch.end(TURNS - 1)
            for q in range(2):
                chunk(TURNS - 1, q, True)

        @block.scalar
        def _(act):
            with act.Fori(0, TURNS) as i:
                for q in range(2):
                    act.wait_ge(landed, i * 2 + q + 2)
                    for b in range(NB):
                        n = i * (2 * NB) + (q * NB + b + 1 + NB)
                        act.wait_ge(sum_ready, n)
                        act.activation(sums[q][:, 4 * b:4 * b + 4, :], sps[(q * NB + b) % 2][:, :].rearrange("p (j c) -> p j c", c=D), ACT.Copy).then_inc(sum_out, 1)

        @block.tensor
        def _(pe):
            pe.wait_ge(dve_step, 2)
            with pe.Fori(0, TURNS) as i:
                for q in range(2):
                    pe.wait_ge(srow_in[q], i * 16 + 16)
                    pe.wait_ge(attr_in[q], i * 16 + 16)

                    def fill(b):
                        z = (q * NB + b) % 2
                        c = slice(b * 512, (b + 1) * 512)
                        lo = (q * NB + b - 1 + NB) if q * NB + b >= 2 else NB
                        pe.wait_ge(same_ready, i * (2 * NB) + lo)
                        pe.matmul(bps[z][:, :], k.ones_bf[0:2, :], srow[q][:, c], start=True, stop=True).then_inc(b_ready, 1)
                        pe.wait_ge(msg_ready, i * (2 * NB) + lo)
                        for j in range(4):
                            mm = pe.matmul(vps[z][:, j * P:(j + 1) * P], attr[q][0:65, (4 * b + j) * P:(4 * b + j + 1) * P], k.we[0:65, :], start=True, stop=True)
                        mm.then_inc(v_ready, 1)

                    fill(0)
                    for b in range(NB):
                        if b + 1 < NB:
                            fill(b + 1)
                        n = i * (2 * NB) + (q * NB + b + 1 + NB)
                        z = (q * NB + b) % 2
                        pe.wait_ge(msg_ready, n)
                        pe.wait_ge(same_ready, n)
                        lo = (q * NB + b - 1 + NB) if q * NB + b >= 2 else NB
                        pe.wait_ge(sum_out, i * (2 * NB) + lo)
                        for j in range(4):
                            mm = pe.matmul(sps[z][:, j * D:(j + 1) * D], same[z][:, j, :], F[q][:, 4 * b + j, 0:D], start=True, stop=True)
                        mm.then_inc(sum_ready, 1)


def ring(t, n, j=None):
    lo = n % 4 * 512
    return t[:, lo:lo + 512] if j is None else t[:, lo + j * D:lo + (j + 1) * D]


def seam_phase(nc, k, a, layer):
    SOFT = layer in (0, 3)
    W = {0: 136, 2: 128, 3: 136}[layer]
    rows = {0: k.rows0, 2: k.rows2, 3: k.rows0}[layer]
    with Phase(nc, f"s{layer}") as ph:
        row = ph.sb("row", [P, W])
        ps = ph.ps("ps", [P, 512])
        last = k.last
        row_in, row_out, fixed = ph.sem("row_in"), ph.sem("row_out"), ph.sem("fixed")
        dve_step, pe_step, act_step = ph.sem("dve_step"), ph.sem("pe_step"), ph.sem("act_step")
        if SOFT:
            dg = ph.sb("dg", [P, HEADS, P])
            am = ph.sb("am", [P, HEADS, P])
            ngm = ph.sb("ngm", [P, P])
            cm = ph.sb("cm", [P, HEADS])
            wt = ph.sb("wt", [P, HEADS, P])
            ex = ph.sb("ex", [P, 2, HEADS])
            mm = ph.sb("mm", [P, HEADS])
            ps2 = ph.ps("ps2", [P, 512])
        waited = ph.sem("waited")
        block = ph.block()

        @block.gpsimd
        def _(pool):
            pool.indirect_dma_start(row[:, :], None, rows, bass.IndirectOffsetOnAxis(ap=k.seam_row[:, 0:1], axis=0)).then_inc(row_in, 16)
            pool.wait_ge(fixed, 1)
            pool.indirect_dma_start(rows, bass.IndirectOffsetOnAxis(ap=k.seam_row[:, 0:1], axis=0), row[:, :], None).then_inc(row_out, 16)
            pool.wait_ge(row_out, 16)

        if not SOFT:
            @block.tensor
            def _(pe):
                pe.matmul(ps[:, 0:W], k.seam[:, :], last[:, 0:W], start=True, stop=True).then_inc(pe_step, 1)

            @block.vector
            def _(v):
                v.wait_ge(pe_step, 1)
                v.wait_ge(row_in, 16)
                v.tensor_tensor(row[:, :], row[:, :], ps[:, 0:W], ALU.add).then_inc(fixed, 1)
            return

        @block.tensor
        def _(pe):
            pe.wait_ge(dve_step, 4)
            pe.matmul(ps[:, :], k.ones[:, :], dg[:, :, :].rearrange("p h q -> p (h q)"), start=True, stop=True).then_inc(pe_step, 1)
            pe.wait_ge(dve_step, 10)
            for h in range(HEADS):
                t = pe.transpose(ps2[:, h * P:(h + 1) * P], am[:, h, :], k.ident[:, :])
            t.then_inc(pe_step, 1)
            pe.wait_ge(dve_step, 11)
            for h in range(HEADS):
                pe.matmul(ps[:, h * HDIM:(h + 1) * HDIM], wt[:, h, :], last[:, h * HDIM:(h + 1) * HDIM], start=True, stop=True)
                t = pe.matmul(ps[:, D + h:D + h + 1], wt[:, h, :], last[:, D + h:D + h + 1], start=True, stop=True)
            t.then_inc(pe_step, 1)

        @block.scalar
        def _(act):
            act.wait_ge(dve_step, 9)
            act.activation(am[:, :, :], am[:, :, :], ACT.Exp).then_inc(act_step, 1)
            act.wait_ge(dve_step, 14)
            act.activation(ex[:, :, :], ex[:, :, :], ACT.Exp).then_inc(act_step, 1)

        @block.vector
        def _(v):
            ch = Chain(v, dve_step)
            for h in range(HEADS):
                ch.step(v.tensor_scalar(dg[:, h, :], k.ident[:, :], last[:, 132 + h:133 + h], None, ALU.mult))
            ch.link(v.tensor_scalar(ngm[:, :], k.seamT[:, :], -1.0, BIG, ALU.add, ALU.mult))
            v.wait_ge(pe_step, 1)
            ch.link(v.tensor_tensor(am[:, :, :], ps[:, :].rearrange("p (h q) -> p h q", h=HEADS), bc_mid(ngm[:, :], HEADS), ALU.add))
            ch.link(v.tensor_reduce(out=cm[:, :], in_=am[:, :, :], op=ALU.max, axis=AX.X))
            ch.link(v.tensor_tensor(am[:, :, :], am[:, :, :], bc_last(cm[:, :], P), ALU.subtract))
            ch.link(v.tensor_scalar(am[:, :, :], am[:, :, :], 0.0, None, ALU.min))
            v.wait_ge(act_step, 1)
            ch.link(v.tensor_tensor(am[:, :, :], am[:, :, :], bc_mid(k.seamT[:, :], HEADS), ALU.mult))
            v.wait_ge(pe_step, 2)
            ch.link(v.tensor_copy(wt[:, :, :], ps2[:, :].rearrange("p (h q) -> p h q", h=HEADS)))
            v.wait_ge(row_in, 16)
            ch.link(v.tensor_tensor(mm[:, :], row[:, 132:136], cm[:, :], ALU.max))
            ch.step(v.tensor_tensor(ex[:, 0, :], row[:, 132:136], mm[:, :], ALU.subtract))
            ch.link(v.tensor_tensor(ex[:, 1, :], cm[:, :], mm[:, :], ALU.subtract))
            v.wait_ge(act_step, 2)
            v.wait_ge(pe_step, 3)
            ch.step(v.tensor_copy(row[:, 132:136], mm[:, :]))
            ch.step(v.tensor_tensor(row[:, 0:D].rearrange("p (h c) -> p h c", h=HEADS), row[:, 0:D].rearrange("p (h c) -> p h c", h=HEADS),
                                    bc_last(ex[:, 0, :], HDIM), ALU.mult))
            ch.step(v.tensor_tensor(row[:, D:132], row[:, D:132], ex[:, 0, :], ALU.mult))
            ch.step(v.tensor_tensor(dg[:, 0, :].rearrange("p (h c) -> p h c", h=HEADS), ps[:, 0:D].rearrange("p (h c) -> p h c", h=HEADS),
                                    bc_last(ex[:, 1, :], HDIM), ALU.mult))
            ch.link(v.tensor_tensor(dg[:, 1, 0:HEADS], ps[:, D:132], ex[:, 1, :], ALU.mult))
            ch.link(v.tensor_tensor(row[:, 0:D], row[:, 0:D], dg[:, 0, :], ALU.add))
            v.tensor_tensor(row[:, D:132], row[:, D:132], dg[:, 1, 0:HEADS], ALU.add).then_inc(fixed, 1)


def fill_phase(nc, k):
    S = k.S
    with Phase(nc, "fill") as ph:
        z = ph.sb("z", [P, S, HEADS])
        z_in, first_in, filled = ph.sem("z_in"), ph.sem("first_in"), ph.sem("filled")
        block = ph.block()

        @block.sync
        def _(sp):
            sp.dma_start(z[:, :, :], k.starts[0:k.EP, :].rearrange("(p s) c -> p s c", s=S)).then_inc(z_in, 16)

        @block.gpsimd
        def _(pool):
            pool.wait_ge(z_in, 16)
            pool.indirect_dma_start(z[:, 0, :], None, k.ar_tab, bass.IndirectOffsetOnAxis(ap=k.first_dst[:, 0:1], axis=0)).then_inc(first_in, 16)

        @block.vector
        def _(v):
            v.wait_ge(first_in, 16)
            for h in range(HEADS):
                v.tensor_tensor_scan(out=k.AR[:, h, :], data0=k.keep[:, 0:S], data1=z[:, :, h], initial=0.0,
                                     op0=ALU.mult, op1=ALU.add).then_inc(filled, 1)


def gnn_program(nc, a):
    k = Ctx()
    k.EP = a["dst"].shape[0] * a["dst"].shape[1]
    k.S = a["dst"].shape[1]
    k.NT = a["x"].shape[0] // P
    k.NG = k.NT // GT
    k.PIECES = k.S // (2 * JC)
    k.TURNS = k.S // (BUFS * JC)
    NP = P * k.NT

    def dram(name, shape, dt=FP):
        return nc.dram_tensor(name, shape, dt, kind="Internal").ap()

    k.tab0s, k.tab0d, k.tab1 = (dram(n, (NP, 132)) for n in ("tab0s", "tab0d", "tab1"))
    k.tab2 = dram("tab2", (NP, D))
    k.spread = dram("spread", (k.EP + NP, 132))
    k.tab3, k.ar_tab = dram("tab3", (NP, 132)), dram("ar_tab", (NP, HEADS))
    k.rows0, k.rows2 = dram("rows0", (k.EP + 1, 136)), dram("rows2", (k.EP + 1, D))
    k.by_src = [dram(f"by_src{t}", (NP + P, D)) for t in range(SUMS)]
    k.src_parts = dram("src_parts", (2, k.EP), BF)
    k.starts = dram("starts", (k.EP + NP, HEADS))
    k.counts = dram("counts", (1, NP + 1))
    with ExitStack() as st:
        def sb(n, shape, dt=FP):
            return st.enter_context(nc.sbuf_tensor(n, shape, dt))

        k.X = sb("X", [P, k.NT, D])
        k.keep, k.cut = sb("keep", [P, k.S + 1]), sb("cut", [P, k.S])
        k.ident, k.ones, k.seam, k.seamT = (sb(n, [P, P]) for n in ("ident", "ones", "seam", "seamT"))
        k.node, k.deg = sb("node", [P, k.NT]), sb("deg", [P, k.NT])
        k.end_row, k.start_row = sb("end_row", [P, k.NT], I32), sb("start_row", [P, k.NT], I32)
        k.cont, k.attn_cols, k.attn02 = sb("cont", [P, 1]), sb("attn_cols", [P, HEADS]), sb("attn02", [P, D])
        k.seam_row, k.first_dst = sb("seam_row", [P, 1], I32), sb("first_dst", [P, 1], I32)
        k.sself = sb("sself", [P, k.NT, HEADS])
        k.last = sb("last", [P, 136])
        k.trash, k.before = sb("trash", [P, 1]), sb("before", [P, P])
        k.w0, k.b0, k.attn = sb("w0", [P, 2 * D]), sb("b0", [P, 2 * D]), sb("attn", [P, D])
        k.ones_bf = sb("ones_bf", [3, P], BF)
        k.w1, k.b1, k.we = sb("w1", [P, D]), sb("b1", [P, D]), sb("we", [65, D])
        k.fw1, k.fw2, k.fb2 = sb("fw1", [51, D]), sb("fw2", [P, D]), sb("fb2", [3, 4 * D], BF)
        k.pw, k.pb, k.mw1, k.mw2, k.mb2 = (sb(n, [P, D]) for n in ("pw", "pb", "mw1", "mw2", "mb2"))
        k.mb1, k.rbf_bias, k.rbf_scale = sb("mb1", [P, 1]), sb("rbf_bias", [51, 1]), sb("rbf_scale", [51, 1])
        k.w3, k.wet, k.lns, k.lnb = sb("w3", [P, 136]), sb("wet", [16, HEADS]), sb("lns", [P, D]), sb("lnb", [P, D])

        with (nc.sbuf_tensor("zero_rows", [P, JC * 132], FP) as k.zero_rows, nc.semaphore("spread_cleared") as k.spread_cleared,
              nc.sbuf_tensor("coarse_i", [P, a["dst_blocks"].shape[0]], I32) as k.coarse_i):
            setup_phase(nc, k, a)
            ends_phase(nc, k, a)
            node_phase(nc, k, a, None, 0)
        for layer in range(3):
            if layer == 1:
                scatter_phase(nc, k, a)
            else:
                edge_phase(nc, k, a, layer)
                seam_phase(nc, k, a, layer)
            node_phase(nc, k, a, layer, layer + 1)
        k.AR = sb("AR", [P, HEADS, k.S])
        fill_phase(nc, k)
        edge_phase(nc, k, a, 3)
        seam_phase(nc, k, a, 3)
        node_phase(nc, k, a, 3, None)




def kernel(**inputs):
    import numpy as np
    import concourse.bacc as _bacc
    from concourse import mybir as _mybir
    from concourse.bass_utils import run_bass_kernel_spmd as _run

    x, src, dst = (np.asarray(inputs[n]) for n in ("x", "src", "dst"))
    N, E = x.shape[0], src.shape[0]
    per = P * BUFS * JC
    EP = -(-E // per) * per
    S = EP // P
    NP = -(-N // (P * GT)) * P * GT
    pad_e = EP - E

    def padded(v, n, fill=0):
        v = np.asarray(v)
        return np.concatenate([v, np.full((n,) + v.shape[1:], fill, v.dtype)])

    arrays = {"x": padded(x, NP - N)}
    src_p = padded(src, pad_e, NP - 1).reshape(P, S)
    dst_p = padded(dst, pad_e, NP - 1)
    arrays["dst"] = dst_p.reshape(P, S)
    arrays["src"] = src_p
    arrays["dst_last"] = dst_p.reshape(P, S)[:, -1].reshape(1, P)
    block = min(b for b in range(1, EP + 1) if EP % b == 0 and b * b >= EP)
    arrays["dst_blocks"] = dst_p.reshape(-1, block)
    arrays["dst_coarse"] = dst_p[::block].reshape(1, -1)
    ew = padded(inputs["edge_weight"], pad_e).reshape(P, S)
    arrays["edge_weight"] = ew
    arrays["dist_T"] = ew.T.reshape(1, EP)
    arrays["src_T"] = src_p.T.reshape(1, EP)
    e64 = padded(inputs["edge_attr_64"], pad_e).reshape(P, S, 64)
    arrays["edge_attr_64_T"] = e64.transpose(2, 1, 0).reshape(64, EP)
    ea = padded(inputs["edge_attr_16"], pad_e).reshape(P, S, 16)
    arrays["edge_attr_16_T"] = ea.transpose(2, 1, 0).reshape(16, EP)
    for n in sorted(inputs):
        if n.startswith("L"):
            v = np.asarray(inputs[n])
            arrays[n] = v.reshape(1, -1) if v.ndim == 1 else v
    arrays["L3_gnn_W_T"] = np.asarray(inputs["L3_gnn_W"]).T
    arrays["L3_gnn_W_e_T"] = np.asarray(inputs["L3_gnn_W_e"]).T

    nc = _bacc.Bacc("TRN2", target_bir_lowering=False, num_devices=1)
    feed, a = {}, {}
    for n, v in arrays.items():
        v = np.ascontiguousarray(v)
        feed[f"in_{n}"] = v
        a[n] = nc.dram_tensor(f"in_{n}", v.shape, _mybir.dt.from_np(v.dtype), kind="ExternalInput").ap()
    a["out"] = nc.dram_tensor("out_0", (NP, D), _mybir.dt.float32, kind="ExternalOutput").ap()
    gnn_program(nc, a)
    r = _run(nc, [feed], core_ids=[0])
    return r.results[0]["out_0"][:N]
```

```python
import concourse.bass as bass
from concourse import mybir
from contextlib import ExitStack

P = 128
HEADS, HDIM = 4, 32
D = HEADS * HDIM
JC = 28
BUFS = 4
GT = 7
SUMS = 7
BIG = 1.0e38
EPS = 1e-5
PI = 3.141592653589793
FP = mybir.dt.float32
BF = mybir.dt.bfloat16
I32 = mybir.dt.int32
ALU = mybir.AluOpType
ACT = mybir.ActivationFunctionType
AX = mybir.AxisListType


class Chain:

    def __init__(self, eng, sem):
        self.eng, self.sem, self.base, self.n = eng, sem, 0, 0

    def loop(self, i, per_turn):
        self.start = self.base + self.n
        self.base = i * per_turn + self.start
        self.n = 0
        self.per_turn = per_turn

    def end(self, turns):
        assert self.n == self.per_turn, (self.n, self.per_turn)
        self.base, self.n = self.start + turns * self.per_turn, 0

    def step(self, ins):
        ins.then_inc(self.sem, 1)
        self.n += 1

    def link(self, ins):
        self.step(ins)
        self.eng.wait_ge(self.sem, self.base + self.n)


class Ctx:
    pass


def bc_mid(ap, n):
    return ap.unsqueeze(1).to_broadcast([ap.shape[0], n, ap.shape[1]])


def bc_last(ap, n):
    return ap.unsqueeze(len(ap.shape)).to_broadcast(list(ap.shape) + [n])


class Phase:

    def __init__(self, nc, name):
        self.nc, self.name, self.stack, self.sems, self.credits = nc, name, ExitStack(), [], []

    def __enter__(self):
        self.stack.__enter__()
        return self

    def __exit__(self, *a):
        self.stack.__exit__(*a)
        if a[0] is None:
            self.nc.clear_and_free_semaphores(self.sems)
            self.nc.all_engine_barrier()

    def sb(self, n, shape, dt=FP):
        return self.stack.enter_context(self.nc.sbuf_tensor(f"{self.name}_{n}", shape, dt))

    def ps(self, n, shape):
        return self.stack.enter_context(self.nc.psum_tensor(f"{self.name}_{n}", shape, FP))

    def sem(self, n, credit=0):
        self.sems.append(self.nc.alloc_semaphore(f"{self.name}_{n}"))
        if credit:
            self.credits.append((self.sems[-1], credit))
        return self.sems[-1]

    def give_credits(self, sp):
        for sem, credit in self.credits:
            sp.sem_inc(sem, credit)

    def block(self):
        return self.stack.enter_context(self.nc.Block())




def setup_phase(nc, k, a):
    S, NT = k.S, k.NT
    with Phase(nc, "setup") as ph:
        dst_i = ph.sb("dst_i", [P, S], I32)
        dst_f = ph.sb("dst_f", [P, S])
        lastd_i = ph.sb("lastd_i", [P, P], I32)
        lastd_f = ph.sb("lastd_f", [P, P])
        col = ph.sb("col", [P, P])
        part = ph.sb("part", [P, 1])
        eqf = ph.sb("eqf", [P, S])
        cnt = ph.sb("cnt", [P, 1])
        rowf = ph.sb("rowf", [P, 1])
        mlow = ph.sb("mlow", [P, P])
        seam_ps = ph.ps("seam_ps", [P, 512])
        w3_ps = ph.ps("w3_ps", [P, 512])
        zrow = ph.sb("zrow", [1, 192])
        wfull = ph.sb("wfull", [P, D])
        acol = ph.sb("acol", [P, 8])
        dist = ph.sb("dist", [P, S])
        dgt = ph.sb("dgt", [P, S])
        srcT_i = ph.sb("srcT_i", [P, S], I32)
        srcT = ph.sb("srcT", [P, S])
        src_hi, src_lo = ph.sb("src_hi", [P, S], BF), ph.sb("src_lo", [P, S], BF)
        fb, fb_sum = ph.sb("fb", [3, 4 * D]), ph.sb("fb_sum", [3, 4 * D])
        fb_part = ph.sb("fb_part", [3, 4 * D], BF)
        pick = ph.sb("pick", [P, 3])

        dma_in = ph.sem("dma_in")
        acol_zero = ph.sem("acol_zero")
        acol_in = ph.sem("acol_in")
        pool_step = ph.sem("pool_step")
        dve_step = ph.sem("dve_step")
        pe_step = ph.sem("pe_step")
        seamT_ready = ph.sem("seamT_ready")
        cut_arg = ph.sem("cut_arg")
        cut_cos = ph.sem("cut_cos")
        attn_in = ph.sem("attn_in")
        src_split = ph.sem("src_split")
        src_out = ph.sem("src_out")
        zero_ready = ph.sem("zero_ready")
        zero_out = ph.sem("zero_out")
        block = ph.block()
        loads = [
            (dst_i[:, :], a["dst"]), (lastd_i[:, :], a["dst_last"].to_broadcast([P, P])),
            (k.X[:, :, :], a["x"].rearrange("(p t) c -> p t c", t=NT)),
            (k.w0[:, 0:D], a["L0_gnn_W_src"]), (k.w0[:, D:2 * D], a["L0_gnn_W_dst"]),
            (k.b0[:, 0:D], a["L0_gnn_b_src"].to_broadcast([P, D])),
            (k.b0[:, D:2 * D], a["L0_gnn_b_dst"].to_broadcast([P, D])),
            (k.attn[:, :], a["L0_gnn_attn"].rearrange("h d -> (h d)").unsqueeze(0).to_broadcast([P, D])),
            (k.w1[:, :], a["L1_gnn_W_lin"]), (k.b1[:, :], a["L1_gnn_b_lin"].to_broadcast([P, D])),
            (k.we[0:64, :], a["L1_gnn_W_edge"]), (k.we[64:65, :], a["L1_gnn_b_edge"]),
            (k.fw1[0:50, :], a["L2_gnn_fw1"]), (k.fw1[50:51, :], a["L2_gnn_fb1"]),
            (k.fw2[:, :], a["L2_gnn_fw2"]),
            (k.pw[:, :], a["L2_gnn_pw"]), (k.pb[:, :], a["L2_gnn_pb"].to_broadcast([P, D])),
            (k.mw1[:, :], a["L2_gnn_mw1"]), (k.mb1[:, :], a["L2_gnn_mb1"].rearrange("o c -> c o")),
            (k.mw2[:, :], a["L2_gnn_mw2"]), (k.mb2[:, :], a["L2_gnn_mb2"].to_broadcast([P, D])),
            (k.w3[:, 0:D], a["L3_gnn_W_T"]), (wfull[:, :], a["L3_gnn_W"]),
            (k.wet[:, :], a["L3_gnn_W_e_T"]),
            (k.lns[:, :], a["L3_gnn_ln_scale"].to_broadcast([P, D])),
            (k.lnb[:, :], a["L3_gnn_ln_bias"].to_broadcast([P, D])),
            (dist[:, :], a["edge_weight"]), (srcT_i[:, :], a["src_T"].rearrange("o (p s) -> (o p) s", s=S)),
            (k.coarse_i[:, :], a["dst_coarse"].to_broadcast([P, a["dst_coarse"].shape[1]])),
        ] + [(fb[:, j * D:(j + 1) * D], a["L2_gnn_fb2"].to_broadcast([3, D])) for j in range(4)]

        @block.sync
        def _(sp):
            ph.give_credits(sp)
            with nc.allow_non_contiguous_dma(reason="a bias column"):
                for out, in_ in loads:
                    sp.dma_start(out, in_).then_inc(dma_in, 16)
            sp.wait_ge(acol_zero, 1)
            with nc.allow_non_contiguous_dma(reason="the attention vectors as columns"):
                for h in range(HEADS):
                    sp.dma_start(k.attn_cols[h * HDIM:(h + 1) * HDIM, h:h + 1], a["L0_gnn_attn"][h:h + 1, :].rearrange("o c -> c o")).then_inc(attn_in, 16)
                    for half in range(2):
                        sp.dma_start(acol[h * HDIM:(h + 1) * HDIM, half * 4 + h:half * 4 + h + 1],
                                     a["L3_gnn_a"][h:h + 1, half * HDIM:(half + 1) * HDIM]
                                     .rearrange("o c -> c o")).then_inc(acol_in, 16)
            sp.wait_ge(zero_ready, 1)
            sp.dma_start(k.rows0[k.EP:k.EP + 1, :], zrow[0:1, 0:136]).then_inc(zero_out, 16)
            sp.dma_start(k.rows2[k.EP:k.EP + 1, :], zrow[0:1, 0:128]).then_inc(zero_out, 16)
            sp.wait_ge(zero_out, 32)
            sp.wait_ge(attn_in, 16 * HEADS)
            sp.wait_ge(src_split, 2)
            for n, t in enumerate((src_hi, src_lo)):
                sp.dma_start(k.src_parts[n:n + 1, :].rearrange("o (p s) -> (o p) s", s=S), t[:, :]).then_inc(src_out, 16)
            sp.wait_ge(src_out, 32)

        @block.gpsimd
        def _(pool):
            ch = Chain(pool, pool_step)
            ch.link(pool.memset(k.ident[:, :], 0.0))
            ch.step(pool.affine_select(out=k.ident[:, :], in_=k.ident[:, :], compare_op=ALU.not_equal, fill=1.0,
                                       base=0, pattern=[[-1, P]], channel_multiplier=1))
            ch.step(pool.iota(col[:, :], pattern=[[1, P]], base=0, channel_multiplier=0,
                              allow_small_or_imprecise_dtypes=True))
            ch.step(pool.iota(part[:, :], pattern=[[0, 1]], base=0, channel_multiplier=1,
                              allow_small_or_imprecise_dtypes=True))
            ch.step(pool.iota(rowf[:, :], pattern=[[0, 1]], base=0, channel_multiplier=S,
                              allow_small_or_imprecise_dtypes=True))
            ch.step(pool.iota(k.node[:, :], pattern=[[1, NT]], base=0, channel_multiplier=NT,
                              allow_small_or_imprecise_dtypes=True))

        @block.vector
        def _(v):
            ch = Chain(v, dve_step)
            ch.step(v.memset(k.zero_rows[:, :], 0.0))
            ch.link(v.memset(k.attn_cols[:, :], 0.0))
            v.memset(acol[:, :], 0.0).then_inc(acol_zero, 1)
            ch.step(v.memset(k.ones[:, :], 1.0))
            ch.link(v.memset(zrow[:, :], 0.0))
            v.memset(zrow[:, 132:136], -BIG).then_inc(zero_ready, 1)
            v.wait_ge(dma_in, 16 * len(loads))
            v.wait_ge(pool_step, 6)
            ch.step(v.tensor_scalar(k.attn02[:, :], k.attn[:, :], 0.2, None, ALU.mult))
            ch.link(v.scalar_tensor_tensor(out=dgt[:, :], in0=dist[:, :], scalar=-1.0, in1=dist[:, :], op0=ALU.mult, op1=ALU.max))
            ch.link(v.tensor_scalar(dgt[:, :], dgt[:, :], 10.0, -PI / 10.0, ALU.min, ALU.mult))
            ch.link(v.tensor_scalar(dgt[:, :], dgt[:, :], PI / 2, None, ALU.add))
            v.tensor_scalar(dist[:, :], dist[:, :], 10.0, 0.5, ALU.is_le, ALU.mult).then_inc(cut_arg, 1)
            ch.link(v.tensor_scalar(k.rbf_bias[0:51, :], part[0:51, :], -10.0 / 49.0, None, ALU.mult))
            ch.link(v.tensor_scalar(k.rbf_scale[0:51, :], part[0:51, :], 49.5, None, ALU.is_lt))
            ch.link(v.tensor_tensor(k.rbf_bias[0:51, :], k.rbf_bias[0:51, :], k.rbf_scale[0:51, :], ALU.mult))
            ch.link(v.tensor_copy(dst_f[:, :], dst_i[:, :]))
            ch.step(v.memset(k.keep[:, 0:1], 1.0))
            ch.step(v.memset(k.keep[:, S:S + 1], 0.0))
            ch.link(v.tensor_tensor(k.keep[:, 1:S], dst_f[:, 1:S], dst_f[:, 0:S - 1], ALU.is_equal))
            ch.link(v.tensor_tensor(eqf[:, :], dst_f[:, :], dst_f[:, 0:1].to_broadcast([P, S]), ALU.is_equal))
            ch.link(v.tensor_reduce(out=cnt[:, :], in_=eqf[:, :], op=ALU.add, axis=AX.X))
            ch.link(v.scalar_tensor_tensor(out=cnt[:, :], in0=cnt[:, :], scalar=-1.0, in1=rowf[:, :],
                                           op0=ALU.add, op1=ALU.add))
            ch.link(v.tensor_copy(k.seam_row[:, :], cnt[:, :]))
            ch.link(v.tensor_copy(k.first_dst[:, :], dst_i[:, 0:1]))
            ch.link(v.tensor_copy(lastd_f[:, :], lastd_i[:, :]))
            ch.link(v.tensor_scalar(mlow[:, :], col[:, :], part[:, 0:1], None, ALU.is_lt))
            v.scalar_tensor_tensor(out=k.seamT[:, :], in0=lastd_f[:, :], scalar=dst_f[:, 0:1],
                                   in1=mlow[:, :], op0=ALU.is_equal, op1=ALU.mult).then_inc(seamT_ready, 1)
            v.wait_ge(seamT_ready, 1)
            ch.step(v.tensor_reduce(out=k.cont[:, :], in_=k.seamT[:, :], op=ALU.max, axis=AX.X))
            ch.step(v.tensor_copy(k.before[:, :], mlow[:, :]))
            ch.link(v.tensor_scalar(k.trash[:, :], part[:, :], float(P * NT), None, ALU.add))
            ch.link(v.tensor_copy(srcT[:, :], srcT_i[:, :]))
            v.tensor_copy(src_hi[:, :], srcT[:, :]).then_inc(src_split, 1)
            v.wait_ge(src_split, 1)
            v.tensor_tensor(src_lo[:, :], srcT[:, :], src_hi[:, :], ALU.subtract).then_inc(src_split, 1)
            for i in range(3):
                ch.step(v.tensor_scalar(pick[:, i:i + 1], part[:, :], float(i), None, ALU.is_equal))
            ch.step(v.memset(k.ones_bf[:, :], 1.0))
            ch.link(v.memset(fb_sum[:, :], 0.0))
            for i in range(3):
                ch.link(v.tensor_copy(fb_part[:, :], fb[:, :]))
                ch.link(v.scalar_tensor_tensor(out=fb_sum[:, :], in0=fb_part[:, :], scalar=pick[0:3, i:i + 1], in1=fb_sum[:, :], op0=ALU.mult, op1=ALU.add))
                ch.link(v.tensor_tensor(fb[:, :], fb[:, :], fb_part[:, :], ALU.subtract))
            ch.step(v.tensor_copy(k.fb2[:, :], fb_sum[:, :]))
            v.wait_ge(pe_step, 1)
            ch.link(v.tensor_copy(k.seam[:, :], seam_ps[:, 0:P]))
            v.wait_ge(pe_step, 2)
            ch.link(v.tensor_copy(k.w3[:, D:D + 8], w3_ps[:, 0:8]))
            v.wait_ge(cut_cos, 1)
            ch.link(v.scalar_tensor_tensor(out=k.cut[:, :], in0=dgt[:, :], scalar=1.0, in1=dist[:, :],
                                           op0=ALU.add, op1=ALU.mult))

        @block.scalar
        def _(act):
            act.wait_ge(cut_arg, 1)
            act.activation(dgt[:, :], dgt[:, :], ACT.Sin).then_inc(cut_cos, 1)

        @block.tensor
        def _(pe):
            pe.wait_ge(pool_step, 6)
            pe.wait_ge(seamT_ready, 1)
            pe.transpose(seam_ps[:, 0:P], k.seamT[:, :], k.ident[:, :]).then_inc(pe_step, 1)
            pe.wait_ge(dma_in, 16 * len(loads))
            pe.wait_ge(acol_in, 128)
            pe.matmul(w3_ps[:, 0:8], wfull[:, :], acol[:, :], start=True, stop=True).then_inc(pe_step, 1)


def clear_spread(act, k, n, cleared):
    w = k.S // (4 * k.NG)
    v = k.spread[0:k.EP, :].rearrange("(p s) c -> p (s c)", p=P)
    for piece in range(2):
        act.dma_start(v[:, bass.ds((n * 2 + piece) * (w * 132), w * 132)], k.zero_rows[:, 0:w * 132]).then_inc(cleared, 16)


def ends_phase(nc, k, a):
    NT, NG = k.NT, k.NG
    BN, BW = a["dst_blocks"].shape
    with Phase(nc, "ends") as ph:
        coarse = ph.sb("coarse", [P, BN])
        below = ph.sb("below", [P, GT, BN])
        bg, cg = ph.sb("bg", [P, GT]), ph.sb("cg", [P, GT])
        blk = ph.sb("blk", [P, NT])
        blk_i = ph.sb("blk_i", [P, NT], I32)
        bidx = [ph.sb(f"bidx{q}", [P, GT], I32) for q in range(2)]
        fine_i = [ph.sb(f"fine_i{q}", [P, GT, BW], I32) for q in range(2)]
        le = ph.sb("le", [P, GT, BW])
        c2 = ph.sb("c2", [P, NT])
        cnt = ph.sb("cnt", [P, NT])
        prev = ph.sb("prev", [P, NT])
        has = ph.sb("has", [P, NT])
        tmp = ph.sb("tmp", [P, NT])
        zero1 = ph.sb("zero1", [1, 1])
        arg = [ph.sb(f"arg{q}", [P, GT, 132]) for q in range(2)]
        sidx = [ph.sb(f"sidx{q}", [P, GT], I32) for q in range(2)]
        cleared, starts_ready, sidx_ready = ph.sem("cleared"), ph.sem("starts_ready"), ph.sem("sidx_ready")
        arg_in, sent = ([ph.sem(f"{n}{q}") for q in range(2)] for n in ("arg_in", "sent"))
        dve_step = ph.sem("dve_step")
        blocks_found = ph.sem("blocks_found")
        bidx_ready = ph.sem("bidx_ready")
        fine_in = [ph.sem(f"fine_in{q}") for q in range(2)]
        fine_used = [ph.sem(f"fine_used{q}", credit=1) for q in range(2)]
        cnt_ready = ph.sem("cnt_ready")
        cnt_out = ph.sem("cnt_out")
        prev_in = ph.sem("prev_in")
        waited, waited_act, waited_sp = ph.sem("waited"), ph.sem("waited_act"), ph.sem("waited_sp")
        block = ph.block()

        @block.sync
        def _(sp):
            ph.give_credits(sp)

            def load(i, q):
                sp.dma_start(arg[q][:, :, :], k.tab0d.rearrange("(p t) c -> p t c", t=NT)[:, bass.ds((i * 2 + q) * GT, GT), :]).then_inc(arg_in[q], 16)

            for q in range(2):
                load(0, q)
            sp.wait_ge(cnt_ready, 1)
            sp.dma_start(k.counts[0:1, 0:1], zero1[:, :]).then_inc(cnt_out, 16)
            sp.dma_start(k.counts[0:1, 1:1 + P * NT].rearrange("o (p t) -> (o p) t", t=NT), cnt[:, :]).then_inc(cnt_out, 16)
            sp.wait_ge(cnt_out, 32)
            sp.dma_start(prev[:, :], k.counts[0:1, 0:P * NT].rearrange("o (p t) -> (o p) t", t=NT)).then_inc(prev_in, 16)
            if NG > 2:
                with sp.Fori(1, NG // 2) as i:
                    for q in range(2):
                        sp.wait_ge(sent[q], i * (16 * GT))
                        sp.sem_inc(waited_sp, 1)
                        load(i, q)

        @block.gpsimd
        def _(pool):
            with pool.Fori(0, NG // 2) as i:
                for q in range(2):
                    pool.wait_ge(blocks_found, i * 2 + (q + 1))
                    pool.wait_ge(fine_used[q], i + 1)
                    pool.tensor_copy(bidx[q][:, :], blk_i[:, bass.ds((i * 2 + q) * GT, GT)]).then_inc(bidx_ready, 1)
                    pool.wait_ge(bidx_ready, i * 2 + (q + 1))
                    pool.sem_inc(waited, 1)
                    for t in range(GT):
                        pool.indirect_dma_start(fine_i[q][:, t, :], None, a["dst_blocks"],
                                                bass.IndirectOffsetOnAxis(ap=bidx[q][:, t:t + 1], axis=0)).then_inc(fine_in[q], 16)

            def send(i, q):
                pool.tensor_copy(sidx[q][:, :], k.start_row[:, bass.ds((i * 2 + q) * GT, GT)]).then_inc(sidx_ready, 1)
                pool.wait_ge(sidx_ready, i * 2 + (q + 1))
                pool.wait_ge(arg_in[q], i * 16 + 16)
                pool.sem_inc(waited, 1)
                for t in range(GT):
                    pool.indirect_dma_start(k.spread, bass.IndirectOffsetOnAxis(ap=sidx[q][:, t:t + 1], axis=0), arg[q][:, t, :], None).then_inc(sent[q], 16)

            pool.wait_ge(starts_ready, 1)
            pool.wait_ge(cleared, 2 * NG * 16)
            for q in range(2):
                send(0, q)
            if NG > 2:
                with pool.Fori(1, NG // 2) as i:
                    for q in range(2):
                        pool.wait_ge(sent[q], i * (16 * GT))
                        send(i, q)
            for q in range(2):
                pool.wait_ge(sent[q], NG // 2 * (16 * GT))

        @block.scalar
        def _(act):
            with act.Fori(0, NG) as g:
                act.wait_ge(blocks_found, g + 1)
                act.sem_inc(waited_act, 1)
                clear_spread(act, k, g + NG, cleared)

        @block.vector
        def _(v):
            ch = Chain(v, dve_step)
            ch.step(v.memset(zero1[:, :], 0.0))
            ch.link(v.tensor_copy(coarse[:, :], k.coarse_i[:, :]))

            def find(g):
                at = bass.ds(g * GT, GT)
                ch.link(v.tensor_tensor(below[:, :, :], bc_mid(coarse[:, :], GT), bc_last(k.node[:, at], BN), ALU.is_le))
                ch.link(v.tensor_reduce(out=bg[:, :], in_=below[:, :, :], op=ALU.add, axis=AX.X))
                ch.link(v.tensor_scalar(bg[:, :], bg[:, :], -1.0, 0.0, ALU.add, ALU.max))
                ch.step(v.tensor_copy(blk[:, at], bg[:, :]))
                v.tensor_copy(blk_i[:, at], bg[:, :]).then_inc(blocks_found, 1)
                v.wait_ge(blocks_found, g + 1)

            def count(i, q):
                at = bass.ds((i * 2 + q) * GT, GT)
                v.wait_ge(fine_in[q], i * (16 * GT) + 16 * GT)
                ch.link(v.tensor_tensor(le[:, :, :], fine_i[q][:, :, :], bc_last(k.node[:, at], BW), ALU.is_le))
                v.tensor_reduce(out=cg[:, :], in_=le[:, :, :], op=ALU.add, axis=AX.X).then_inc(fine_used[q], 1)
                v.wait_ge(fine_used[q], i + 2)
                ch.link(v.tensor_copy(c2[:, at], cg[:, :]))

            for q in range(2):
                find(q)
            if NG > 2:
                with v.Fori(1, NG // 2) as i:
                    ch.loop(i - 1, 12)
                    for q in range(2):
                        find(i * 2 + q)
                        count(i - 1, q)
                ch.end(NG // 2 - 1)
            for q in range(2):
                count(NG // 2 - 1, q)
            v.scalar_tensor_tensor(out=cnt[:, :], in0=blk[:, :], scalar=float(BW), in1=c2[:, :],
                                   op0=ALU.mult, op1=ALU.add).then_inc(cnt_ready, 1)
            v.wait_ge(cnt_ready, 1)
            v.wait_ge(prev_in, 16)
            ch.link(v.tensor_tensor(k.deg[:, :], cnt[:, :], prev[:, :], ALU.subtract))
            ch.link(v.tensor_scalar(has[:, :], k.deg[:, :], 0.5, None, ALU.is_gt))
            ch.link(v.tensor_scalar(tmp[:, :], cnt[:, :], -1.0 - k.EP, None, ALU.add))
            ch.link(v.tensor_tensor(tmp[:, :], tmp[:, :], has[:, :], ALU.mult))
            ch.link(v.tensor_scalar(tmp[:, :], tmp[:, :], float(k.EP), None, ALU.add))
            ch.link(v.tensor_copy(k.end_row[:, :], tmp[:, :]))
            ch.link(v.tensor_tensor(tmp[:, :], prev[:, :], k.node[:, :], ALU.subtract))
            ch.link(v.tensor_scalar(tmp[:, :], tmp[:, :], -float(k.EP), None, ALU.add))
            ch.link(v.tensor_tensor(tmp[:, :], tmp[:, :], has[:, :], ALU.mult))
            ch.link(v.tensor_tensor(tmp[:, :], tmp[:, :], k.node[:, :], ALU.add))
            ch.link(v.tensor_scalar(tmp[:, :], tmp[:, :], float(k.EP), None, ALU.add))
            v.tensor_copy(k.start_row[:, :], tmp[:, :]).then_inc(starts_ready, 1)




def two_ahead(eng, n, ahead, behind):
    ahead(0)
    ahead(1)
    if n > 2:
        ahead(2)
    behind(0)
    if n > 3:
        with eng.Fori(1, n - 2) as g:
            ahead(g + 2)
            behind(g)
    for g in range(max(1, n - 2), n):
        behind(g)


def node_phase(nc, k, a, post, pre):
    NT, NG = k.NT, k.NG
    W = {None: 0, 0: 136, 1: 0, 2: 128, 3: 136}[post]
    NC = {0: 256, 1: 128, 2: 128, 3: 136, None: 0}[pre]
    ST = {0: 256, 1: 128, 2: 128, 3: 256, None: 0}[pre]
    rows = {0: k.rows0, 1: None, 2: k.rows2, 3: k.rows0, None: None}[post]
    GW = {0: 136, 1: 0, 2: 128, 3: 136, None: 0}[post]
    TW = {0: 264, 1: 132, 2: 128, 3: 136, None: 0}[pre]
    SPREAD = pre in (1, 3)
    n_out = {0: 32, 1: 16, 2: 16, 3: 32, None: 16}[pre]
    with Phase(nc, f"n{post}{pre}") as ph:
        N3 = [P, GT, D]
        s7, m7, v7, r7 = (ph.sb(x, [P, GT]) for x in ("s7", "m7", "v7", "r7"))
        cen, sq, h = ph.sb("cen", N3), ph.sb("sq", N3), ph.sb("h", N3)
        hT = ph.sb("hT", [P, GT * P])
        psA = ph.ps("psA", [P, 1024])
        psB = ph.ps("psB", [P, 1024])
        psC = ph.ps("psC", [P, 2048])
        if post is not None:
            y = ph.sb("y", N3)
        if post == 1:
            part = ph.sb("part", [P, SUMS, GT, D])
            y2 = ph.sb("y2", N3)
        elif post is not None:
            rg = ph.sb("rg", [P, GT, W])
            gidx = ph.sb("gidx", [P, GT], I32)
        if post == 0:
            fsn = ph.sb("fsn", N3)
            mx = ph.sb("mx", [P, GT, HEADS])
            ex = ph.sb("ex", [P, 2, GT * HEADS])
            den = ph.sb("den", [P, GT * HEADS])
        if post == 3:
            den = ph.sb("den", [P, GT, HEADS])
        if post == 2:
            aT = ph.sb("aT", [P, GT * P])
            uT = ph.sb("uT", [P, GT * P])
        if pre is not None:
            tab = ph.sb("tab", [P, GT, TW])
        if pre == 0:
            cleared = ph.sem("cleared")
        if SPREAD:
            sidx = ph.sb("sidx", [P, GT], I32)
            sidx_ready, sent, tab_sent = ph.sem("sidx_ready"), ph.sem("sent"), ph.sem("tab_sent", credit=1)
        if pre == 0:
            e = ph.sb("e", N3)

        dve_step = ph.sem("dve_step")
        gidx_ready, rows_in, rows_used = ph.sem("gidx_ready"), ph.sem("rows_in"), ph.sem("rows_used", credit=1)
        fsn_in, fsn_used = ph.sem("fsn_in"), ph.sem("fsn_used", credit=1)
        gelu_done = ph.sem("gelu_done")
        ex_arg, ex_done = ph.sem("ex_arg"), ph.sem("ex_done")
        aT_ps, aT_ready, post_mm = ph.sem("aT_ps"), ph.sem("aT_ready"), ph.sem("post_mm")
        z_ps, u_ready, post_used = ph.sem("z_ps"), ph.sem("u_ready"), ph.sem("post_used", credit=1)
        x_done = ph.sem("x_done")
        cen_ready, sq_ready, var_ready, std_ready = ph.sem("cen_ready"), ph.sem("sq_ready"), ph.sem("var_ready"), ph.sem("std_ready")
        h_ready, hT_ps, hT_ready = ph.sem("h_ready"), ph.sem("hT_ps"), ph.sem("hT_ready")
        tab_ps, tab_ready, tab_out = ph.sem("tab_ps"), ph.sem("tab_ready", credit=1), ph.sem("tab_out", credit=n_out)
        waited = ph.sem("waited")
        block = ph.block()
        fs_v = k.tab0s.rearrange("(p t) c -> p t c", t=NT)
        fd_v = k.tab0d.rearrange("(p t) c -> p t c", t=NT)
        t1_v = k.tab1.rearrange("(p t) c -> p t c", t=NT)
        t2_v = k.tab2.rearrange("(p t) c -> p t c", t=NT)
        t3_v = k.tab3.rearrange("(p t) c -> p t c", t=NT)
        ar_v = k.ar_tab.rearrange("(p t) c -> p t c", t=NT)
        out_v = a["out"].rearrange("(p t) c -> p t c", t=NT)

        @block.sync
        def _(sp):
            ph.give_credits(sp)

            def load(g):
                if post == 1:
                    sp.wait_ge(rows_used, g + 1)
                    for t in range(SUMS):
                        sp.dma_start(part[:, t, :, :], k.by_src[t][0:P * NT, :].rearrange("(p t) c -> p t c", t=NT)[:, bass.ds(g * GT, GT), :]).then_inc(rows_in, 16)
                if post == 0:
                    sp.wait_ge(fsn_used, g + 1)
                    sp.dma_start(fsn[:, :, :], fs_v[:, bass.ds(g * GT, GT), 0:D]).then_inc(fsn_in, 16)

            def store(g):
                at = bass.ds(g * GT, GT)
                if pre is not None:
                    sp.wait_ge(tab_ready, g + 2)
                if pre == 0:
                    sp.dma_start(fs_v[:, at, :], tab[:, :, 0:132]).then_inc(tab_out, 16)
                    sp.dma_start(fd_v[:, at, :], tab[:, :, 132:264]).then_inc(tab_out, 16)
                elif pre in (1, 2):
                    sp.dma_start((t1_v if pre == 1 else t2_v)[:, at, :], tab[:, :, :]).then_inc(tab_out, 16)
                elif pre == 3:
                    sp.dma_start(t3_v[:, at, :], tab[:, :, 0:132]).then_inc(tab_out, 16)
                    sp.dma_start(ar_v[:, at, :], tab[:, :, 132:136]).then_inc(tab_out, 16)
                else:
                    sp.wait_ge(x_done, g + 1)
                    sp.sem_inc(waited, 1)
                    sp.dma_start(out_v[:, at, :], k.X[:, at, :]).then_inc(tab_out, 16)

            two_ahead(sp, NG, load, store)
            sp.wait_ge(tab_out, (NG + 1) * n_out)

        @block.gpsimd
        def _(pool):
            def gather(g):
                if post in (None, 1):
                    return
                pool.wait_ge(rows_used, g + 1)
                pool.tensor_copy(gidx[:, :], k.end_row[:, bass.ds(g * GT, GT)]).then_inc(gidx_ready, 1)
                pool.wait_ge(gidx_ready, g + 1)
                pool.sem_inc(waited, 1)
                for t in range(GT):
                    pool.indirect_dma_start(rg[:, t, 0:GW], None, rows,
                                            bass.IndirectOffsetOnAxis(ap=gidx[:, t:t + 1], axis=0)).then_inc(rows_in, 16)

            def scatter(g):
                if not SPREAD:
                    return
                to, at = (k.starts, 132) if pre == 3 else (k.spread, TW - 132)
                if not (isinstance(g, int) and g == 0):
                    pool.wait_ge(sent, g * (16 * GT))
                    pool.sem_inc(tab_sent, 1)
                pool.tensor_copy(sidx[:, :], k.start_row[:, bass.ds(g * GT, GT)]).then_inc(sidx_ready, 1)
                pool.wait_ge(sidx_ready, g + 1)
                pool.wait_ge(tab_ready, g + 2)
                pool.sem_inc(waited, 1)
                for t in range(GT):
                    pool.indirect_dma_start(to, bass.IndirectOffsetOnAxis(ap=sidx[:, t:t + 1], axis=0), tab[:, t, at:TW], None).then_inc(sent, 16)

            two_ahead(pool, NG, gather, scatter)
            if SPREAD:
                pool.wait_ge(sent, NG * (16 * GT))

        @block.vector
        def _(v):
            ch = Chain(v, dve_step)
            if pre == 1:
                ch.link(v.memset(tab[:, :, 128:132], 0.0))

            def finish(g):
                xg = k.X[:, bass.ds(g * GT, GT), :]
                if post == 1:
                    v.wait_ge(rows_in, g * (16 * SUMS) + 16 * SUMS)
                elif post is not None:
                    v.wait_ge(rows_in, g * (16 * GT) + 16 * GT)
                if post == 0:
                    ss = k.sself[:, bass.ds(g * GT, GT), :]
                    ch.link(v.tensor_tensor(mx[:, :, :], rg[:, :, 132:136], ss, ALU.max))
                    ch.step(v.tensor_tensor(ex[:, 0, :].rearrange("p (t h) -> p t h", h=HEADS), rg[:, :, 132:136], mx[:, :, :], ALU.subtract))
                    v.tensor_tensor(ex[:, 1, :].rearrange("p (t h) -> p t h", h=HEADS), ss, mx[:, :, :], ALU.subtract).then_inc(ex_arg, 1)
                    v.wait_ge(ex_done, g + 1)
                    d3 = den[:, :].rearrange("p (t h) -> p t h", h=HEADS)
                    ch.link(v.tensor_tensor(d3, rg[:, :, 128:132], ex[:, 0, :].rearrange("p (t h) -> p t h", h=HEADS), ALU.mult))
                    ch.link(v.tensor_tensor(den[:, :], den[:, :], ex[:, 1, :], ALU.add))
                    ch.link(v.reciprocal(den[:, :], den[:, :]))
                    ch.link(v.tensor_tensor(ex[:, :, :], ex[:, :, :], bc_mid(den[:, :], 2), ALU.mult))
                    q4 = "p t (h c) -> p (t h) c"
                    a4 = rg[:, :, 0:D].rearrange("p t (h c) -> p t h c", h=HEADS)
                    v.tensor_tensor(y[:, :, :].rearrange("p t (h c) -> p t h c", h=HEADS), a4,
                                    bc_last(ex[:, 0, :].rearrange("p (t h) -> p t h", h=HEADS), HDIM), ALU.mult).then_inc(rows_used, 1)
                    v.wait_ge(fsn_in, g * 16 + 16)
                    v.tensor_tensor(cen[:, :, :].rearrange(q4, h=HEADS), fsn[:, :, :].rearrange(q4, h=HEADS),
                                    bc_last(ex[:, 1, :], HDIM), ALU.mult).then_inc(fsn_used, 1)
                    v.wait_ge(rows_used, g + 2)
                    v.wait_ge(fsn_used, g + 2)
                    v.tensor_tensor(y[:, :, :], y[:, :, :], cen[:, :, :], ALU.add).then_inc(post_mm, 1)
                    v.wait_ge(post_mm, g + 1)
                    v.scalar_tensor_tensor(out=xg, in0=y[:, :, :], scalar=0.0, in1=xg, op0=ALU.max, op1=ALU.add).then_inc(x_done, 1)
                    v.wait_ge(x_done, g + 1)
                elif post == 1:
                    ch.link(v.tensor_tensor(part[:, 0:3, :, :], part[:, 0:3, :, :], part[:, 3:6, :, :], ALU.add))
                    ch.step(v.tensor_tensor(y[:, :, :], part[:, 0, :, :], part[:, 1, :, :], ALU.add))
                    v.tensor_tensor(y2[:, :, :], part[:, 2, :, :], part[:, 6, :, :], ALU.add).then_inc(rows_used, 1)
                    v.wait_ge(rows_used, g + 2)
                    ch.link(v.tensor_tensor(y[:, :, :], y[:, :, :], y2[:, :, :], ALU.add))
                    v.scalar_tensor_tensor(out=xg, in0=y[:, :, :], scalar=0.0, in1=xg, op0=ALU.max, op1=ALU.add).then_inc(x_done, 1)
                    v.wait_ge(x_done, g + 1)
                elif post == 2:
                    v.wait_ge(post_mm, g + 1)
                    v.tensor_tensor(y[:, :, :], psB[:, 0:GT * D].rearrange("p (t c) -> p t c", c=D), bc_mid(k.mb2[:, :], GT), ALU.add).then_inc(post_used, 1)
                    v.wait_ge(post_used, g + 2)
                    v.tensor_tensor(xg, y[:, :, :], xg, ALU.add).then_inc(x_done, 1)
                    v.wait_ge(x_done, g + 1)
                elif post == 3:
                    ch.link(v.tensor_scalar(den[:, :, :], rg[:, :, 128:132], 1e-9, None, ALU.add))
                    ch.link(v.reciprocal(den[:, :, :], den[:, :, :]))
                    v.tensor_tensor(y[:, :, :].rearrange("p t (h c) -> p t h c", h=HEADS),
                                    rg[:, :, 0:D].rearrange("p t (h c) -> p t h c", h=HEADS),
                                    bc_last(den[:, :, :], HDIM), ALU.mult).then_inc(rows_used, 1)
                    v.wait_ge(gelu_done, g + 1)
                    ch.link(v.tensor_reduce(out=s7[:, :], in_=y[:, :, :], op=ALU.add, axis=AX.X))
                    ch.link(v.tensor_scalar(m7[:, :], s7[:, :], 1.0 / D, None, ALU.mult))
                    v.tensor_tensor(cen[:, :, :], y[:, :, :], bc_last(m7[:, :], D), ALU.subtract).then_inc(cen_ready, 1)
                    v.wait_ge(sq_ready, g + 1)
                    ch.link(v.tensor_reduce(out=s7[:, :], in_=sq[:, :, :], op=ALU.add, axis=AX.X))
                    v.tensor_scalar(v7[:, :], s7[:, :], 1.0 / D, EPS, ALU.mult, ALU.add).then_inc(var_ready, 1)
                    v.wait_ge(std_ready, g + 1)
                    ch.link(v.reciprocal(r7[:, :], v7[:, :]))
                    ch.link(v.tensor_tensor(cen[:, :, :], cen[:, :, :], bc_last(r7[:, :], D), ALU.mult))
                    ch.link(v.tensor_tensor(cen[:, :, :], cen[:, :, :], bc_mid(k.lns[:, :], GT), ALU.mult))
                    ch.link(v.tensor_tensor(cen[:, :, :], cen[:, :, :], bc_mid(k.lnb[:, :], GT), ALU.add))
                    v.tensor_tensor(xg, cen[:, :, :], xg, ALU.add).then_inc(x_done, 1)
                    v.wait_ge(x_done, g + 1)

            def norm(g):
                xg = k.X[:, bass.ds(g * GT, GT), :]
                if pre is not None:
                    v.sem_inc(waited, 1)
                    ch.link(v.tensor_reduce(out=s7[:, :], in_=xg, op=ALU.add, axis=AX.X))
                    ch.link(v.tensor_scalar(m7[:, :], s7[:, :], 1.0 / D, None, ALU.mult))
                    v.tensor_tensor(cen[:, :, :], xg, bc_last(m7[:, :], D), ALU.subtract).then_inc(cen_ready, 1)
                    v.wait_ge(sq_ready, g + 1)
                    ch.link(v.tensor_reduce(out=s7[:, :], in_=sq[:, :, :], op=ALU.add, axis=AX.X))
                    v.tensor_scalar(v7[:, :], s7[:, :], 1.0 / D, EPS, ALU.mult, ALU.add).then_inc(var_ready, 1)
                    v.wait_ge(std_ready, g + 1)
                    ch.link(v.reciprocal(r7[:, :], v7[:, :]))
                    v.scalar_tensor_tensor(out=h[:, :, :], in0=cen[:, :, :], scalar=0.0, in1=bc_last(r7[:, :], D),
                                           op0=ALU.max, op1=ALU.mult).then_inc(h_ready, 1)
                    if pre == 2:
                        v.wait_ge(h_ready, g + 1)
                        ch.link(v.tensor_tensor(xg, xg, h[:, :, :], ALU.add))

            def table(g):
                if pre is not None:
                    v.wait_ge(tab_ps, g + 1)
                    v.wait_ge(tab_out, g * n_out + n_out)
                    v.sem_inc(waited, 1)
                    pc = psC[:, 0:GT * ST].rearrange("p (t c) -> p t c", c=ST)[:, :, 0:NC]
                    if SPREAD:
                        v.wait_ge(tab_sent, g + 1)
                        v.sem_inc(waited, 1)
                    if pre == 3:
                        v.tensor_copy(tab[:, :, :], pc).then_inc(tab_ready, 1)
                    elif pre == 0:
                        for half in range(2):
                            lo = half * 132
                            ch.step(v.tensor_tensor(tab[:, :, lo:lo + D], pc[:, :, half * D:half * D + D], bc_mid(k.b0[:, half * D:half * D + D], GT), ALU.add))
                        v.wait_ge(dve_step, ch.base + ch.n)
                        for half in range(2):
                            lo = half * 132
                            ch.link(v.tensor_tensor(e[:, :, :], tab[:, :, lo:lo + D], bc_mid(k.attn02[:, :], GT), ALU.mult))
                            r = v.tensor_reduce(out=tab[:, :, lo + D:lo + 132], in_=e[:, :, :].rearrange("p t (h c) -> p t h c", h=HEADS), op=ALU.add, axis=AX.X)
                            if half == 0:
                                ch.link(r)
                            else:
                                r.then_inc(tab_ready, 1)
                    else:
                        bias = {1: k.b1, 2: k.pb}[pre]
                        v.tensor_tensor(tab[:, :, 0:D], pc, bc_mid(bias[:, :], GT), ALU.add).then_inc(tab_ready, 1)
                    if pre == 3:
                        v.wait_ge(tab_ready, g + 2)
                    if pre == 0:
                        v.wait_ge(tab_ready, g + 2)
                        ch.link(v.tensor_tensor(e[:, :, :], tab[:, :, 0:D], tab[:, :, 132:132 + D], ALU.add))
                        ch.link(v.scalar_tensor_tensor(out=e[:, :, :], in0=e[:, :, :], scalar=0.2, in1=e[:, :, :], op0=ALU.mult, op1=ALU.max))
                        ch.link(v.tensor_tensor(e[:, :, :], e[:, :, :], bc_mid(k.attn[:, :], GT), ALU.mult))
                        v.sem_inc(waited, 1)
                        ch.link(v.tensor_reduce(out=k.sself[:, bass.ds(g * GT, GT), :], in_=e[:, :, :].rearrange("p t (h c) -> p t h c", h=HEADS),
                                                op=ALU.add, axis=AX.X))

            turn = {None: 0, 0: 6, 1: 3, 2: 0, 3: 9}[post] + {0: 13, 1: 4, 2: 5, 3: 4, None: 0}[pre]
            finish(0)
            norm(0)
            with v.Fori(1, NG) as g:
                ch.loop(g - 1, turn)
                finish(g)
                norm(g)
                table(g - 1)
            ch.end(NG - 1)
            table(NG - 1)

        @block.scalar
        def _(act):
            def mlp(g):
                act.wait_ge(aT_ps, g + 1)
                act.activation(aT[:, :], psA[:, 0:GT * P], ACT.Copy).then_inc(aT_ready, 1)
                act.wait_ge(z_ps, g + 1)
                act.activation(uT[:, :], psB[:, 0:GT * P], ACT.Silu, bias=k.mb1[:, 0:1]).then_inc(u_ready, 1)

            def group(g, final):
                if pre == 0:
                    clear_spread(act, k, g, cleared)
                if post == 0:
                    act.wait_ge(ex_arg, g + 1)
                    act.activation(ex[:, :, :], ex[:, :, :], ACT.Exp).then_inc(ex_done, 1)
                if post == 3:
                    act.wait_ge(rows_used, g + 2)
                    act.activation(y[:, :, :], y[:, :, :], ACT.Gelu).then_inc(gelu_done, 1)
                if pre is not None or post == 3:
                    act.wait_ge(cen_ready, g + 1)
                    act.activation(sq[:, :, :], cen[:, :, :], ACT.Square).then_inc(sq_ready, 1)
                    act.wait_ge(var_ready, g + 1)
                    act.activation(v7[:, :], v7[:, :], ACT.Sqrt).then_inc(std_ready, 1)
                if post == 2 and not final:
                    mlp(g + 1)
                if pre is not None:
                    act.wait_ge(hT_ps, g + 1)
                    act.activation(hT[:, :], psA[:, 0:GT * P], ACT.Copy).then_inc(hT_ready, 1)

            if post == 2:
                mlp(0)
            with act.Fori(0, NG - 1) as g:
                group(g, False)
            group(NG - 1, True)
            if pre == 0:
                act.wait_ge(cleared, 2 * NG * 16)

        @block.tensor
        def _(pe):
            def mlp(g):
                pe.wait_ge(rows_in, g * (16 * GT) + 16 * GT)
                for t in range(GT):
                    last = pe.transpose(psA[:, t * P:(t + 1) * P], rg[:, t, :], k.ident[:, :])
                last.then_inc(aT_ps, 1)
                pe.wait_ge(aT_ps, g + 1)
                pe.sem_inc(rows_used, 1)
                pe.wait_ge(aT_ready, g + 1)
                pe.wait_ge(post_used, g + 1)
                pe.matmul(psB[:, 0:512], k.mw1[:, :], aT[:, 0:512], start=True, stop=True)
                pe.matmul(psB[:, 512:GT * P], k.mw1[:, :], aT[:, 512:GT * P], start=True, stop=True).then_inc(z_ps, 1)
                pe.wait_ge(u_ready, g + 1)
                for t in range(GT):
                    last = pe.matmul(psB[:, t * D:(t + 1) * D], uT[:, t * P:(t + 1) * P], k.mw2[:, :], start=True, stop=True)
                last.then_inc(post_mm, 1)

            def group(g, final):
                if post == 2 and not final:
                    mlp(g + 1)
                if pre is not None:
                    w = {0: k.w0, 1: k.w1, 2: k.pw, 3: k.w3}[pre]
                    pe.wait_ge(h_ready, g + 1)
                    for t in range(GT):
                        last = pe.transpose(psA[:, t * P:(t + 1) * P], h[:, t, :], k.ident[:, :])
                    last.then_inc(hT_ps, 1)
                    pe.wait_ge(hT_ready, g + 1)
                    pe.wait_ge(tab_ready, g + 1)
                    for t in range(GT):
                        last = pe.matmul(psC[:, t * ST:t * ST + NC], hT[:, t * P:(t + 1) * P], w[:, 0:NC], start=True, stop=True)
                    last.then_inc(tab_ps, 1)

            if post == 2:
                mlp(0)
            if pre is not None:
                with pe.Fori(0, NG - 1) as g:
                    group(g, False)
                group(NG - 1, True)




class Fill:

    def __init__(self, v, ch, k, carry, filled):
        self.v, self.ch, self.k, self.carry, self.filled = v, ch, k, carry, filled

    def begin(self, z_in, n, F, kb, at):
        self.F, self.kb = F, kb
        self.ch.link(self.v.tensor_copy(kb[:, :], self.k.keep[:, at]))
        self.v.wait_ge(z_in, n)

    def slots(self, lo, hi):
        for j in range(lo, hi):
            prev = self.carry[:, :] if j == 0 else self.F[:, j - 1, :]
            self.ch.link(self.v.scalar_tensor_tensor(out=self.F[:, j, :], in0=prev, scalar=self.kb[:, j:j + 1], in1=self.F[:, j, :],
                                                     op0=ALU.mult, op1=ALU.add))

    def end(self, n):
        self.v.tensor_copy(self.carry[:, :], self.F[:, JC - 1, :]).then_inc(self.filled, 1)
        self.v.wait_ge(self.filled, n)


FILL_STEPS = 1 + JC


def edge_phase(nc, k, a, layer):
    S, TURNS = k.S, k.TURNS
    SOFT = layer in (0, 3)
    W = {0: 136, 2: 128, 3: 136}[layer]
    SUM = {0: 132, 2: 128, 3: 132}[layer]
    GC = {0: 132, 2: 128, 3: 132}[layer]
    table = {0: k.tab0s, 2: k.tab2, 3: k.tab3}[layer]
    rows = {0: k.rows0, 2: k.rows2, 3: k.rows0}[layer]
    rows_v = rows[0:k.EP, :].rearrange("(p s) c -> p s c", s=S)
    z_v = k.spread[0:k.EP, :].rearrange("(p s) c -> p s c", s=S)
    NB = JC // 4
    TB = BUFS * NB
    with Phase(nc, f"e{layer}") as ph:
        R = [ph.sb(f"row{q}", [P, JC, W]) for q in range(BUFS)]
        sidx = [ph.sb(f"sidx{q}", [P, JC], I32) for q in range(BUFS)]
        kb = [ph.sb(f"kb{q}", [P, JC + 1]) for q in range(BUFS)]
        last = k.last
        carry = ph.sb("carry", [P, 132])
        if SOFT:
            ng = ph.sb("ng", [P, JC + 1])
            sc, run, M = (ph.sb(x, [P, HEADS, JC]) for x in ("sc", "run", "M"))
            df = ph.sb("df", [P, HEADS, JC + 1])
            rc = ph.sb("rc", [P, HEADS])
            scp = [ph.ps(f"scp{z}", [P, 512]) for z in range(2)]
            scp_ready = ph.sem("scp_ready")
            scp_used = [ph.sem(f"scp_used{z}", credit=1) for z in range(2)]
        if layer == 0:
            F = [ph.sb(f"f{z}", [P, JC, 132]) for z in range(2)]
            fcarry = ph.sb("fcarry", [P, 132])
            rT = ph.sb("rT", [P, 2048])
            eT = ph.ps("eT", [P, 2048])
            cw, sw = k.by_src[0].shape[0] // P * D // TURNS, S * HEADS // TURNS
            zero = ph.sb("zero", [P, max(cw, sw)])
            zero_ready, cleared = ph.sem("zero_ready"), ph.sem("cleared")
            z_in = [ph.sem(f"z_in{z}") for z in range(2)]
            filled, first_in = ph.sem("filled"), ph.sem("first_in")
            eT_ready, r_ready, r_used = ph.sem("eT_ready"), ph.sem("r_ready", credit=4), ph.sem("r_used", credit=4)
        if layer == 3:
            floor = ph.sb("floor", [P, HEADS, JC])
            eft = [ph.sb(f"eft{z}", [16, JC * P]) for z in range(2)]
            attr_in = [ph.sem(f"attr_in{z}") for z in range(2)]
        if layer == 2:
            cb = ph.sb("cb", [P, JC])
            dist = ph.sb("dist", [51, JC * P])
            rbf = ph.sb("rbf", [51, JC * P])
            u = ph.sb("u", [P, JC * P])
            zps = ph.ps("zps", [P, 2048])
            wps = ph.ps("wps", [P, 2048])
            dist_in, dist_used = ph.sem("dist_in"), ph.sem("dist_used")
            rbf_ready = ph.sem("rbf_ready")
            z_ready, u_ready, w_ready, w_used = (ph.sem(x, credit=NB) for x in ("z_ready", "u_ready", "w_ready", "w_used"))

        dve_step = ph.sem("dve_step")
        idx_in = [ph.sem(f"idx_in{q}") for q in range(BUFS)]
        rows_in = [ph.sem(f"rows_in{q}") for q in range(BUFS)]
        rows_out = [ph.sem(f"rows_out{q}", credit=16) for q in range(BUFS)]
        summed = ph.sem("summed")
        exp_arg, exp_done = ph.sem("exp_arg"), ph.sem("exp_done")
        waited = ph.sem("waited")
        block = ph.block()

        @block.sync
        def _(sp):
            ph.give_credits(sp)

            def load_idx(q, at):
                sp.dma_start(sidx[q][:, :], a["src"][:, at]).then_inc(idx_in[q], 16)

            def load_chunk(q, c):
                z = q % 2
                if layer == 0:
                    sp.dma_start(F[z][:, :, :], z_v[:, bass.ds(c * JC, JC), :]).then_inc(z_in[z], 16)
                if layer == 3:
                    sp.dma_start(eft[z][:, :], a["edge_attr_16_T"][:, bass.ds(c * (JC * P), JC * P)]).then_inc(attr_in[z], 16)

            def load_dist(c):
                sp.dma_start(dist[:, :], a["dist_T"][0:1, bass.ds(c * (JC * P), JC * P)].to_broadcast([51, JC * P])).then_inc(dist_in, 16)

            for q in range(BUFS):
                load_idx(q, bass.ds(q * JC, JC))
            for q in range(2):
                load_chunk(q, q)
            if layer == 2:
                load_dist(0)
            if layer == 0:
                sp.wait_ge(zero_ready, 1)

            def turn(i, final):
                if layer == 0:
                    for t in range(SUMS):
                        sp.dma_start(k.by_src[t].rearrange("(p r) c -> p (r c)", p=P)[:, bass.ds(i * cw, cw)], zero[:, 0:cw]).then_inc(cleared, 16)
                    sp.dma_start(k.starts[0:k.EP, :].rearrange("(p s) c -> p (s c)", p=P)[:, bass.ds(i * sw, sw)], zero[:, 0:sw]).then_inc(cleared, 16)
                for q in range(BUFS):
                    if layer == 2 and not (final and q == BUFS - 1):
                        sp.wait_ge(dist_used, i * BUFS + q + 1)
                        sp.sem_inc(waited, 1)
                        load_dist(i * BUFS + (q + 1))
                    if not final:
                        sp.wait_ge(rows_in[q], (i + 1) * (16 * JC))
                        sp.sem_inc(waited, 1)
                        load_idx(q, bass.ds((i + 1) * (BUFS * JC) + q * JC, JC))
                    if SOFT and not (final and q >= BUFS - 2):
                        sp.wait_ge(scp_used[q % 2], i * (BUFS // 2) + (q // 2 + 2))
                        sp.sem_inc(waited, 1)
                        load_chunk(q, i * BUFS + (q + 2))
                    sp.wait_ge(summed, i * BUFS + (q + 1))
                    sp.dma_start(rows_v[:, bass.ds(i * (BUFS * JC) + q * JC, JC), :], R[q][:, :, :]).then_inc(rows_out[q], 16)

            with sp.Fori(0, TURNS - 1) as i:
                turn(i, False)
            turn(TURNS - 1, True)
            for q in range(BUFS):
                sp.wait_ge(rows_out[q], TURNS * 16 + 16)
            if layer == 0:
                sp.wait_ge(cleared, TURNS * (SUMS + 1) * 16)

        @block.gpsimd
        def _(pool):
            if layer == 0:
                pool.indirect_dma_start(fcarry[:, :], None, k.tab0d, bass.IndirectOffsetOnAxis(ap=k.first_dst[:, 0:1], axis=0)).then_inc(first_in, 16)
            with pool.Fori(0, TURNS) as i:
                for q in range(BUFS):
                    pool.wait_ge(idx_in[q], (i + 1) * 16)
                    pool.wait_ge(rows_out[q], i * 16 + 16)
                    pool.sem_inc(waited, 1)
                    for j in range(JC):
                        pool.indirect_dma_start(R[q][:, j, 0:GC], None, table,
                                                bass.IndirectOffsetOnAxis(ap=sidx[q][:, j:j + 1], axis=0)).then_inc(rows_in[q], 16)

        @block.vector
        def _(v):
            ch = Chain(v, dve_step)
            if layer == 0:
                v.memset(zero[:, :], 0.0).then_inc(zero_ready, 1)
            ch.link(v.memset(last[:, 0:SUM], 0.0))
            if SOFT:
                ch.link(v.memset(last[:, 132:136], -BIG))

            def fill(i, q, c):
                f.begin(z_in[q % 2], i * (BUFS // 2 * 16) + (q // 2 + 1) * 16, F[q % 2], kb[q % BUFS], bass.ds(c * JC, JC + 1))
                f.slots(0, JC)
                f.end(c + 1)

            if layer == 0:
                f = Fill(v, ch, k, fcarry, filled)
                v.wait_ge(first_in, 16)
                ch.link(v.tensor_scalar(fcarry[:, :], fcarry[:, :], k.cont[:, 0:1], None, ALU.mult))
                fill(0, 0, 0)

            def chunk(i, q, final):
                at = i * (BUFS * JC) + q * JC
                c1 = i * BUFS + (q + 1)
                z = q % 2
                rq = R[q]
                if layer == 0:
                    if not (final and q == BUFS - 1):
                        fill(i, q + 1, i * BUFS + (q + 1))
                else:
                    ch.link(v.tensor_copy(kb[q][:, :], k.keep[:, bass.ds(at, JC + 1)]))
                if SOFT:
                    ch.link(v.tensor_scalar(ng[:, :], kb[q][:, :], -1.0, BIG, ALU.add, ALU.mult))
                v.wait_ge(rows_in[q], (i + 1) * (16 * JC))
                if SOFT:
                    v.wait_ge(scp_ready, c1)
                    scv = scp[z][:, 0:JC * HEADS].rearrange("p (j h) -> p h j", h=HEADS)
                if layer == 0:
                    ch.link(v.tensor_tensor(sc[:, :, :], rq[:, :, 128:132].rearrange("p j h -> p h j"), F[z][:, :, 128:132].rearrange("p j h -> p h j"), ALU.add))
                    v.tensor_tensor(sc[:, :, :], sc[:, :, :], scv, ALU.add).then_inc(scp_used[z], 1)
                    v.wait_ge(scp_used[z], i * (BUFS // 2) + (q // 2 + 2))
                    top = sc
                if layer == 3:
                    ch.link(v.tensor_tensor(sc[:, :, :], rq[:, :, 128:132].rearrange("p j h -> p h j"), k.AR[:, :, bass.ds(at, JC)], ALU.add))
                    ch.link(v.scalar_tensor_tensor(out=sc[:, :, :], in0=sc[:, :, :], scalar=0.2, in1=sc[:, :, :], op0=ALU.mult, op1=ALU.max))
                    v.tensor_tensor(sc[:, :, :], sc[:, :, :], scv, ALU.add).then_inc(scp_used[z], 1)
                    v.wait_ge(scp_used[z], i * (BUFS // 2) + (q // 2 + 2))
                    ch.link(v.tensor_scalar(floor[:, :, :], sc[:, :, :], -1e9, None, ALU.max))
                    top = floor
                if SOFT:
                    for h in range(HEADS):
                        ch.step(v.tensor_tensor_scan(out=run[:, h, :], data0=ng[:, 0:JC], data1=top[:, h, :],
                                                     initial=last[:, 132 + h:133 + h], op0=ALU.add, op1=ALU.max))
                    v.wait_ge(dve_step, ch.base + ch.n)
                    for h in range(HEADS):
                        ch.step(v.tensor_tensor_scan(out=M[:, h, ::-1], data0=ng[:, JC:0:-1], data1=run[:, h, ::-1],
                                                     initial=-BIG, op0=ALU.add, op1=ALU.max))
                    v.wait_ge(dve_step, ch.base + ch.n)
                    ch.step(v.tensor_tensor(df[:, :, 0:JC], sc[:, :, :], M[:, :, :], ALU.subtract))
                    ch.link(v.tensor_tensor(df[:, :, JC:JC + 1], last[:, 132:136].unsqueeze(2), M[:, :, 0:1], ALU.subtract))
                    v.tensor_scalar(df[:, :, JC:JC + 1], df[:, :, JC:JC + 1], 0.0, None, ALU.min).then_inc(exp_arg, 1)
                    ch.step(v.tensor_copy(rq[:, :, 132:136].rearrange("p j h -> p h j"), M[:, :, :]))
                    v.wait_ge(exp_done, c1 * 2)
                    ch.step(v.tensor_tensor(rq[:, :, 0:D].rearrange("p j (h c) -> p j h c", h=HEADS), rq[:, :, 0:D].rearrange("p j (h c) -> p j h c", h=HEADS),
                                            bc_last(rq[:, :, 128:132], HDIM), ALU.mult))
                    ch.step(v.tensor_tensor(carry[:, 0:D].rearrange("p (h c) -> p h c", h=HEADS), last[:, 0:D].rearrange("p (h c) -> p h c", h=HEADS),
                                            bc_last(rc[:, :], HDIM), ALU.mult))
                    ch.link(v.tensor_tensor(carry[:, D:D + HEADS], last[:, D:D + HEADS], rc[:, :], ALU.mult))
                    before = carry[:, 0:SUM]
                else:
                    before = last[:, 0:SUM]
                if layer == 2:
                    ch.link(v.tensor_copy(cb[:, :], k.cut[:, bass.ds(at, JC)]))
                    for b in range(NB):
                        v.wait_ge(w_ready, i * TB + (q * NB + b + 1 + NB))
                        for j in range(4):
                            s = 4 * b + j
                            ins = v.scalar_tensor_tensor(out=rq[:, s, :], in0=ring(wps, q * NB + b, j), scalar=cb[:, s:s + 1], in1=rq[:, s, :],
                                                         op0=ALU.mult, op1=ALU.mult)
                            if j < 3:
                                ch.step(ins)
                            else:
                                ins.then_inc(w_used, 1)
                    v.wait_ge(w_used, i * TB + (q + 2) * NB)
                for j in range(JC):
                    prev = before if j == 0 else rq[:, j - 1, 0:SUM]
                    ch.link(v.scalar_tensor_tensor(out=rq[:, j, 0:SUM], in0=prev, scalar=kb[q][:, j:j + 1], in1=rq[:, j, 0:SUM],
                                                   op0=ALU.mult, op1=ALU.add))
                v.tensor_copy(last[:, 0:W], rq[:, JC - 1, 0:W]).then_inc(summed, 1)
                v.wait_ge(summed, c1)

            per_turn = BUFS * (JC + {0: 16 + FILL_STEPS, 2: 2 + 3 * NB, 3: 19}[layer])
            with v.Fori(0, TURNS - 1) as i:
                ch.loop(i, per_turn)
                for q in range(BUFS):
                    chunk(i, q, False)
            ch.end(TURNS - 1)
            for q in range(BUFS):
                chunk(TURNS - 1, q, True)

        @block.scalar
        def _(act):
            with act.Fori(0, TURNS) as i:
                for q in range(BUFS):
                    n = i * BUFS + q
                    if layer == 0:
                        for b in range(NB):
                            m = i * TB + (q * NB + b)
                            act.wait_ge(eT_ready, m + 1)
                            act.wait_ge(r_used, m + 1)
                            act.activation(ring(rT, q * NB + b), ring(eT, q * NB + b), ACT.Relu, scale=0.8).then_inc(r_ready, 1)
                    if SOFT:
                        act.wait_ge(exp_arg, n + 1)
                        act.activation(R[q][:, :, 128:132].rearrange("p j h -> p h j"), df[:, :, 0:JC], ACT.Exp).then_inc(exp_done, 1)
                        act.activation(rc[:, :].unsqueeze(2), df[:, :, JC:JC + 1], ACT.Exp).then_inc(exp_done, 1)
                    if layer == 2:
                        act.wait_ge(dist_in, n * 16 + 16)
                        act.wait_ge(z_ready, n * NB + NB)
                        act.activation(rbf[:, :], dist[:, :], ACT.Square, bias=k.rbf_bias[0:51, 0:1], scale=k.rbf_scale[0:51, 0:1]).then_inc(dist_used, 1)
                        act.wait_ge(dist_used, n + 1)
                        act.activation(rbf[:, :], rbf[:, :], ACT.Exp, scale=-50.0).then_inc(rbf_ready, 1)
                        act.wait_ge(w_ready, n * NB + NB)
                        for b in range(NB):
                            act.wait_ge(z_ready, n * NB + b + 1 + NB)
                            act.activation(u[:, b * 512:(b + 1) * 512], ring(zps, q * NB + b), ACT.Silu).then_inc(u_ready, 1)

        @block.tensor
        def _(pe):
            if layer == 0:
                with pe.Fori(0, TURNS) as i:
                    for q in range(BUFS):
                        z = q % 2
                        pe.wait_ge(rows_in[q], (i + 1) * (16 * JC))
                        pe.wait_ge(filled, i * BUFS + (q + 1))
                        pe.wait_ge(scp_used[z], i * (BUFS // 2) + (q // 2 + 1))

                        def sums(b):
                            pe.wait_ge(r_ready, i * TB + (q * NB + b + 1))
                            for j in range(4):
                                o = ring(eT, q * NB + b, j)
                                pe.matmul(o, R[q][:, 4 * b + j, 0:D], k.ident[:, :], start=True, stop=False)
                                mm = pe.matmul(o, F[z][:, 4 * b + j, 0:D], k.ident[:, :], start=False, stop=True)
                            mm.then_inc(eT_ready, 1)

                        def scores(b):
                            pe.wait_ge(r_ready, i * TB + (q * NB + b + 5))
                            for j in range(4):
                                mm = pe.matmul(scp[z][:, (4 * b + j) * HEADS:(4 * b + j + 1) * HEADS], ring(rT, q * NB + b, j), k.attn_cols[:, :], start=True, stop=True)
                            mm.then_inc(r_used, 1)

                        sums(0)
                        for b in range(NB):
                            if b + 1 < NB:
                                sums(b + 1)
                            scores(b)
                        pe.wait_ge(r_used, i * TB + (q * NB + NB + 4))
                        pe.sem_inc(scp_ready, 1)
            if layer == 3:
                with pe.Fori(0, TURNS) as i:
                    for q in range(BUFS):
                        z = q % 2
                        pe.wait_ge(attr_in[z], i * (BUFS // 2 * 16) + (q // 2 + 1) * 16)
                        pe.wait_ge(scp_used[z], i * (BUFS // 2) + (q // 2 + 1))
                        for j in range(JC):
                            mm = pe.matmul(scp[z][:, j * HEADS:(j + 1) * HEADS], eft[z][:, j * P:(j + 1) * P], k.wet[:, :], start=True, stop=True)
                        mm.then_inc(scp_ready, 1)
            if layer == 2:
                with pe.Fori(0, TURNS) as i:
                    for q in range(BUFS):
                        n = i * BUFS + q

                        def z_block(b):
                            pe.matmul(ring(zps, q * NB + b), k.fw1[:, :], rbf[:, b * 512:(b + 1) * 512], start=True, stop=True).then_inc(z_ready, 1)

                        pe.wait_ge(rbf_ready, n + 1)
                        pe.wait_ge(u_ready, n * NB + NB)
                        for b in range(3):
                            z_block(b)
                        for b in range(NB):
                            if b + 3 < NB:
                                if b >= 1:
                                    pe.wait_ge(u_ready, n * NB + b + NB)
                                z_block(b + 3)
                            pe.wait_ge(u_ready, n * NB + b + 1 + NB)
                            pe.wait_ge(w_used, n * NB + b - 3 + NB)
                            pe.matmul(ring(wps, q * NB + b), k.ones_bf[:, :], k.fb2[:, :], start=True, stop=False)
                            for j in range(4):
                                mm = pe.matmul(ring(wps, q * NB + b, j), u[:, (4 * b + j) * P:(4 * b + j + 1) * P], k.fw2[:, :], start=False, stop=(j == 3))
                            mm.then_inc(w_ready, 1)


def scatter_phase(nc, k, a):
    S = k.S
    TURNS = k.TURNS
    NB = JC // 4
    TB = BUFS * NB
    z_v = k.spread[0:k.EP, :].rearrange("(p s) c -> p s c", s=S)
    PARTS = NB - 2
    with Phase(nc, "e1") as ph:
        scol_i = [ph.sb(f"scol_i{q}", [P, JC], I32) for q in range(2)]
        F = [ph.sb(f"f{q}", [P, JC, 132]) for q in range(2)]
        kb = [ph.sb(f"kb{q}", [P, JC + 1]) for q in range(2)]
        fcarry = ph.sb("fcarry", [P, 132])
        attr = [ph.sb(f"attr{q}", [65, JC * P]) for q in range(2)]
        srow = ph.sb("srow", [2, JC * P], BF)
        scol = ph.sb("scol", [P, JC])
        same = [ph.sb(f"same{z}", [P, 4, P]) for z in range(2)]
        dup = ph.sb("dup", [P, 4, P])
        first = ph.sb("first", [P, JC])
        sums = [ph.sb(f"sums{q}", [P, JC, D]) for q in range(BUFS)]
        to_f = ph.sb("to_f", [P, JC])
        to = [ph.sb(f"to{q}", [P, JC], I32) for q in range(BUFS)]
        bps = [ph.ps(f"bps{z}", [P, 512]) for z in range(2)]
        vps = [ph.ps(f"vps{z}", [P, 512]) for z in range(2)]
        sps = [ph.ps(f"sps{z}", [P, 512]) for z in range(2)]

        dve_step = ph.sem("dve_step")
        z_in = [ph.sem(f"z_in{q}") for q in range(2)]
        filled, first_in = ph.sem("filled"), ph.sem("first_in")
        scol_in, attr_in = ([ph.sem(f"{n}{q}") for q in range(2)] for n in ("scol_in", "attr_in"))
        srow_in = ph.sem("srow_in")
        scol_ready = ph.sem("scol_ready", credit=1)
        to_ready = ph.sem("to_ready")
        scattered = [ph.sem(f"scattered{t}") for t in range(SUMS)]
        landed = ph.sem("landed", credit=BUFS)
        b_ready, v_ready, sq_ready, same_ready, dup_ready, msg_ready, sum_ready, sum_out = (
            ph.sem(n, credit=NB) for n in ("b_ready", "v_ready", "sq_ready", "same_ready", "dup_ready", "msg_ready", "sum_ready", "sum_out"))
        waited = ph.sem("waited")
        block = ph.block()

        @block.sync
        def _(sp):
            ph.give_credits(sp)

            def load(q, c):
                sp.dma_start(F[q][:, :, :], z_v[:, bass.ds(c * JC, JC), :]).then_inc(z_in[q], 16)
                sp.dma_start(attr[q][0:64, :], a["edge_attr_64_T"][:, bass.ds(c * (JC * P), JC * P)]).then_inc(attr_in[q], 16)
                sp.dma_start(scol_i[q][:, :], a["src"][:, bass.ds(c * JC, JC)]).then_inc(scol_in[q], 16)

            def load_srow(c):
                sp.dma_start(srow[:, :], k.src_parts[:, bass.ds(c * (JC * P), JC * P)]).then_inc(srow_in, 16)

            load(0, 0)
            load_srow(0)
            load(1, 1)

            def turn(i, final):
                for q in range(BUFS):
                    if not (final and q == BUFS - 1):
                        sp.wait_ge(b_ready, i * TB + (q + 2) * NB)
                        sp.sem_inc(waited, 1)
                        load_srow(i * BUFS + (q + 1))
                    if not (final and q >= BUFS - 2):
                        sp.wait_ge(sum_ready, i * TB + (q + 2) * NB)
                        sp.sem_inc(waited, 1)
                        load(q % 2, i * BUFS + (q + 2))

            with sp.Fori(0, TURNS - 1) as i:
                turn(i, False)
            turn(TURNS - 1, True)

        @block.gpsimd
        def _(pool):
            pool.indirect_dma_start(fcarry[:, :], None, k.tab1, bass.IndirectOffsetOnAxis(ap=k.first_dst[:, 0:1], axis=0)).then_inc(first_in, 16)

            def turn(i, first):
                for q in range(BUFS):
                    pool.wait_ge(to_ready, i * BUFS + (q + 1))
                    for j in range(JC):
                        if j % 4 == 0:
                            pool.wait_ge(sum_out, i * TB + (q * NB + j // 4 + 1 + NB))
                        if not (first and q == 0 and j < SUMS):
                            pool.wait_ge(scattered[j % SUMS], i * (BUFS * JC // SUMS * 16) + (q * JC + j) // SUMS * 16)
                        pool.sem_inc(landed if j == SUMS - 1 else waited, 1)
                        pool.indirect_dma_start(k.by_src[j % SUMS], bass.IndirectOffsetOnAxis(ap=to[q][:, j:j + 1], axis=0),
                                                sums[q][:, j, :], None, compute_op=ALU.add).then_inc(scattered[j % SUMS], 16)
            turn(0, True)
            with pool.Fori(1, TURNS) as i:
                turn(i, False)
            for t in range(SUMS):
                pool.wait_ge(scattered[t], TURNS * (BUFS * JC // SUMS * 16))

        @block.vector
        def _(v):
            ch = Chain(v, dve_step)
            ch.step(v.memset(attr[0][64:65, :], 1.0))
            ch.link(v.memset(attr[1][64:65, :], 1.0))

            f = Fill(v, ch, k, fcarry, filled)

            def fill(i, q, c, part=None):
                if part in (None, 0):
                    f.begin(z_in[q % 2], i * (BUFS // 2 * 16) + (q // 2 + 1) * 16, F[q % 2], kb[q % 2], bass.ds(c * JC, JC + 1))
                f.slots(*((0, JC) if part is None else (part * JC // PARTS, (part + 1) * JC // PARTS)))
                if part in (None, PARTS - 1):
                    f.end(c + 1)

            v.wait_ge(first_in, 16)
            ch.link(v.tensor_scalar(fcarry[:, :], fcarry[:, :], k.cont[:, 0:1], None, ALU.mult))
            fill(0, 0, 0)

            def chunk(i, q, final):
                w = q % 2
                v.wait_ge(scol_in[w], i * (BUFS // 2 * 16) + (q // 2 + 1) * 16)
                v.tensor_copy(scol[:, :], scol_i[w][:, :]).then_inc(scol_ready, 1)
                v.wait_ge(scol_ready, i * BUFS + (q + 2))
                for b in range(NB):
                    n = i * TB + (q * NB + b + 1 + NB)
                    z = (q * NB + b) % 2
                    hb = F[w][:, 4 * b:4 * b + 4, 0:D]
                    v.wait_ge(v_ready, n)
                    v.tensor_tensor(hb, hb, vps[z][:, :].rearrange("p (j c) -> p j c", c=D), ALU.add).then_inc(msg_ready, 1)
                    v.wait_ge(same_ready, n)
                    v.tensor_tensor(dup[:, :, :], same[z][:, :, :], bc_mid(k.before[:, :], 4), ALU.mult).then_inc(dup_ready, 1)
                    v.wait_ge(dup_ready, n)
                    ch.link(v.tensor_reduce(out=first[:, 4 * b:4 * b + 4], in_=dup[:, :, :], op=ALU.add, axis=AX.X))
                    if b >= NB - PARTS and not (final and q == BUFS - 1):
                        fill(i, q + 1, i * BUFS + (q + 1), b - (NB - PARTS))
                ch.link(v.tensor_scalar(first[:, :], first[:, :], 0.5, None, ALU.is_lt))
                ch.link(v.scalar_tensor_tensor(out=to_f[:, :], in0=scol[:, :], scalar=k.trash[:, 0:1], in1=first[:, :],
                                               op0=ALU.subtract, op1=ALU.mult))
                ch.link(v.tensor_scalar(to_f[:, :], to_f[:, :], k.trash[:, 0:1], None, ALU.add))
                v.wait_ge(landed, i * BUFS + (q + 2))
                v.tensor_copy(to[q][:, :], to_f[:, :]).then_inc(to_ready, 1)

            with v.Fori(0, TURNS - 1) as i:
                ch.loop(i, BUFS * (NB + 3 + FILL_STEPS))
                for q in range(BUFS):
                    chunk(i, q, False)
            ch.end(TURNS - 1)
            for q in range(BUFS):
                chunk(TURNS - 1, q, True)

        @block.scalar
        def _(act):
            with act.Fori(0, TURNS) as i:
                for q in range(BUFS):
                    def masks(b):
                        n = i * TB + (q * NB + b + 1 + NB)
                        z = (q * NB + b) % 2
                        lo = (q * NB + b - 1 + NB) if q * NB + b >= 2 else NB
                        act.wait_ge(sum_ready, i * TB + lo)
                        act.wait_ge(dup_ready, i * TB + lo)
                        act.wait_ge(b_ready, n)
                        for j in range(4):
                            a1 = act.activation(same[z][:, j, :], bps[z][:, j * P:(j + 1) * P], ACT.Square, bias=scol[:, 4 * b + j:4 * b + j + 1], scale=-1.0)
                        a1.then_inc(sq_ready, 1)
                        act.wait_ge(sq_ready, n)
                        act.activation(same[z][:, :, :], same[z][:, :, :], ACT.Relu, bias=k.ones[:, 0:1], scale=-1.0).then_inc(same_ready, 1)

                    act.wait_ge(scol_ready, i * BUFS + (q + 2))
                    masks(0)
                    act.wait_ge(landed, i * BUFS + (q + 2))
                    for b in range(NB):
                        if b + 1 < NB:
                            masks(b + 1)
                        n = i * TB + (q * NB + b + 1 + NB)
                        act.wait_ge(sum_ready, n)
                        act.activation(sums[q][:, 4 * b:4 * b + 4, :], sps[(q * NB + b) % 2][:, :].rearrange("p (j c) -> p j c", c=D), ACT.Copy).then_inc(sum_out, 1)

        @block.tensor
        def _(pe):
            pe.wait_ge(dve_step, 2)
            with pe.Fori(0, TURNS) as i:
                for q in range(BUFS):
                    w = q % 2
                    pe.wait_ge(srow_in, i * (BUFS * 16) + (q + 1) * 16)
                    pe.wait_ge(attr_in[w], i * (BUFS // 2 * 16) + (q // 2 + 1) * 16)

                    def fill(b):
                        z = (q * NB + b) % 2
                        c = slice(b * 512, (b + 1) * 512)
                        lo = (q * NB + b - 1 + NB) if q * NB + b >= 2 else NB
                        pe.wait_ge(same_ready, i * TB + lo)
                        pe.matmul(bps[z][:, :], k.ones_bf[0:2, :], srow[:, c], start=True, stop=True).then_inc(b_ready, 1)
                        pe.wait_ge(msg_ready, i * TB + lo)
                        for j in range(4):
                            mm = pe.matmul(vps[z][:, j * P:(j + 1) * P], attr[w][0:65, (4 * b + j) * P:(4 * b + j + 1) * P], k.we[0:65, :], start=True, stop=True)
                        mm.then_inc(v_ready, 1)

                    fill(0)
                    for b in range(NB):
                        if b + 1 < NB:
                            fill(b + 1)
                        n = i * TB + (q * NB + b + 1 + NB)
                        z = (q * NB + b) % 2
                        pe.wait_ge(msg_ready, n)
                        pe.wait_ge(same_ready, n)
                        lo = (q * NB + b - 1 + NB) if q * NB + b >= 2 else NB
                        pe.wait_ge(sum_out, i * TB + lo)
                        for j in range(4):
                            mm = pe.matmul(sps[z][:, j * D:(j + 1) * D], same[z][:, j, :], F[w][:, 4 * b + j, 0:D], start=True, stop=True)
                        mm.then_inc(sum_ready, 1)


def ring(t, n, j=None):
    lo = n % 4 * 512
    return t[:, lo:lo + 512] if j is None else t[:, lo + j * D:lo + (j + 1) * D]


def seam_phase(nc, k, a, layer):
    SOFT = layer in (0, 3)
    W = {0: 136, 2: 128, 3: 136}[layer]
    rows = {0: k.rows0, 2: k.rows2, 3: k.rows0}[layer]
    with Phase(nc, f"s{layer}") as ph:
        row = ph.sb("row", [P, W])
        ps = ph.ps("ps", [P, 512])
        last = k.last
        row_in, row_out, fixed = ph.sem("row_in"), ph.sem("row_out"), ph.sem("fixed")
        dve_step, pe_step, act_step = ph.sem("dve_step"), ph.sem("pe_step"), ph.sem("act_step")
        if SOFT:
            dg = ph.sb("dg", [P, HEADS, P])
            am = ph.sb("am", [P, HEADS, P])
            ngm = ph.sb("ngm", [P, P])
            cm = ph.sb("cm", [P, HEADS])
            wt = ph.sb("wt", [P, HEADS, P])
            ex = ph.sb("ex", [P, 2, HEADS])
            mm = ph.sb("mm", [P, HEADS])
            ps2 = ph.ps("ps2", [P, 512])
        block = ph.block()

        @block.gpsimd
        def _(pool):
            pool.indirect_dma_start(row[:, :], None, rows, bass.IndirectOffsetOnAxis(ap=k.seam_row[:, 0:1], axis=0)).then_inc(row_in, 16)
            pool.wait_ge(fixed, 1)
            pool.indirect_dma_start(rows, bass.IndirectOffsetOnAxis(ap=k.seam_row[:, 0:1], axis=0), row[:, :], None).then_inc(row_out, 16)
            pool.wait_ge(row_out, 16)

        if not SOFT:
            @block.tensor
            def _(pe):
                pe.matmul(ps[:, 0:W], k.seam[:, :], last[:, 0:W], start=True, stop=True).then_inc(pe_step, 1)

            @block.vector
            def _(v):
                v.wait_ge(pe_step, 1)
                v.wait_ge(row_in, 16)
                v.tensor_tensor(row[:, :], row[:, :], ps[:, 0:W], ALU.add).then_inc(fixed, 1)
            return

        @block.tensor
        def _(pe):
            pe.wait_ge(dve_step, 4)
            pe.matmul(ps[:, :], k.ones[:, :], dg[:, :, :].rearrange("p h q -> p (h q)"), start=True, stop=True).then_inc(pe_step, 1)
            pe.wait_ge(dve_step, 10)
            for h in range(HEADS):
                t = pe.transpose(ps2[:, h * P:(h + 1) * P], am[:, h, :], k.ident[:, :])
            t.then_inc(pe_step, 1)
            pe.wait_ge(dve_step, 11)
            for h in range(HEADS):
                pe.matmul(ps[:, h * HDIM:(h + 1) * HDIM], wt[:, h, :], last[:, h * HDIM:(h + 1) * HDIM], start=True, stop=True)
                t = pe.matmul(ps[:, D + h:D + h + 1], wt[:, h, :], last[:, D + h:D + h + 1], start=True, stop=True)
            t.then_inc(pe_step, 1)

        @block.scalar
        def _(act):
            act.wait_ge(dve_step, 9)
            act.activation(am[:, :, :], am[:, :, :], ACT.Exp).then_inc(act_step, 1)
            act.wait_ge(dve_step, 14)
            act.activation(ex[:, :, :], ex[:, :, :], ACT.Exp).then_inc(act_step, 1)

        @block.vector
        def _(v):
            ch = Chain(v, dve_step)
            for h in range(HEADS):
                ch.step(v.tensor_scalar(dg[:, h, :], k.ident[:, :], last[:, 132 + h:133 + h], None, ALU.mult))
            ch.link(v.tensor_scalar(ngm[:, :], k.seamT[:, :], -1.0, BIG, ALU.add, ALU.mult))
            v.wait_ge(pe_step, 1)
            ch.link(v.tensor_tensor(am[:, :, :], ps[:, :].rearrange("p (h q) -> p h q", h=HEADS), bc_mid(ngm[:, :], HEADS), ALU.add))
            ch.link(v.tensor_reduce(out=cm[:, :], in_=am[:, :, :], op=ALU.max, axis=AX.X))
            ch.link(v.tensor_tensor(am[:, :, :], am[:, :, :], bc_last(cm[:, :], P), ALU.subtract))
            ch.link(v.tensor_scalar(am[:, :, :], am[:, :, :], 0.0, None, ALU.min))
            v.wait_ge(act_step, 1)
            ch.link(v.tensor_tensor(am[:, :, :], am[:, :, :], bc_mid(k.seamT[:, :], HEADS), ALU.mult))
            v.wait_ge(pe_step, 2)
            ch.link(v.tensor_copy(wt[:, :, :], ps2[:, :].rearrange("p (h q) -> p h q", h=HEADS)))
            v.wait_ge(row_in, 16)
            ch.link(v.tensor_tensor(mm[:, :], row[:, 132:136], cm[:, :], ALU.max))
            ch.step(v.tensor_tensor(ex[:, 0, :], row[:, 132:136], mm[:, :], ALU.subtract))
            ch.link(v.tensor_tensor(ex[:, 1, :], cm[:, :], mm[:, :], ALU.subtract))
            v.wait_ge(act_step, 2)
            v.wait_ge(pe_step, 3)
            ch.step(v.tensor_copy(row[:, 132:136], mm[:, :]))
            ch.step(v.tensor_tensor(row[:, 0:D].rearrange("p (h c) -> p h c", h=HEADS), row[:, 0:D].rearrange("p (h c) -> p h c", h=HEADS),
                                    bc_last(ex[:, 0, :], HDIM), ALU.mult))
            ch.step(v.tensor_tensor(row[:, D:132], row[:, D:132], ex[:, 0, :], ALU.mult))
            ch.step(v.tensor_tensor(dg[:, 0, :].rearrange("p (h c) -> p h c", h=HEADS), ps[:, 0:D].rearrange("p (h c) -> p h c", h=HEADS),
                                    bc_last(ex[:, 1, :], HDIM), ALU.mult))
            ch.link(v.tensor_tensor(dg[:, 1, 0:HEADS], ps[:, D:132], ex[:, 1, :], ALU.mult))
            ch.link(v.tensor_tensor(row[:, 0:D], row[:, 0:D], dg[:, 0, :], ALU.add))
            v.tensor_tensor(row[:, D:132], row[:, D:132], dg[:, 1, 0:HEADS], ALU.add).then_inc(fixed, 1)


def fill_phase(nc, k):
    S = k.S
    with Phase(nc, "fill") as ph:
        z = ph.sb("z", [P, S, HEADS])
        z_in, first_in, filled = ph.sem("z_in"), ph.sem("first_in"), ph.sem("filled")
        block = ph.block()

        @block.sync
        def _(sp):
            sp.dma_start(z[:, :, :], k.starts[0:k.EP, :].rearrange("(p s) c -> p s c", s=S)).then_inc(z_in, 16)

        @block.gpsimd
        def _(pool):
            pool.wait_ge(z_in, 16)
            pool.indirect_dma_start(z[:, 0, :], None, k.ar_tab, bass.IndirectOffsetOnAxis(ap=k.first_dst[:, 0:1], axis=0)).then_inc(first_in, 16)

        @block.vector
        def _(v):
            v.wait_ge(first_in, 16)
            for h in range(HEADS):
                v.tensor_tensor_scan(out=k.AR[:, h, :], data0=k.keep[:, 0:S], data1=z[:, :, h], initial=0.0,
                                     op0=ALU.mult, op1=ALU.add).then_inc(filled, 1)


def gnn_program(nc, a):
    k = Ctx()
    k.EP = a["dst"].shape[0] * a["dst"].shape[1]
    k.S = a["dst"].shape[1]
    k.NT = a["x"].shape[0] // P
    k.NG = k.NT // GT
    assert k.S % (4 * k.NG) == 0 and k.S // (4 * k.NG) <= JC and k.NG % 2 == 0
    k.TURNS = k.S // (BUFS * JC)
    NP = P * k.NT

    def dram(name, shape, dt=FP):
        return nc.dram_tensor(name, shape, dt, kind="Internal").ap()

    k.tab0s, k.tab0d, k.tab1 = (dram(n, (NP, 132)) for n in ("tab0s", "tab0d", "tab1"))
    k.tab2 = dram("tab2", (NP, D))
    k.spread = dram("spread", (k.EP + NP, 132))
    k.tab3, k.ar_tab = dram("tab3", (NP, 132)), dram("ar_tab", (NP, HEADS))
    k.rows0, k.rows2 = dram("rows0", (k.EP + 1, 136)), dram("rows2", (k.EP + 1, D))
    NR = next(n for n in range(k.NT + 1, 2 * k.NT + k.TURNS) if n * D % k.TURNS == 0)
    k.by_src = [dram(f"by_src{t}", (P * NR, D)) for t in range(SUMS)]
    k.src_parts = dram("src_parts", (2, k.EP), BF)
    k.starts = dram("starts", (k.EP + NP, HEADS))
    k.counts = dram("counts", (1, NP + 1))
    with ExitStack() as st:
        def sb(n, shape, dt=FP):
            return st.enter_context(nc.sbuf_tensor(n, shape, dt))

        k.X = sb("X", [P, k.NT, D])
        k.keep, k.cut = sb("keep", [P, k.S + 1]), sb("cut", [P, k.S])
        k.ident, k.ones, k.seam, k.seamT = (sb(n, [P, P]) for n in ("ident", "ones", "seam", "seamT"))
        k.node, k.deg = sb("node", [P, k.NT]), sb("deg", [P, k.NT])
        k.end_row, k.start_row = sb("end_row", [P, k.NT], I32), sb("start_row", [P, k.NT], I32)
        k.cont, k.attn_cols, k.attn02 = sb("cont", [P, 1]), sb("attn_cols", [P, HEADS]), sb("attn02", [P, D])
        k.seam_row, k.first_dst = sb("seam_row", [P, 1], I32), sb("first_dst", [P, 1], I32)
        k.sself = sb("sself", [P, k.NT, HEADS])
        k.last = sb("last", [P, 136])
        k.trash, k.before = sb("trash", [P, 1]), sb("before", [P, P])
        k.w0, k.b0, k.attn = sb("w0", [P, 2 * D]), sb("b0", [P, 2 * D]), sb("attn", [P, D])
        k.ones_bf = sb("ones_bf", [3, P], BF)
        k.w1, k.b1, k.we = sb("w1", [P, D]), sb("b1", [P, D]), sb("we", [65, D])
        k.fw1, k.fw2, k.fb2 = sb("fw1", [51, D]), sb("fw2", [P, D]), sb("fb2", [3, 4 * D], BF)
        k.pw, k.pb, k.mw1, k.mw2, k.mb2 = (sb(n, [P, D]) for n in ("pw", "pb", "mw1", "mw2", "mb2"))
        k.mb1, k.rbf_bias, k.rbf_scale = sb("mb1", [P, 1]), sb("rbf_bias", [51, 1]), sb("rbf_scale", [51, 1])
        k.w3, k.wet, k.lns, k.lnb = sb("w3", [P, 136]), sb("wet", [16, HEADS]), sb("lns", [P, D]), sb("lnb", [P, D])

        with (nc.sbuf_tensor("zero_rows", [P, JC * 132], FP) as k.zero_rows,
              nc.sbuf_tensor("coarse_i", [P, a["dst_blocks"].shape[0]], I32) as k.coarse_i):
            setup_phase(nc, k, a)
            node_phase(nc, k, a, None, 0)
            ends_phase(nc, k, a)
        for layer in range(3):
            if layer == 1:
                scatter_phase(nc, k, a)
            else:
                edge_phase(nc, k, a, layer)
                seam_phase(nc, k, a, layer)
            node_phase(nc, k, a, layer, layer + 1)
        k.AR = sb("AR", [P, HEADS, k.S])
        fill_phase(nc, k)
        edge_phase(nc, k, a, 3)
        seam_phase(nc, k, a, 3)
        node_phase(nc, k, a, 3, None)




def kernel(**inputs):
    import numpy as np
    import concourse.bacc as _bacc
    from concourse import mybir as _mybir
    from concourse.bass_utils import run_bass_kernel_spmd as _run

    x, src, dst = (np.asarray(inputs[n]) for n in ("x", "src", "dst"))
    N, E = x.shape[0], src.shape[0]
    per = P * BUFS * JC
    EP = -(-E // per) * per
    S = EP // P
    NP = -(-N // (P * GT)) * P * GT
    pad_e = EP - E

    def padded(v, n, fill=0):
        v = np.asarray(v)
        return np.concatenate([v, np.full((n,) + v.shape[1:], fill, v.dtype)])

    arrays = {"x": padded(x, NP - N)}
    src_p = padded(src, pad_e, NP - 1).reshape(P, S)
    dst_p = padded(dst, pad_e, NP - 1)
    arrays["dst"] = dst_p.reshape(P, S)
    arrays["src"] = src_p
    arrays["dst_last"] = dst_p.reshape(P, S)[:, -1].reshape(1, P)
    block = min(b for b in range(1, EP + 1) if EP % b == 0 and b * b >= EP)
    arrays["dst_blocks"] = dst_p.reshape(-1, block)
    arrays["dst_coarse"] = dst_p[::block].reshape(1, -1)
    ew = padded(inputs["edge_weight"], pad_e).reshape(P, S)
    arrays["edge_weight"] = ew
    arrays["dist_T"] = ew.T.reshape(1, EP)
    arrays["src_T"] = src_p.T.reshape(1, EP)
    e64 = padded(inputs["edge_attr_64"], pad_e).reshape(P, S, 64)
    arrays["edge_attr_64_T"] = e64.transpose(2, 1, 0).reshape(64, EP)
    ea = padded(inputs["edge_attr_16"], pad_e).reshape(P, S, 16)
    arrays["edge_attr_16_T"] = ea.transpose(2, 1, 0).reshape(16, EP)
    for n in sorted(inputs):
        if n.startswith("L"):
            v = np.asarray(inputs[n])
            arrays[n] = v.reshape(1, -1) if v.ndim == 1 else v
    arrays["L3_gnn_W_T"] = np.asarray(inputs["L3_gnn_W"]).T
    arrays["L3_gnn_W_e_T"] = np.asarray(inputs["L3_gnn_W_e"]).T

    nc = _bacc.Bacc("TRN2", target_bir_lowering=False, num_devices=1)
    feed, a = {}, {}
    for n, v in arrays.items():
        v = np.ascontiguousarray(v)
        feed[f"in_{n}"] = v
        a[n] = nc.dram_tensor(f"in_{n}", v.shape, _mybir.dt.from_np(v.dtype), kind="ExternalInput").ap()
    a["out"] = nc.dram_tensor("out_0", (NP, D), _mybir.dt.float32, kind="ExternalOutput").ap()
    gnn_program(nc, a)
    r = _run(nc, [feed], core_ids=[0])
    return r.results[0]["out_0"][:N]
```
